# Optimizing a Trainium2 kernel written in Bass

```python
import numpy as np
import jax
import jax.numpy as jnp

def _softmax(x, axis=-1):
    return jax.nn.softmax(x, axis=axis)

def _gelu(x):
    return jax.nn.gelu(x, approximate=True)

def _silu(x):
    return jax.nn.silu(x)

def _sigmoid(x):
    return jax.nn.sigmoid(x)

def _layernorm(x, axis=-1, eps=1e-05):
    m = jnp.mean(x, axis=axis, keepdims=True)
    v = jnp.var(x, axis=axis, keepdims=True)
    return (x - m) / jnp.sqrt(v + eps)

def _scatter_add(tgt, idx, src, axis=0):
    return tgt.at[idx].add(src)

def _segment_sum(src, seg, n):
    return jax.ops.segment_sum(src, seg, n)
kernel_name = 'mk_decoder_preln_d1_seqx_r2_619706'

def setup_inputs(seed: int=0):
    np.random.seed(seed)
    _w = jnp.asarray

    def _rec_inputs():
        import jax
        import jax.numpy as jnp
        _rk = jax.random.key(seed)
        x = 7.22e-05 + 1 * jax.random.normal(jax.random.fold_in(_rk, 1), (4, 1024, 1024), jnp.float32)
        _lenS = 1024 - jax.random.randint(jax.random.fold_in(_rk, 7), (4,), 0, max(1, 1024 // 4) + 1, jnp.int32)
        _lenS2 = 1024 - jax.random.randint(jax.random.fold_in(_rk, 8), (4,), 0, max(1, 1024 // 4) + 1, jnp.int32)
        _ctx_1024P = jax.random.normal(jax.random.fold_in(_rk, 11), (4, 16, 512), jnp.float32)
        _ctx_1024c = jax.random.dirichlet(jax.random.fold_in(_rk, 511), 0.3 * jnp.ones((16,), jnp.float32), (4, 1024))
        _ctx_1024t = jnp.einsum('bsk,bkd->bsd', _ctx_1024c, _ctx_1024P)
        _ctx_1024t = _ctx_1024t * jax.lax.rsqrt(jnp.mean(jnp.square(_ctx_1024t)) + 1e-12) * 0.953939
        ctx_1024 = 2.81802e-05 + 1.00001 * (_ctx_1024t + 0.3 * jax.random.normal(jax.random.fold_in(_rk, 611), (4, 1024, 512), jnp.float32))
        return (x, ctx_1024)
    x, ctx_1024 = _rec_inputs()

    def _L0_attn_setup():
        import jax, jax.numpy as jnp
        import numpy as np
        HIDDEN = 1024
        HEADS = 16
        HEAD_DIM = HIDDEN // HEADS
        NEG = -10000000000.0
        key = jax.random.key(seed)
        k1, k2, k3 = jax.random.split(key, 3)
        x = jax.random.normal(k1, (2, 1024, HIDDEN), dtype=jnp.float32)
        w_qkv = jax.random.normal(k2, (HIDDEN, 3 * HIDDEN), dtype=jnp.float32) / np.sqrt(HIDDEN)
        w_out = jax.random.normal(k3, (HIDDEN, HIDDEN), dtype=jnp.float32) / np.sqrt(HIDDEN)
        return {'x': x, 'w_qkv': w_qkv, 'w_out': w_out}
    _L0_attn_all = _L0_attn_setup()
    _L0_attn_in = {k: v for k, v in _L0_attn_all.items() if k in ('w_qkv', 'w_out')}
    del _L0_attn_all

    def _L0_xattn_setup():
        import jax, jax.numpy as jnp
        import numpy as np
        key = jax.random.key(seed)
        ks = jax.random.split(key, 6)
        B, L, N, C, D = (8, 256, 1024, 512, 128)
        return {'teacher_logits': jax.random.normal(ks[0], (B, L, N), dtype=jnp.float32), 'teacher_features': jax.random.normal(ks[1], (B, N, C), dtype=jnp.float32), 'Wq': jax.random.normal(ks[2], (D, C), dtype=jnp.float32) * (1.0 / np.sqrt(C)), 'bq': jnp.zeros((D,), dtype=jnp.float32), 'Wk': jax.random.normal(ks[3], (D, C), dtype=jnp.float32) * (1.0 / np.sqrt(C)), 'bk': jnp.zeros((D,), dtype=jnp.float32)}
    _L0_xattn_all = _L0_xattn_setup()
    _L0_xattn_in = {k: v for k, v in _L0_xattn_all.items() if k in ('Wq', 'bq', 'Wk', 'bk')}
    del _L0_xattn_all

    def _L0_ffn_setup():
        import jax, jax.numpy as jnp
        import numpy as np
        B, T, D = (4, 512, 1024)
        N, S, H = (8, 8, 8)
        ETA = 1.0
        key = jax.random.key(seed)
        ks = jax.random.split(key, 9)
        return {'x': jax.random.normal(ks[0], (B, T, D), jnp.float32), 'select_weight': jax.random.normal(ks[1], (N, D, S), jnp.float32) / D, 'select_mean_diff': jax.random.normal(ks[2], (N, D), jnp.float32) / D, 'imp_center': jax.random.normal(ks[3], (N,), jnp.float32), 'imp_slope': jax.random.normal(ks[4], (N,), jnp.float32) * 5.0, 'lora_update': jax.random.normal(ks[5], (N, D, H), jnp.float32) * 0.02, 'lora_degen': jax.random.normal(ks[6], (N, D, H), jnp.float32) * 0.02, 'bias_w': jax.random.normal(ks[7], (N, D), jnp.float32) * 0.02, 'debias_w': jax.random.normal(ks[8], (N, D), jnp.float32) * 0.02}
    _L0_ffn_all = _L0_ffn_setup()
    _L0_ffn_in = {k: v for k, v in _L0_ffn_all.items() if k in ('select_weight', 'select_mean_diff', 'imp_center', 'imp_slope', 'lora_update', 'lora_degen', 'bias_w', 'debias_w')}
    del _L0_ffn_all
    return {'x': x, 'ctx_1024': ctx_1024, 'L0_attn_w_qkv': _L0_attn_in['w_qkv'], 'L0_attn_w_out': _L0_attn_in['w_out'], 'L0_xattn_Wq': _L0_xattn_in['Wq'], 'L0_xattn_bq': _L0_xattn_in['bq'], 'L0_xattn_Wk': _L0_xattn_in['Wk'], 'L0_xattn_bk': _L0_xattn_in['bk'], 'L0_ffn_select_weight': _L0_ffn_in['select_weight'], 'L0_ffn_select_mean_diff': _L0_ffn_in['select_mean_diff'], 'L0_ffn_imp_center': _L0_ffn_in['imp_center'], 'L0_ffn_imp_slope': _L0_ffn_in['imp_slope'], 'L0_ffn_lora_update': _L0_ffn_in['lora_update'], 'L0_ffn_lora_degen': _L0_ffn_in['lora_degen'], 'L0_ffn_bias_w': _L0_ffn_in['bias_w'], 'L0_ffn_debias_w': _L0_ffn_in['debias_w']}

def reference(x, ctx_1024, L0_attn_w_qkv, L0_attn_w_out, L0_xattn_Wq, L0_xattn_bq, L0_xattn_Wk, L0_xattn_bk, L0_ffn_select_weight, L0_ffn_select_mean_diff, L0_ffn_imp_center, L0_ffn_imp_slope, L0_ffn_lora_update, L0_ffn_lora_degen, L0_ffn_bias_w, L0_ffn_debias_w):
    import jax
    import jax.numpy as jnp

    def _L0_attn_ref(x, w_qkv, w_out):
        import jax, jax.numpy as jnp
        import numpy as np
        HIDDEN = 1024
        HEADS = 16
        HEAD_DIM = HIDDEN // HEADS
        NEG = -10000000000.0
        b, s, _ = x.shape
        qkv = x @ w_qkv
        qkv = qkv.reshape(b, s, 3, HEADS, HEAD_DIM)
        q, k, v = (qkv[:, :, 0], qkv[:, :, 1], qkv[:, :, 2])
        scale = jnp.sqrt(jnp.float32(HEAD_DIM)).astype(x.dtype)
        q = q / scale
        scores = jnp.einsum('bqhd,bkhd->bhqk', q, k)
        causal_mask = jnp.arange(s)[:, None] >= jnp.arange(s)[None, :]
        scores = jnp.where(causal_mask[None, None], scores, NEG)
        attn = jax.nn.softmax(scores, axis=-1)
        out = jnp.einsum('bhqk,bkhd->bqhd', attn, v).reshape(b, s, HIDDEN)
        return out @ w_out

    def _L0_xattn_ref(teacher_logits, teacher_features, Wq, bq, Wk, bk):
        import jax, jax.numpy as jnp
        import numpy as np
        query = jnp.einsum('bnc,dc->bnd', teacher_features, Wq) + bq
        key = jnp.einsum('bnc,dc->bnd', teacher_features, Wk) + bk
        energy = jnp.einsum('bnd,bmd->bnm', query, key)
        attention = jax.nn.softmax(energy, axis=-1)
        x_m = jnp.einsum('bln,bmn->blm', teacher_logits, attention)
        return x_m

    def _L0_ffn_ref(x, select_weight, select_mean_diff, imp_center, imp_slope, lora_update, lora_degen, bias_w, debias_w):
        import jax, jax.numpy as jnp
        import numpy as np
        B, T, D = (4, 512, 1024)
        N, S, H = (8, 8, 8)
        ETA = 1.0
        x_diff = x[:, None, :, :] - select_mean_diff[None, :, None, :]
        x_diff = x_diff / jnp.linalg.norm(x_diff, axis=3, keepdims=True)
        cont = jnp.einsum('nds,bntd->bnts', select_weight, x_diff) ** 2
        score = cont.sum(axis=-1)
        gate = jax.nn.sigmoid(imp_slope[None, :, None] * (score - imp_center[None, :, None]))
        sel_scale = gate.max(axis=1)[..., None]
        sel_idx = gate.argmax(axis=1)
        debias = jnp.take(debias_w, sel_idx, axis=0)
        bias = jnp.take(bias_w, sel_idx, axis=0)
        upd = jnp.take(lora_update, sel_idx, axis=0)
        dgn = jnp.take(lora_degen, sel_idx, axis=0)
        x_debias = x - debias
        mod_x = jnp.einsum('btdh,btd->bth', upd, x_debias)
        degen_up = jnp.einsum('btdh,bth->btd', dgn, mod_x)
        mod_x_bias = ETA * (bias + degen_up)
        return (1.0 - sel_scale) * x + sel_scale * mod_x_bias
    x = x + _L0_attn_ref(_layernorm(x, axis=-1), L0_attn_w_qkv, L0_attn_w_out)
    x = x + _L0_xattn_ref(_layernorm(x, axis=-1), ctx_1024, L0_xattn_Wq, L0_xattn_bq, L0_xattn_Wk, L0_xattn_bk)
    x = x + _L0_ffn_ref(_layernorm(x, axis=-1), L0_ffn_select_weight, L0_ffn_select_mean_diff, L0_ffn_imp_center, L0_ffn_imp_slope, L0_ffn_lora_update, L0_ffn_lora_degen, L0_ffn_bias_w, L0_ffn_debias_w)
    return x

_drawn_inputs = setup_inputs


def setup_inputs(seed=0):
    import zlib

    import numpy as np

    out = dict(_drawn_inputs(seed))
    spreads = {'L0_xattn_bq': (0.0, 0.1), 'L0_xattn_bk': (0.0, 2.0)}
    factors = {'L0_ffn_bias_w': 3.542, 'L0_ffn_debias_w': 64.0}
    for name, (base, spread) in spreads.items():
        noise = np.random.default_rng([zlib.crc32(name.encode()), seed]).standard_normal(out[name].shape)
        drawn = base * np.exp(spread * noise) if base else spread * noise
        out[name] = jnp.asarray(drawn.astype(out[name].dtype))
    for name, factor in factors.items():
        out[name] = (out[name] * factor).astype(out[name].dtype)
    return out
```

```python
from contextlib import ExitStack

import concourse.bass as bass
from concourse import mybir

F32 = mybir.dt.float32
F32R = mybir.dt.float32r
BF16 = mybir.dt.bfloat16
ALU = mybir.AluOpType
ACT = mybir.ActivationFunctionType
AX_X = mybir.AxisListType.X

P = 128
BATCH, SEQ, DM = 4, 1024, 1024
HEADS, HD = 16, 64
PAIRS = HEADS // 2
TB = SEQ // P
KC = DM // P
CTX, CD = 512, 128
CC = CTX // P
EXPERTS, SEL, LOW = 8, 8, 8
FW = EXPERTS * SEL + EXPERTS * LOW + EXPERTS
GK = EXPERTS * LOW + EXPERTS
HALF = 512
EPS = 1e-5
NEG = -1e10
A, B = 0, 1



def attention_order(last):
    parts = [("proj", t, h, k) for t in range(3) for h in range(2) for k in range(2)]
    order = []

    def s(j, qb):
        order.append(("scores", j, qb))

    def t(j, g, kb):
        order.append(("turn", j, g, kb))

    def m(j, g, kb):
        order.append(("mix", j, g, kb))

    def p(n=1):
        for _ in range(n):
            if parts and not last:
                order.append(parts.pop(0))

    def early(j):
        s(j, 4); p(); t(j, 0, 0); s(j, 5); t(j, 0, 1); m(j, 0, 0)
        p(); s(j, 6); t(j, 0, 2); m(j, 0, 1); s(j, 7); t(j, 0, 3); m(j, 0, 2)

    order.append(("stack", B))
    s(A, 0); p(); s(A, 1); s(A, 2); p(); s(A, 3); order.append(("vturn", B)); p()
    early(A); p(); m(A, 0, 3)
    s(B, 0); p(); t(A, 1, 0); s(B, 1); t(A, 1, 1); m(A, 1, 0); p(); s(B, 2); t(A, 1, 2); m(A, 1, 1)
    p(); s(B, 3); t(A, 1, 3); m(A, 1, 2); t(A, 1, 4); m(A, 1, 3); p(); t(A, 1, 5); m(A, 1, 4)
    t(A, 1, 6); m(A, 1, 5); t(A, 1, 7); m(A, 1, 6); m(A, 1, 7)
    early(B); p(); m(B, 0, 3)
    if not last:
        assert not parts
        order.append(("stack", "next"))
    t(B, 1, 0)
    for kb in range(1, TB):
        t(B, 1, kb)
        if kb == 3 and not last:
            order.append(("vturn", "next"))
        m(B, 1, kb - 1)
    m(B, 1, TB - 1)
    return order


def decoder_layer(nc, x, w_qkv, w_out, ctx_t, w_ctx, b_ctx, w_ffn, v_ffn, w_up, center, slope, out):
    es = ExitStack()
    with es:
        def sem(name):
            return es.enter_context(nc.semaphore(name))

        def sb(stack, name, shape, dt=F32):
            return stack.enter_context(nc.sbuf_tensor(name, shape, dt))

        ident = sb(es, "ident", [P, P])
        ident_bf = sb(es, "ident_bf", [P, P], BF16)
        mask_bf = sb(es, "mask_bf", [P, P], BF16)
        ffn_hi = sb(es, "ffn_hi", [P, KC, FW], F32R)
        ffn_lo = sb(es, "ffn_lo", [P, KC, FW], F32R)
        up_hi = sb(es, "up_hi", [GK, DM], F32R)
        up_lo = sb(es, "up_lo", [GK, DM], F32R)
        ffn_c = sb(es, "ffn_c", [P, FW])
        center_b = sb(es, "center_b", [P, EXPERTS])
        slope_b = sb(es, "slope_b", [P, EXPERTS])
        rank = sb(es, "rank", [P, EXPERTS])
        neg_half = sb(es, "neg_half", [P, 1])
        bias_c = sb(es, "bias_c", [P, 2])
        otx = sb(es, "otx", [P, TB, KC, P])
        w_raw = sb(es, "w_raw", [P, 2, CC, P])
        w_hi = sb(es, "w_hi", [P, 3, CC, P], F32R)
        w_lo = sb(es, "w_lo", [P, 3, CC, P], F32R)
        bn = sb(es, "bn", [P, 2, 2, 6])
        mv = sb(es, "mv", [P, 2, 2])
        veps = sb(es, "veps", [P, 2])
        rstd = sb(es, "rstd", [P, 2])
        low = sb(es, "low", [P, 2 * HEADS])
        den = sb(es, "den", [P, 2 * HEADS])
        rden = sb(es, "rden", [P, 2 * HEADS])

        with ExitStack() as s0:
            ffn_raw = sb(s0, "ffn_raw", [P, KC, FW])
            vec_raw = sb(s0, "vec_raw", [P, KC, 2 * EXPERTS])
            ffn_prod = sb(s0, "ffn_prod", [P, KC, FW])
            up_raw = sb(s0, "up_raw", [GK, DM])
            ones = sb(s0, "ones", [P, P])
        with ExitStack() as s1:
            xt_hi = sb(s1, "xt_hi", [P, KC, SEQ], F32R)
            xt_lo = sb(s1, "xt_lo", [P, KC, SEQ], F32R)
            with ExitStack() as s2:
                x_in = sb(s2, "x_in", [P, 2, DM])
                xn = sb(s2, "xn", [P, 2, DM])
            qkv = sb(s1, "qkv", [P, 3, SEQ])
            q_st = [sb(s1, f"q_st{j}", [P, SEQ], F32R) for j in range(2)]
            k_hi = [sb(s1, f"k_hi{j}", [P, SEQ], F32R) for j in range(2)]
            k_lo = [sb(s1, f"k_lo{j}", [P, SEQ], F32R) for j in range(2)]
            v_st = [sb(s1, f"v_st{j}", [P, TB, 2 * HD], F32R) for j in range(2)]
            probs = sb(s1, "probs", [P, TB * (TB + 1) // 2 * P])
            pt_hi = sb(s1, "pt_hi", [P, 2, HALF], F32R)
            pt_lo = sb(s1, "pt_lo", [P, 2, HALF], F32R)
            o_lo = sb(s1, "o_lo", [HD, HALF])
        with ExitStack() as s3:
            wo_hi = sb(s3, "wo_hi", [P, KC, DM], F32R)
            wo_lo = sb(s3, "wo_lo", [P, KC, DM], F32R)
            wo_raw = sb(s3, "wo_raw", [P, 2, DM])
            o_hi = sb(s3, "o_hi", [P, 2, KC, P], F32R)
            o_rest = sb(s3, "o_rest", [P, 2, KC, P], F32R)
            x_res = sb(s3, "x_res", [P, 2, DM])
        with ExitStack() as s4:
            at_hi = sb(s4, "at_hi", [P, KC, DM], F32R)
            at_lo = sb(s4, "at_lo", [P, KC, DM], F32R)
            with ExitStack() as s5:
                wc_raw = sb(s5, "wc_raw", [P, 2, CC, CD])
                wc_hi = sb(s5, "wc_hi", [P, 2, CC, CD], F32R)
                wc_lo = sb(s5, "wc_lo", [P, 2, CC, CD], F32R)
                ctx_raw = sb(s5, "ctx_raw", [P, CC, HALF])
                ctx_hi = sb(s5, "ctx_hi", [P, CC, HALF], F32R)
                ctx_lo = sb(s5, "ctx_lo", [P, CC, HALF], F32R)
                qk_hi = sb(s5, "qk_hi", [P, 2, SEQ], F32R)
                qk_lo = sb(s5, "qk_lo", [P, 2, SEQ], F32R)
                c_probs = sb(s5, "c_probs", [P, 2, SEQ])
            with ExitStack() as s6:
                xn2 = sb(s6, "xn2", [P, DM])
                xn3 = sb(s6, "xn3", [P, DM])
                t2_hi = sb(s6, "t2_hi", [P, KC, P], F32R)
                t2_lo = sb(s6, "t2_lo", [P, KC, P], F32R)
                t3_hi = sb(s6, "t3_hi", [P, KC, P], F32R)
                t3_lo = sb(s6, "t3_lo", [P, KC, P], F32R)
                sel_u = sb(s6, "sel_u", [P, EXPERTS * SEL])
                sel_sq = sb(s6, "sel_sq", [P, EXPERTS * SEL])
                g8 = sb(s6, "g8", [P, 12, EXPERTS])
                g1 = sb(s6, "g1", [P, 8])
                low_h = sb(s6, "low_h", [P, GK])
                lt_hi = sb(s6, "lt_hi", [GK, P], F32R)
                lt_lo = sb(s6, "lt_lo", [GK, P], F32R)

        ps_s = [es.enter_context(nc.psum_tensor(f"ps_s{i}", [P, DM], F32)) for i in range(2)]
        ps_t = [es.enter_context(nc.psum_tensor(f"ps_t{i}", [P, HALF], F32)) for i in range(2)]
        ps_o = es.enter_context(nc.psum_tensor("ps_o", [P, HALF], F32))
        ps_p = es.enter_context(nc.psum_tensor("ps_p", [P, HALF], F32))

        phase_done = sem("phase_done")
        passed = sem("passed")
        PHASES = 5
        setup_in, setup_cst, setup_prod, setup_mm, setup_split = (
            sem(n) for n in ("setup_in", "setup_cst", "setup_prod", "setup_mm", "setup_split"))
        ln_in = [sem(f"ln_in{s}") for s in range(2)]
        ln_bn, ln_mv, ln_ve, ln_rs, ln_xn, ln_turn, ln_hi, ln_lo = (
            sem(n) for n in ("ln_bn", "ln_mv", "ln_ve", "ln_rs", "ln_xn", "ln_turn", "ln_hi", "ln_lo"))
        w_in = [sem(f"w_in{s}") for s in range(2)]
        w_hi_ok, w_split, part_ok, proj_out = (sem(n) for n in ("w_hi_ok", "w_split", "part_ok", "proj_out"))
        q_hi_ok, k_hi_ok, k_lo_ok, stack_ok = (sem(n) for n in ("q_hi_ok", "k_hi_ok", "k_lo_ok", "stack_ok"))
        scores_ok, low_ok, exp_ok, rden_ok, norm_ok = (
            sem(n) for n in ("scores_ok", "low_ok", "exp_ok", "rden_ok", "norm_ok"))
        turn_ok, hi_ok, lo_ok, mix_ok, o_lo_ok, o_ok = (
            sem(n) for n in ("turn_ok", "hi_ok", "lo_ok", "mix_ok", "o_lo_ok", "o_ok"))
        wo_in = [sem(f"wo_in{s}") for s in range(2)]
        wo_hi_ok, wo_ok, st_hi, st_ok, out_mm, x1_ok = (
            sem(n) for n in ("wo_hi_ok", "wo_ok", "st_hi", "st_ok", "out_mm", "x1_ok"))
        xr_in = [sem(f"xr_in{s}") for s in range(2)]
        c_win, c_in, c_whi, c_wok, c_hi, c_split, c_mm, c_qhi, c_qk = (
            sem(n) for n in ("c_win", "c_in", "c_whi", "c_wok", "c_hi", "c_split", "c_mm", "c_qhi", "c_qk"))
        e_mm, e_mx, e_neg, e_exp, e_rd, e_norm, e_turn, e_hi, e_lo = (
            sem(n) for n in ("e_mm", "e_mx", "e_neg", "e_exp", "e_rd", "e_norm", "e_turn", "e_hi", "e_lo"))
        t_bn, t_mv, t_ve, t_rs, t_xn2, t_xn3 = (sem(n) for n in ("t_bn", "t_mv", "t_ve", "t_rs", "t_xn2", "t_xn3"))
        t_turn, t_hi, t_lo, xm_ok, x2_ok = (sem(n) for n in ("t_turn", "t_hi", "t_lo", "xm_ok", "x2_ok"))
        f_mm, f_step, f_e, f_z, f_w, f_x, f_g, l_turn, l_hi, l_ok, u_mm, y_ok, y_out = (
            sem(n) for n in ("f_mm", "f_step", "f_e", "f_z", "f_w", "f_x", "f_g", "l_turn", "l_hi", "l_ok", "u_mm", "y_ok", "y_out"))

        C_EXP, C_LO, C_TURN, C_MIX, C_O, C_PROJ, C_SCORES, C_PART, C_SPLIT = 2, 2, 26, 24, 1, 1, 16, 6, 2
        C_LN_TURN, C_LN, C_OUT, C_ONE = 4, 2, 2, 1

        body, tail_body = attention_order(False), attention_order(True)
        TURNS = sum(e[0] in ("turn", "vturn") for e in body)
        MIXES = sum(e[0] == "mix" for e in body)
        TURNS_B = 1 + (PAIRS - 1) * TURNS + sum(e[0] in ("turn", "vturn") for e in tail_body)
        assert TURNS % 2 == 0 and TURNS_B % 2 == 0 and C_TURN == TURNS and C_MIX == MIXES

        def numbered(order, kinds):
            n, at = 0, {}
            for e in order:
                if e[0] in kinds:
                    at[e] = n
                    n += 1
            return at

        body_turns, body_mixes = numbered(body, ("turn", "vturn")), numbered(body, ("mix",))
        tail_turns = numbered(tail_body, ("turn", "vturn"))
        assert numbered(tail_body, ("mix",)) == body_mixes
        prev_last_turn = {g: body_turns[("turn", B, g, 4 * g + 3)] for g in range(2)}

        def off(qb):
            return qb * (qb + 1) // 2 * P

        def cols(g, kb):
            return max(kb - 4 * g, 0) * P

        def opposite(j):
            return slice(HD * (1 - j), HD * (1 - j) + HD)

        def own(j):
            return slice(HD * j, HD * j + HD)

        def f(ap):
            return ap.bitcast(F32)

        def alone(eng):
            eng.sem_inc(passed, 1)

        def end_phase(eng, b, k):
            alone(eng)
            eng.drain().then_inc(phase_done, 1)
            eng.wait_ge(phase_done, b * (5 * PHASES) + 5 * (k + 2))
            alone(eng)

        def end_setup(eng):
            eng.drain().then_inc(phase_done, 1)
            eng.wait_ge(phase_done, 5)

        def turns4(ps, half):
            return ps[:, :].rearrange("p (k t) -> p k t", k=4)

        def turn_base(b, i, k):
            base = b * (4 * TB)
            if isinstance(i, int):
                if k == 0:
                    return base + (0 if i == 0 else 2 if i == 1 else 4 * i - 2)
                return base + (4 * i + 4 if i < TB - 1 else 4 * TB - 2)
            return base + i * 4 - 2 if k == 0 else base + i * 4 + 4

        def norm_base(b, i, k):
            base = b * (2 * TB)
            if k == 0:
                return base + (0 if isinstance(i, int) and i == 0 else i * 2 - 1)
            return base + (2 * TB - 1 if isinstance(i, int) and i == TB - 1 else i * 2 + 2)

        with nc.Block() as block:

            @block.sync
            def _(sp):
                sp.dma_start(ffn_raw[:, :, :], w_ffn.rearrange("(k p) c -> p k c", p=P)).then_inc(setup_in, 16)
                sp.dma_start(vec_raw[:, :, :], v_ffn.rearrange("(k p) c -> p k c", p=P)).then_inc(setup_in, 16)
                sp.dma_start(up_raw[:, :], w_up).then_inc(setup_in, 16)
                sp.dma_start(center_b[:, :], center.broadcast_to([P, EXPERTS])).then_inc(setup_in, 16)
                sp.dma_start(slope_b[:, :], slope.broadcast_to([P, EXPERTS])).then_inc(setup_in, 16)
                sp.dma_start(bias_c[:, :], b_ctx).then_inc(setup_in, 16)
                for u in range(2):
                    sp.dma_start(w_raw[:, u, :, :], w_qkv[0, :, u]).then_inc(w_in[u], 16)
                sp.wait_ge(setup_in, 96)
                end_setup(sp)

                with sp.Fori(0, BATCH) as b:
                    with sp.Fori(0, TB // 2) as v:
                        for s in range(2):
                            sp.wait_ge(ln_xn, b * TB + v * 2 + s + 1)
                            alone(sp)
                            sp.dma_start(x_in[:, s, :], x[b, v * 2 + s]).then_inc(ln_in[s], 16)
                    end_phase(sp, b, 0)

                    with sp.Fori(0, 3 * PAIRS - 1) as t:
                        for u in range(2):
                            sp.wait_ge(w_split, b * (6 * PAIRS) + t * 2 + u + C_SPLIT + 1)
                            alone(sp)
                            sp.dma_start(w_raw[:, u, :, :], w_qkv[t + 1, :, u]).then_inc(w_in[u], 16)
                    for u in range(2):
                        sp.wait_ge(w_split, b * (6 * PAIRS) + 6 * PAIRS - 2 + u + C_SPLIT + 1)
                        alone(sp)
                        sp.dma_start(w_raw[:, u, :, :], w_qkv[0, :, u]).then_inc(w_in[u], 16)
                    end_phase(sp, b, 1)

                    with sp.Fori(0, KC // 2) as v:
                        for s in range(2):
                            sp.wait_ge(wo_ok, b * KC + v * 2 + s + 1)
                            alone(sp)
                            sp.dma_start(wo_raw[:, s, :], w_out[v * 2 + s]).then_inc(wo_in[s], 16)
                    with sp.Fori(0, TB // 2) as v:
                        for s in range(2):
                            sp.wait_ge(x1_ok, b * TB + v * 2 + s + 1)
                            alone(sp)
                            sp.dma_start(x_res[:, s, :], x[b, v * 2 + s]).then_inc(xr_in[s], 16)
                    end_phase(sp, b, 2)

                    sp.dma_start(wc_raw[:, :, :, :], w_ctx).then_inc(c_win, 16)
                    for h in range(2):
                        sp.wait_ge(c_split, b * 2 + h + 1)
                        alone(sp)
                        sp.dma_start(ctx_raw[:, :, :], ctx_t[b, :, :, h * HALF:(h + 1) * HALF]).then_inc(c_in, 16)
                    end_phase(sp, b, 3)

                    with sp.Fori(0, TB) as i:
                        sp.wait_ge(y_ok, b * TB + i + 1 + C_ONE)
                        alone(sp)
                        sp.dma_start(out[b, i], otx[:, i, :, :].rearrange("p k t -> p (k t)")).then_inc(y_out, 16)
                    sp.wait_ge(y_out, b * (16 * TB) + 16 * TB)
                    alone(sp)
                    end_phase(sp, b, 4)

            @block.tensor
            def _(pe):
                def split_mm(ps, lhs, rhs, n, steps, start, stop):
                    for k in steps:
                        (lh, ll), (rh, rl) = lhs(k), rhs(k)
                        pe.matmul(ps, lh, rh, start=start and k == steps[0], stop=False)
                        pe.matmul(ps, lh, rl, start=False, stop=False)
                        mm = pe.matmul(ps, ll, rh, start=False, stop=stop and k == steps[-1])
                    return mm

                pe.wait_ge(setup_prod, 1)
                pe.wait_ge(setup_cst, 1)
                for k in range(KC):
                    mm = pe.matmul(ps_p[:, 0:FW], ones[:, :], ffn_prod[:, k, :], start=k == 0, stop=k == KC - 1)
                mm.then_inc(setup_mm, 1)
                end_setup(pe)

                def project(b, pair, t, h, k):
                    n = b * PAIRS + pair
                    if k == 0:
                        pe.wait_ge(proj_out, n * 6 + 2 * t + h + C_PROJ)
                    if h == 0:
                        pe.wait_ge(w_split, n * 6 + 2 * t + k + 1 + C_SPLIT)
                    slot = (2 * t + k) % 3
                    split_mm(ps_p[:, :],
                             lambda c: (w_hi[:, slot, c - 4 * k, :], w_lo[:, slot, c - 4 * k, :]),
                             lambda c: (xt_hi[:, c, h * HALF:(h + 1) * HALF], xt_lo[:, c, h * HALF:(h + 1) * HALF]),
                             HALF, list(range(4 * k, 4 * k + 4)), k == 0, k == 1).then_inc(part_ok, 1)

                def turn_values(b, pair, j, turn, bank):
                    pe.wait_ge(lo_ok, turn + C_LO - 1)
                    pe.wait_ge(proj_out, (b * PAIRS + pair) * 6 + 6 + C_PROJ)
                    alone(pe)
                    for kb in range(TB):
                        mm = pe.transpose(bank[:, kb * HD:(kb + 1) * HD],
                                          qkv[own(j), 2, kb * P:(kb + 1) * P], ident[own(j), own(j)])
                    mm.then_inc(turn_ok, 1)

                def attend(b, hp, order, turns):
                    n = b * PAIRS + hp
                    t0 = b * TURNS_B + hp * TURNS + 1
                    for e in order:
                        if e[0] == "scores":
                            _, j, qb = e
                            i, w = 8 * j + qb, (qb + 1) * P
                            pe.wait_ge(exp_ok, n * 16 + i + C_EXP - 1)
                            if qb == 0:
                                pe.wait_ge(stack_ok, n * 2 + j + 1)
                            q = q_st[j][:, qb * P:(qb + 1) * P]
                            for c in range(0, w, HALF):
                                d = min(c + HALF, w)
                                o = ps_s[qb % 2][:, c:d]
                                pe.matmul(o, q, k_hi[j][:, c:d], start=True, stop=False)
                                pe.matmul(o, q, k_lo[j][:, c:d], start=False, stop=True)
                            mm = pe.matmul(ps_s[qb % 2][:, w - P:w], ident_bf[:, :], mask_bf[:, :],
                                           start=False, stop=True, skip_group_check=True)
                            mm.then_inc(scores_ok, 1)
                        elif e[0] == "turn":
                            _, j, g, kb = e
                            pe.wait_ge(lo_ok, t0 + turns[e] + C_LO - 1)
                            if kb == 0:
                                pe.wait_ge(norm_ok, n * 16 + 8 * j + 4 * g + 4)
                            for qb in range(max(4 * g, kb), 4 * g + 4):
                                mm = pe.transpose(ps_t[(1 + turns[e]) % 2][:, (qb - 4 * g) * P:(qb - 4 * g + 1) * P],
                                                  probs[:, off(qb) + kb * P:off(qb) + (kb + 1) * P], ident[:, :])
                            mm.then_inc(turn_ok, 1)
                        elif e[0] == "mix":
                            _, j, g, kb = e
                            pe.wait_ge(lo_ok, t0 + turns[("turn", j, g, kb)] + 1 + C_LO)
                            if kb == 0:
                                pe.wait_ge(o_ok, n * 4 + 2 * j + g + C_O)
                            s, c, end = body_mixes[e] % 2, cols(g, kb), kb == 4 * g + 3
                            pe.matmul(ps_o[:, c:HALF], v_st[j][:, kb, :], pt_hi[:, s, c:HALF],
                                      start=kb == 0, stop=False)
                            mm = pe.matmul(ps_o[:, c:HALF], v_st[j][:, kb, :], pt_lo[:, s, c:HALF],
                                           start=False, stop=end)
                            mm.then_inc(mix_ok, 1)
                        elif e[0] == "vturn":
                            bank = ps_t[(1 + turns[e]) % 2]
                            if e[1] == B:
                                turn_values(b, hp, B, t0 + turns[e], bank)
                            else:
                                turn_values(b, hp + 1, A, t0 + turns[e], bank)
                        elif e[0] == "proj":
                            project(b, hp + 1, *e[1:])

                pe.sem_inc(turn_ok, C_TURN)
                pe.sem_inc(mix_ok, C_MIX)
                pe.sem_inc(scores_ok, C_SCORES)
                pe.sem_inc(part_ok, C_PART)
                pe.sem_inc(ln_turn, C_LN_TURN)
                pe.sem_inc(out_mm, C_OUT)
                pe.sem_inc(u_mm, C_ONE)

                with pe.Fori(0, BATCH) as b:
                    with pe.Fori(0, TB // 2) as v:
                        for s in range(2):
                            for h in range(2):
                                if h == 0:
                                    pe.wait_ge(ln_xn, b * TB + v * 2 + s + 1 + C_LN)
                                pe.wait_ge(ln_lo, b * (2 * TB) + v * 4 + 2 * s + h + 1)
                                for c in range(4):
                                    mm = pe.transpose(ps_t[h][:, c * P:(c + 1) * P],
                                                      xn[:, s, (4 * h + c) * P:(4 * h + c + 1) * P], ident[:, :])
                                mm.then_inc(ln_turn, 1)
                    end_phase(pe, b, 0)

                    for t in range(3):
                        for h in range(2):
                            for k in range(2):
                                project(b, 0, t, h, k)
                    turn_values(b, 0, A, b * TURNS_B, ps_t[0])
                    with pe.Fori(0, PAIRS - 1) as hp:
                        attend(b, hp, body, body_turns)
                    attend(b, PAIRS - 1, tail_body, tail_turns)
                    end_phase(pe, b, 1)

                    with pe.Fori(0, TB // 2) as v:
                        for s in range(2):
                            pe.wait_ge(st_ok, b * TB + v * 2 + s + 1)
                            pe.wait_ge(wo_ok, b * KC + KC + 2)
                            pe.wait_ge(x1_ok, b * TB + v * 2 + s + 1)
                            for h in range(2):
                                r = slice(h * HALF, (h + 1) * HALF)
                                mm = split_mm(ps_s[s][:, r], lambda c: (o_hi[:, s, c, :], o_rest[:, s, c, :]),
                                              lambda c: (wo_hi[:, c, r], wo_lo[:, c, r]), HALF, list(range(KC)), True, True)
                            mm.then_inc(out_mm, 1)
                    end_phase(pe, b, 2)

                    pe.wait_ge(c_wok, b + 1)
                    for h in range(2):
                        pe.wait_ge(c_split, b * 2 + h + 1 + 1)
                        for t in range(2):
                            if h == 1:
                                pe.wait_ge(c_qk, b * 4 + t + 1)
                            split_mm(ps_t[t][:, :], lambda c: (wc_hi[:, t, c, :], wc_lo[:, t, c, :]),
                                     lambda c: (ctx_hi[:, c, :], ctx_lo[:, c, :]), HALF, list(range(CC)),
                                     True, True).then_inc(c_mm, 1)
                    pe.wait_ge(c_qk, b * 4 + 4)

                    def energy(mb):
                        if mb >= 2:
                            pe.wait_ge(e_exp, b * TB + mb - 1)
                        q = slice(mb * P, (mb + 1) * P)
                        for h in range(2):
                            r = slice(h * HALF, (h + 1) * HALF)
                            mm = split_mm(ps_s[mb % 2][:, r], lambda c: (qk_hi[:, 0, q], qk_lo[:, 0, q]),
                                          lambda c: (qk_hi[:, 1, r], qk_lo[:, 1, r]), HALF, [0], True, True)
                        mm.then_inc(e_mm, 1)

                    def turn_energy(mb):
                        pe.wait_ge(e_norm, b * TB + mb + 1)
                        for h in range(2):
                            if mb >= 1:
                                pe.wait_ge(e_lo, b * (2 * TB) + 2 * mb + h - 1)
                            for c in range(4):
                                mm = pe.transpose(ps_t[h][:, c * P:(c + 1) * P],
                                                  c_probs[:, mb % 2, (4 * h + c) * P:(4 * h + c + 1) * P], ident[:, :])
                            mm.then_inc(e_turn, 1)

                    for mb in range(TB):
                        energy(mb)
                        if mb >= 1:
                            turn_energy(mb - 1)
                    turn_energy(TB - 1)
                    end_phase(pe, b, 3)

                    def turn_block(i, k, src, ready):
                        pe.wait_ge(ready, b * TB + i + 1)
                        for h in range(2):
                            pe.wait_ge(t_lo, turn_base(b, i, k) + h + 1)
                            for c in range(4):
                                mm = pe.transpose(ps_t[h][:, c * P:(c + 1) * P],
                                                  src[:, (4 * h + c) * P:(4 * h + c + 1) * P], ident[:, :])
                            mm.then_inc(t_turn, 1)

                    def cross(i, h):
                        if h == 0:
                            pe.wait_ge(t_lo, turn_base(b, i, 0) + 2 + 2)
                            pe.wait_ge(x2_ok, b * TB + i + 1)
                        r = slice(h * HALF, (h + 1) * HALF)
                        mm = split_mm(ps_s[0][:, r], lambda c: (t2_hi[:, c, :], t2_lo[:, c, :]),
                                      lambda c: (at_hi[:, c, r], at_lo[:, c, r]), HALF, list(range(KC)), True, True)
                        mm.then_inc(xm_ok, 1)

                    def select(i):
                        pe.wait_ge(t_lo, turn_base(b, i, 1) + 2 + 2)
                        pe.wait_ge(f_g, b * TB + i + 1)
                        split_mm(ps_p[:, 0:FW], lambda c: (t3_hi[:, c, :], t3_lo[:, c, :]),
                                 lambda c: (ffn_hi[:, c, :], ffn_lo[:, c, :]), FW, list(range(KC)),
                                 True, True).then_inc(f_mm, 1)

                    def turn_low(i):
                        pe.wait_ge(f_g, b * TB + i + 1 + 1)
                        pe.wait_ge(l_ok, b * TB + i + 1)
                        pe.transpose(ps_o[0:GK, 0:P], low_h[:, :], ident[:, :]).then_inc(l_turn, 1)

                    def expand(i):
                        pe.wait_ge(l_ok, b * TB + i + 1 + 1)
                        pe.wait_ge(y_ok, b * TB + i + 1)
                        for h in range(2):
                            r = slice(h * HALF, (h + 1) * HALF)
                            mm = split_mm(ps_s[1][:, r], lambda c: (lt_hi[:, :], lt_lo[:, :]),
                                          lambda c: (up_hi[:, r], up_lo[:, r]), HALF, [0], True, True)
                        mm.then_inc(u_mm, 1)

                    def tail_block(i, first, second, lastone):
                        cross(i, 0)
                        if not first and not second:
                            turn_low(i - 2)
                        if not first:
                            turn_block(i - 1, 1, xn3, t_xn3)
                        if not first and not second:
                            expand(i - 2)
                        cross(i, 1)
                        if not lastone:
                            turn_block(i + 1, 0, xn2, t_xn2)
                        if not first:
                            select(i - 1)

                    turn_block(0, 0, xn2, t_xn2)
                    tail_block(0, True, False, False)
                    tail_block(1, False, True, False)
                    with pe.Fori(2, TB - 1) as i:
                        tail_block(i, False, False, False)
                    tail_block(TB - 1, False, False, True)
                    turn_low(TB - 2)
                    turn_block(TB - 1, 1, xn3, t_xn3)
                    expand(TB - 2)
                    select(TB - 1)
                    turn_low(TB - 1)
                    expand(TB - 1)
                    end_phase(pe, b, 4)

            @block.scalar
            def _(act):
                end_setup(act)
                act.sem_inc(exp_ok, C_EXP)
                act.sem_inc(proj_out, C_PROJ)

                def project(b, pair, t, h, k, reuse):
                    if k == 0:
                        return
                    n = b * PAIRS + pair
                    act.wait_ge(part_ok, n * 12 + 4 * t + 2 * h + 2 + C_PART)
                    if reuse is not None:
                        if t < 2:
                            act.wait_ge(stack_ok, n * 2)
                        else:
                            act.wait_ge(turn_ok, reuse + 1 + C_TURN)
                    act.activation(qkv[:, t, h * HALF:(h + 1) * HALF], ps_p[:, :], ACT.Copy,
                                   scale=-(HD ** -0.5) if t == 0 else 1.0).then_inc(proj_out, 1)

                def stack(b, pair, j):
                    n = b * PAIRS + pair
                    act.wait_ge(proj_out, n * 6 + 4 + C_PROJ)
                    act.wait_ge(scores_ok, n * 16 + 8 * j + 8 - 16 + C_SCORES)
                    act.activation(q_st[j][own(j), :], qkv[own(j), 0, :], ACT.Copy).then_inc(q_hi_ok, 1)
                    act.activation(k_hi[j][own(j), :], qkv[own(j), 1, :], ACT.Copy)
                    act.activation(k_hi[j][opposite(j), :], qkv[own(j), 1, :], ACT.Copy).then_inc(k_hi_ok, 1)

                def split_values(j, turn, bank, mixes):
                    act.wait_ge(turn_ok, turn + 1 + C_TURN)
                    if mixes is not None:
                        act.wait_ge(mix_ok, mixes + C_MIX)
                    act.activation(v_st[j][:, :, 0:HD], bank[:, :].rearrange("p (k d) -> p k d", d=HD),
                                   ACT.Copy).then_inc(hi_ok, 1)

                def attend(b, hp, order, turns):
                    n = b * PAIRS + hp
                    t0 = b * TURNS_B + hp * TURNS + 1
                    for e in order:
                        if e[0] == "scores":
                            _, j, qb = e
                            i, w = 8 * j + qb, (qb + 1) * P
                            act.wait_ge(low_ok, n * 16 + i + 1)
                            if qb % 4 == 0:
                                if j == B:
                                    act.wait_ge(turn_ok, t0 + turns[("turn", A, qb // 4, 4 * (qb // 4) + 3)] + 1 + C_TURN)
                                else:
                                    act.wait_ge(turn_ok, t0 - TURNS + prev_last_turn[qb // 4] + 1 + C_TURN)
                            act.activation(probs[:, off(qb):off(qb) + w], ps_s[qb % 2][:, 0:w], ACT.Exp,
                                           bias=low[:, i:i + 1], scale=-1.0,
                                           accum_out=den[:, i:i + 1]).then_inc(exp_ok, 1)
                        elif e[0] == "turn":
                            _, j, g, kb = e
                            c, m = cols(g, kb), body_mixes[("mix", j, g, kb)]
                            act.wait_ge(turn_ok, t0 + turns[e] + 1 + C_TURN)
                            act.wait_ge(mix_ok, n * MIXES + m - 1 + C_MIX)
                            act.activation(pt_hi[:, m % 2, c:HALF], ps_t[(1 + turns[e]) % 2][:, c:HALF],
                                           ACT.Copy).then_inc(hi_ok, 1)
                        elif e[0] == "mix":
                            _, j, g, kb = e
                            if kb == 4 * g + 3:
                                act.wait_ge(mix_ok, n * MIXES + body_mixes[e] + 1 + C_MIX)
                                act.wait_ge(o_ok, n * 4 + 2 * j + g + C_O)
                                act.activation(o_lo[:, :], ps_o[HD:P, :], ACT.Copy).then_inc(o_lo_ok, 1)
                        elif e[0] == "vturn":
                            bank = ps_t[(1 + turns[e]) % 2]
                            if e[1] == B:
                                split_values(B, t0 + turns[e], bank, n * MIXES)
                            else:
                                split_values(A, t0 + turns[e], bank, n * MIXES + MIXES // 2)
                        elif e[0] == "stack":
                            if e[1] == B:
                                stack(b, hp, B)
                            else:
                                stack(b, hp + 1, A)
                        elif e[0] == "proj":
                            project(b, hp + 1, *e[1:], reuse=t0 + turns[("vturn", B)])

                with act.Fori(0, BATCH) as b:
                    with act.Fori(0, TB // 2) as v:
                        for s in range(2):
                            for h in range(2):
                                act.wait_ge(ln_turn, b * (2 * TB) + v * 4 + 2 * s + h + 1 + C_LN_TURN)
                                act.activation(xt_hi[:, 4 * h:4 * h + 4, bass.ts(v * 2 + s, P)], turns4(ps_t[h], h),
                                               ACT.Copy).then_inc(ln_hi, 1)
                    end_phase(act, b, 0)

                    for t in range(3):
                        for h in range(2):
                            project(b, 0, t, h, 1, None)
                    stack(b, 0, A)
                    split_values(A, b * TURNS_B, ps_t[0], None)
                    with act.Fori(0, PAIRS - 1) as hp:
                        attend(b, hp, body, body_turns)
                    attend(b, PAIRS - 1, tail_body, tail_turns)
                    end_phase(act, b, 1)

                    with act.Fori(0, KC // 2) as v:
                        for s in range(2):
                            act.wait_ge(wo_in[s], b * (16 * KC // 2) + v * 16 + 16)
                            act.activation(wo_hi[:, v * 2 + s, :], wo_raw[:, s, :], ACT.Copy).then_inc(wo_hi_ok, 1)
                    with act.Fori(0, TB // 2) as v:
                        for s in range(2):
                            act.wait_ge(out_mm, b * TB + v * 2 + s + 1)
                            act.activation(o_hi[:, s, :, :], otx[:, v * 2 + s, :, :], ACT.Copy).then_inc(st_hi, 1)
                    end_phase(act, b, 2)

                    act.wait_ge(c_win, b * 16 + 16)
                    act.activation(wc_hi[:, :, :, :], wc_raw[:, :, :, :], ACT.Copy).then_inc(c_whi, 1)
                    for h in range(2):
                        act.wait_ge(c_in, b * 32 + h * 16 + 16)
                        if h == 1:
                            act.wait_ge(c_mm, b * 4 + 2)
                        act.activation(ctx_hi[:, :, :], ctx_raw[:, :, :], ACT.Copy).then_inc(c_hi, 1)
                        for t in range(2):
                            act.wait_ge(c_mm, b * 4 + 2 * h + t + 1)
                            act.activation(qk_hi[:, t, h * HALF:(h + 1) * HALF], ps_t[t][:, :], ACT.Identity,
                                           bias=bias_c[:, t:t + 1], scale=1.0).then_inc(c_qhi, 1)

                    def turned(mb):
                        for h in range(2):
                            act.wait_ge(e_turn, b * (2 * TB) + 2 * mb + h + 1)
                            act.activation(at_hi[:, 4 * h:4 * h + 4, mb * P:(mb + 1) * P], turns4(ps_t[h], h),
                                           ACT.Copy).then_inc(e_hi, 1)

                    for mb in range(TB):
                        act.wait_ge(e_neg, b * TB + mb + 1)
                        if mb >= 2:
                            act.wait_ge(e_turn, b * (2 * TB) + 2 * mb - 2)
                        act.activation(c_probs[:, mb % 2, :], ps_s[mb % 2][:, :], ACT.Exp, bias=low[:, 8 + mb:9 + mb],
                                       scale=1.0, accum_out=den[:, mb:mb + 1]).then_inc(e_exp, 1)
                        if mb >= 1:
                            turned(mb - 1)
                    turned(TB - 1)
                    end_phase(act, b, 3)

                    def turned_block(i, k, dst, used):
                        used()
                        for h in range(2):
                            act.wait_ge(t_turn, turn_base(b, i, k) + h + 1)
                            act.activation(dst[:, 4 * h:4 * h + 4, :], turns4(ps_t[h], h), ACT.Copy).then_inc(t_hi, 1)

                    def second(i):
                        turned_block(i, 0, t2_hi, lambda: act.wait_ge(xm_ok, b * (2 * TB) + i * 2) if not isinstance(i, int) or i > 0 else None)

                    def third(i):
                        turned_block(i, 1, t3_hi, lambda: act.wait_ge(f_mm, b * TB + i) if not isinstance(i, int) or i > 0 else None)

                    def gate(i):
                        act.wait_ge(f_z, b * TB + i + 1)
                        act.activation(g8[:, 5, :], g8[:, 4, :], ACT.Exp, scale=-1.0).then_inc(f_e, 1)

                    def lowered(i):
                        act.wait_ge(l_turn, b * TB + i + 1)
                        act.wait_ge(u_mm, b * TB + i + 1)
                        act.activation(lt_hi[:, :], ps_o[0:GK, 0:P], ACT.Copy).then_inc(l_hi, 1)

                    def tail_block(i, first, second_, lastone):
                        if not first and not second_:
                            lowered(i - 2)
                        if not first:
                            third(i - 1)
                        if not lastone:
                            second(i + 1)
                        if not first:
                            gate(i - 1)

                    second(0)
                    tail_block(0, True, False, False)
                    tail_block(1, False, True, False)
                    with act.Fori(2, TB - 1) as i:
                        tail_block(i, False, False, False)
                    tail_block(TB - 1, False, False, True)
                    lowered(TB - 2)
                    third(TB - 1)
                    gate(TB - 1)
                    lowered(TB - 1)
                    end_phase(act, b, 4)

            @block.vector
            def _(dve):
                dve.wait_ge(setup_in, 96)
                for lo_c, hi_c, src in ((0, 64, 0), (64, 128, EXPERTS)):
                    dve.tensor_tensor(
                        ffn_prod[:, :, lo_c:hi_c].rearrange("p k (n s) -> p k n s", s=SEL),
                        ffn_raw[:, :, lo_c:hi_c].rearrange("p k (n s) -> p k n s", s=SEL),
                        vec_raw[:, :, src:src + EXPERTS].unsqueeze(3).broadcast_to([P, KC, EXPERTS, SEL]), ALU.mult)
                dve.tensor_tensor(ffn_prod[:, :, 128:FW], ffn_raw[:, :, 128:FW], vec_raw[:, :, 0:EXPERTS],
                                  ALU.mult).then_inc(setup_prod, 1)
                dve.tensor_copy(ffn_hi[:, :, :], ffn_raw[:, :, :]).then_inc(setup_split, 1)
                dve.tensor_copy(up_hi[:, :], up_raw[:, :]).then_inc(setup_split, 1)
                dve.wait_ge(setup_split, 2)
                dve.tensor_tensor(ffn_lo[:, :, :], ffn_raw[:, :, :], f(ffn_hi[:, :, :]), ALU.subtract)
                dve.tensor_tensor(up_lo[:, :], up_raw[:, :], f(up_hi[:, :]), ALU.subtract)
                dve.wait_ge(setup_mm, 1)
                dve.tensor_copy(ffn_c[:, :], ps_p[:, 0:FW])
                end_setup(dve)
                dve.sem_inc(lo_ok, C_LO)
                dve.sem_inc(o_ok, C_O)
                for s, c in ((ln_xn, 2), (ln_lo, 2), (wo_ok, 2), (x1_ok, 2), (c_split, 1), (t_lo, 2), (x2_ok, 1),
                             (f_g, 1), (l_ok, 1), (y_ok, 1)):
                    dve.sem_inc(s, c)

                def stack(b, pair, j):
                    n = b * PAIRS + pair
                    dve.wait_ge(q_hi_ok, n * 2 + j + 1)
                    dve.tensor_tensor(q_st[j][opposite(j), :], qkv[own(j), 0, :], f(q_st[j][own(j), :]), ALU.subtract)
                    dve.wait_ge(k_hi_ok, n * 2 + j + 1)
                    dve.tensor_tensor(k_lo[j][own(j), :], qkv[own(j), 1, :], f(k_hi[j][own(j), :]),
                                      ALU.subtract).then_inc(k_lo_ok, 1)
                    dve.wait_ge(k_lo_ok, n * 2 + j + 1)
                    dve.tensor_copy(k_lo[j][opposite(j), :], f(k_lo[j][own(j), :])).then_inc(stack_ok, 1)

                def split_values(j, turn, bank):
                    dve.wait_ge(hi_ok, turn + 1)
                    dve.tensor_tensor(v_st[j][:, :, HD:2 * HD], bank[:, :].rearrange("p (k d) -> p k d", d=HD),
                                      f(v_st[j][:, :, 0:HD]), ALU.subtract).then_inc(lo_ok, 1)

                def attend(b, hp, order, turns):
                    n = b * PAIRS + hp
                    t0 = b * TURNS_B + hp * TURNS + 1
                    pending = []

                    def invert():
                        while pending:
                            i = pending.pop(0)
                            dve.wait_ge(exp_ok, n * 16 + i + 1 + C_EXP)
                            dve.reciprocal(rden[:, i:i + 1], den[:, i:i + 1]).then_inc(rden_ok, 1)

                    for e in order:
                        if e[0] == "scores":
                            _, j, qb = e
                            i, w = 8 * j + qb, (qb + 1) * P
                            dve.wait_ge(scores_ok, n * 16 + i + 1 + C_SCORES)
                            dve.tensor_reduce(low[:, i:i + 1], ps_s[qb % 2][:, 0:w], AX_X, ALU.min).then_inc(low_ok, 1)
                            invert()
                            pending.append(i)
                        elif e[0] == "turn":
                            _, j, g, kb = e
                            c, m = cols(g, kb), body_mixes[("mix", j, g, kb)]
                            dve.wait_ge(hi_ok, t0 + turns[e] + 1)
                            dve.tensor_tensor(pt_lo[:, m % 2, c:HALF], ps_t[(1 + turns[e]) % 2][:, c:HALF],
                                              f(pt_hi[:, m % 2, c:HALF]), ALU.subtract).then_inc(lo_ok, 1)
                            invert()
                        elif e[0] == "mix":
                            _, j, g, kb = e
                            if kb == 4 * g + 3:
                                dve.wait_ge(o_lo_ok, n * 4 + 2 * j + g + 1)
                                dve.tensor_tensor(otx[own(j), 4 * g:4 * g + 4, hp, :],
                                                  ps_o[0:HD, :].rearrange("p (t q) -> p t q", q=P),
                                                  o_lo[:, :].rearrange("p (t q) -> p t q", q=P),
                                                  ALU.add).then_inc(o_ok, 1)
                        elif e[0] == "vturn":
                            split_values(B if e[1] == B else A, t0 + turns[e], ps_t[(1 + turns[e]) % 2])
                            invert()
                        elif e[0] == "stack":
                            if e[1] == B:
                                stack(b, hp, B)
                            else:
                                stack(b, hp + 1, A)
                    invert()

                def split_heads(b, v, s):
                    tb = v * 2 + s
                    dve.wait_ge(st_hi, b * TB + tb + 1)
                    dve.tensor_tensor(o_rest[:, s, :, :], otx[:, tb, :, :], f(o_hi[:, s, :, :]),
                                      ALU.subtract).then_inc(st_ok, 1)

                def add_out(b, v, s):
                    tb = v * 2 + s
                    dve.wait_ge(out_mm, b * TB + tb + 1 + C_OUT)
                    dve.wait_ge(xr_in[s], b * (16 * TB // 2) + v * 16 + 16)
                    dve.tensor_tensor(otx[:, tb, :, :].rearrange("p k t -> p (k t)"), ps_s[s][:, :], x_res[:, s, :],
                                      ALU.add).then_inc(x1_ok, 1)

                def stats(src, s, n_bn, ok_bn, ok_mv):
                    alone(dve)
                    for h in range(2):
                        ins = dve.bn_stats(bn[:, s, h, :], src[:, h * HALF:(h + 1) * HALF])
                    ins.then_inc(ok_bn, 1)
                    dve.wait_ge(ok_bn, n_bn)
                    alone(dve)
                    dve.bn_aggr(mv[:, s, :], bn[:, s, :, :].rearrange("p h c -> p (h c)")).then_inc(ok_mv, 1)

                with dve.Fori(0, BATCH) as b:
                    with dve.Fori(0, TB // 2) as v:
                        for s in range(2):
                            dve.wait_ge(ln_in[s], b * (16 * TB // 2) + v * 16 + 16)
                            stats(x_in[:, s, :], s, b * TB + v * 2 + s + 1, ln_bn, ln_mv)
                        for s in range(2):
                            dve.wait_ge(ln_rs, b * TB + v * 2 + s + 1)
                            dve.wait_ge(ln_turn, b * (2 * TB) + v * 4 + 2 * s - 2 + C_LN_TURN)
                            dve.tensor_scalar(xn[:, s, :], x_in[:, s, :], mv[:, s, 0:1], rstd[:, s:s + 1],
                                              ALU.subtract, ALU.mult).then_inc(ln_xn, 1)
                        for s in range(2):
                            for h in range(2):
                                dve.wait_ge(ln_hi, b * (2 * TB) + v * 4 + 2 * s + h + 1)
                                r = bass.ts(v * 2 + s, P)
                                dve.tensor_tensor(xt_lo[:, 4 * h:4 * h + 4, r], turns4(ps_t[h], h),
                                                  f(xt_hi[:, 4 * h:4 * h + 4, r]), ALU.subtract).then_inc(ln_lo, 1)
                    end_phase(dve, b, 0)

                    stack(b, 0, A)
                    split_values(A, b * TURNS_B, ps_t[0])
                    with dve.Fori(0, PAIRS - 1) as hp:
                        attend(b, hp, body, body_turns)
                    attend(b, PAIRS - 1, tail_body, tail_turns)
                    end_phase(dve, b, 1)

                    with dve.Fori(0, KC // 2) as v:
                        for s in range(2):
                            dve.wait_ge(wo_hi_ok, b * KC + v * 2 + s + 1)
                            dve.tensor_tensor(wo_lo[:, v * 2 + s, :], wo_raw[:, s, :], f(wo_hi[:, v * 2 + s, :]),
                                              ALU.subtract).then_inc(wo_ok, 1)
                    for s in range(2):
                        split_heads(b, 0, s)
                    with dve.Fori(0, TB // 2 - 1) as v:
                        for s in range(2):
                            add_out(b, v, s)
                            split_heads(b, v + 1, s)
                    for s in range(2):
                        add_out(b, TB // 2 - 1, s)
                    end_phase(dve, b, 2)

                    dve.wait_ge(c_whi, b + 1)
                    dve.tensor_tensor(wc_lo[:, :, :, :], wc_raw[:, :, :, :], f(wc_hi[:, :, :, :]),
                                      ALU.subtract).then_inc(c_wok, 1)
                    for h in range(2):
                        dve.wait_ge(c_hi, b * 2 + h + 1)
                        dve.tensor_tensor(ctx_lo[:, :, :], ctx_raw[:, :, :], f(ctx_hi[:, :, :]),
                                          ALU.subtract).then_inc(c_split, 1)
                        for t in range(2):
                            dve.wait_ge(c_qhi, b * 4 + 2 * h + t + 1)
                            dve.scalar_tensor_tensor(out=qk_lo[:, t, h * HALF:(h + 1) * HALF], in0=ps_t[t][:, :],
                                                     scalar=bias_c[:, t:t + 1],
                                                     in1=f(qk_hi[:, t, h * HALF:(h + 1) * HALF]),
                                                     op0=ALU.add, op1=ALU.subtract).then_inc(c_qk, 1)

                    def turned(mb):
                        for h in range(2):
                            dve.wait_ge(e_hi, b * (2 * TB) + 2 * mb + h + 1)
                            r = slice(mb * P, (mb + 1) * P)
                            dve.tensor_tensor(at_lo[:, 4 * h:4 * h + 4, r], turns4(ps_t[h], h),
                                              f(at_hi[:, 4 * h:4 * h + 4, r]), ALU.subtract).then_inc(e_lo, 1)

                    for mb in range(TB):
                        dve.wait_ge(e_mm, b * TB + mb + 1)
                        dve.tensor_reduce(low[:, mb:mb + 1], ps_s[mb % 2][:, :], AX_X, ALU.max).then_inc(e_mx, 1)
                        dve.wait_ge(e_mx, b * TB + mb + 1)
                        dve.tensor_scalar(low[:, 8 + mb:9 + mb], low[:, mb:mb + 1], -1.0, None, ALU.mult).then_inc(e_neg, 1)
                        if mb >= 1:
                            turned(mb - 1)
                        dve.wait_ge(e_exp, b * TB + mb + 1)
                        dve.reciprocal(rden[:, mb:mb + 1], den[:, mb:mb + 1]).then_inc(e_rd, 1)
                    turned(TB - 1)
                    end_phase(dve, b, 3)

                    def flat(i):
                        return otx[:, i, :, :].rearrange("p k t -> p (k t)")

                    def norm(i, k, dst, ok):
                        n = norm_base(b, i, k)
                        stats(flat(i), k, n + 1, t_bn, t_mv)
                        dve.wait_ge(t_rs, n + 1)
                        if k == 0:
                            if not isinstance(i, int) or i > 0:
                                dve.wait_ge(t_turn, turn_base(b, i - 1, 0) + 2)
                        elif not isinstance(i, int) or i > 0:
                            dve.wait_ge(t_turn, turn_base(b, i - 1, 1) + 2)
                        dve.tensor_scalar(dst[:, :], flat(i), mv[:, k, 0:1], rstd[:, k:k + 1], ALU.subtract,
                                          ALU.mult).then_inc(ok, 1)

                    def turned_block(i, k, lo_t, hi_t):
                        for h in range(2):
                            dve.wait_ge(t_hi, turn_base(b, i, k) + h + 1)
                            dve.tensor_tensor(lo_t[:, 4 * h:4 * h + 4, :], turns4(ps_t[h], h),
                                              f(hi_t[:, 4 * h:4 * h + 4, :]), ALU.subtract).then_inc(t_lo, 1)

                    def cross(i):
                        dve.wait_ge(xm_ok, b * (2 * TB) + i * 2 + 2)
                        dve.tensor_tensor(flat(i), ps_s[0][:, :], flat(i), ALU.add).then_inc(x2_ok, 1)

                    STEPS = 13

                    def gate(i):
                        base = (b * TB + i) * STEPS
                        count = [0]

                        def step(ins):
                            count[0] += 1
                            ins.then_inc(f_step, 1)
                            dve.wait_ge(f_step, base + count[0])

                        dve.wait_ge(f_mm, b * TB + i + 1)
                        step(dve.tensor_tensor(sel_u[:, :], ps_p[:, 0:64], ffn_c[:, 0:64], ALU.subtract))
                        dve.tensor_tensor(sel_sq[:, :], sel_u[:, :], sel_u[:, :], ALU.mult)
                        step(dve.tensor_scalar(g1[:, 0:1], mv[:, 1, 1:2], float(DM), rstd[:, 1:2], ALU.mult, ALU.mult))
                        step(dve.tensor_scalar(g1[:, 1:2], g1[:, 0:1], rstd[:, 1:2], None, ALU.mult))
                        dve.tensor_reduce(g8[:, 0, :], sel_sq[:, :].rearrange("p (n s) -> p n s", s=SEL), AX_X, ALU.add)
                        step(dve.scalar_tensor_tensor(out=g8[:, 1, :], in0=ps_p[:, 128:FW], scalar=-2.0,
                                                      in1=ffn_c[:, 128:FW], op0=ALU.mult, op1=ALU.add))
                        step(dve.tensor_scalar(g8[:, 2, :], g8[:, 1, :], g1[:, 1:2], None, ALU.add))
                        step(dve.reciprocal(g8[:, 1, :], g8[:, 2, :]))
                        step(dve.tensor_tensor(g8[:, 3, :], g8[:, 0, :], g8[:, 1, :], ALU.mult))
                        step(dve.tensor_tensor(g8[:, 2, :], g8[:, 3, :], center_b[:, :], ALU.subtract))
                        dve.tensor_tensor(g8[:, 4, :], g8[:, 2, :], slope_b[:, :], ALU.mult).then_inc(f_z, 1)
                        dve.tensor_tensor(low_h[:, 0:64], ps_p[:, 64:128], ffn_c[:, 64:128], ALU.subtract)
                        dve.wait_ge(f_e, b * TB + i + 1)
                        step(dve.tensor_scalar(g8[:, 6, :], g8[:, 5, :], 1.0, None, ALU.add))
                        step(dve.reciprocal(g8[:, 7, :], g8[:, 6, :]))
                        step(dve.tensor_reduce(g1[:, 2:3], g8[:, 7, :], AX_X, ALU.max))
                        dve.tensor_scalar(g1[:, 4:5], g1[:, 2:3], -1.0, 1.0, ALU.mult, ALU.add)
                        step(dve.scalar_tensor_tensor(out=g8[:, 8, :], in0=g8[:, 7, :], scalar=g1[:, 2:3],
                                                      in1=rank[:, :], op0=ALU.is_equal, op1=ALU.mult))
                        step(dve.tensor_reduce(g1[:, 3:4], g8[:, 8, :], AX_X, ALU.max))
                        assert count[0] == STEPS
                        dve.tensor_scalar(low_h[:, 64:GK], g8[:, 8, :], g1[:, 3:4], g1[:, 2:3], ALU.is_equal,
                                          ALU.mult).then_inc(f_w, 1)
                        dve.wait_ge(f_w, b * TB + i + 1)
                        lh = low_h[:, 0:64].rearrange("p (n h) -> p n h", h=LOW)
                        dve.tensor_tensor(lh, lh, low_h[:, 64:GK].unsqueeze(2).broadcast_to([P, EXPERTS, LOW]),
                                          ALU.mult).then_inc(f_g, 1)
                        dve.scalar_tensor_tensor(out=flat(i), in0=xn3[:, :], scalar=g1[:, 4:5], in1=flat(i),
                                                 op0=ALU.mult, op1=ALU.add).then_inc(f_x, 1)

                    def lowered(i):
                        dve.wait_ge(l_hi, b * TB + i + 1)
                        dve.tensor_tensor(lt_lo[:, :], ps_o[0:GK, 0:P], f(lt_hi[:, :]), ALU.subtract).then_inc(l_ok, 1)

                    def finish(i):
                        dve.wait_ge(u_mm, b * TB + i + 1 + 1)
                        dve.wait_ge(f_x, b * TB + i + 1)
                        dve.tensor_tensor(flat(i), ps_s[1][:, :], flat(i), ALU.add).then_inc(y_ok, 1)

                    def tail_block(i, first, second_, lastone):
                        if not lastone:
                            norm(i + 1, 0, xn2, t_xn2)
                        if not first and not second_:
                            lowered(i - 2)
                        if not first:
                            turned_block(i - 1, 1, t3_lo, t3_hi)
                        if not first and not second_:
                            finish(i - 2)
                        cross(i)
                        if not lastone:
                            turned_block(i + 1, 0, t2_lo, t2_hi)
                        if not first:
                            gate(i - 1)
                        dve.wait_ge(x2_ok, b * TB + i + 2)
                        norm(i, 1, xn3, t_xn3)

                    norm(0, 0, xn2, t_xn2)
                    turned_block(0, 0, t2_lo, t2_hi)
                    tail_block(0, True, False, False)
                    tail_block(1, False, True, False)
                    with dve.Fori(2, TB - 1) as i:
                        tail_block(i, False, False, False)
                    tail_block(TB - 1, False, False, True)
                    lowered(TB - 2)
                    turned_block(TB - 1, 1, t3_lo, t3_hi)
                    finish(TB - 2)
                    gate(TB - 1)
                    lowered(TB - 1)
                    finish(TB - 1)
                    end_phase(dve, b, 4)

            @block.gpsimd
            def _(pool):
                pool.memset(ones[:, :], 1.0).then_inc(setup_cst, 1)
                pool.memset(neg_half[:, :], -0.5)
                for n in range(EXPERTS):
                    pool.memset(rank[:, n:n + 1], float(EXPERTS - n))
                pool.memset(ident[:, :], 0.0)
                pool.memset(ident_bf[:, :], 0.0)
                pool.memset(mask_bf[:, :], 0.0).then_inc(setup_cst, 1)
                pool.wait_ge(setup_cst, 2)
                for m in (ident, ident_bf):
                    pool.affine_select(out=m[:, :], in_=m[:, :], compare_op=ALU.not_equal, fill=1.0,
                                       base=0, pattern=[[-1, P]], channel_multiplier=1)
                pool.affine_select(out=mask_bf[:, :], in_=mask_bf[:, :], compare_op=ALU.is_ge, fill=-NEG,
                                   base=0, pattern=[[-1, P]], channel_multiplier=1)

                def split_piece(n, k):
                    slot = k % 3
                    pool.wait_ge(w_in[k % 2], n * 48 + 16 * (k // 2 + 1))
                    if not (isinstance(n, int) and n == 0 and k < 2):
                        t, half = divmod(k - 3, 2)
                        pool.wait_ge(part_ok, n * 12 + 4 * t + 2 + half + 1 + C_PART)
                        alone(pool)
                    alone(pool)
                    pool.tensor_scalar(w_hi[:, slot, :, :], w_raw[:, k % 2, :, :], 1.0, 1.0, ALU.mult,
                                       ALU.mult).then_inc(w_hi_ok, 1)
                    pool.wait_ge(w_hi_ok, n * 6 + k + 1)
                    pool.tensor_tensor(w_lo[:, slot, :, :], w_raw[:, k % 2, :, :], f(w_hi[:, slot, :, :]),
                                       ALU.subtract).then_inc(w_split, 1)

                def project(b, pair, t, h, k):
                    if (h, k) == (0, 0):
                        split_piece(b * PAIRS + pair, 2 * t + 2)
                    if (h, k) == (1, 1):
                        split_piece(b * PAIRS + pair, 2 * t + 3)

                def attend(b, hp, order):
                    n = b * PAIRS + hp
                    for e in order:
                        if e[0] == "scores":
                            _, j, qb = e
                            i, r = 8 * j + qb, slice(off(qb), off(qb + 1))
                            pool.wait_ge(rden_ok, n * 16 + i + 1)
                            alone(pool)
                            pool.tensor_scalar(probs[:, r], probs[:, r], rden[:, i:i + 1], 1.0, ALU.mult,
                                               ALU.mult).then_inc(norm_ok, 1)
                        elif e[0] == "proj":
                            project(b, hp + 1, *e[1:])

                def inverse_sigma(s, n, mv_ok, ve_ok, rs_ok):
                    pool.wait_ge(mv_ok, n + 1)
                    alone(pool)
                    pool.tensor_scalar(veps[:, s:s + 1], mv[:, s, 1:2], EPS, 1.0, ALU.add, ALU.mult).then_inc(ve_ok, 1)
                    pool.wait_ge(ve_ok, n + 1)
                    pool.tensor_tensor(rstd[:, s:s + 1], veps[:, s:s + 1], neg_half[:, :], ALU.pow).then_inc(rs_ok, 1)

                end_setup(pool)
                pool.sem_inc(w_split, C_SPLIT)
                for k in range(2):
                    split_piece(0, k)
                with pool.Fori(0, BATCH) as b:
                    with pool.Fori(0, TB // 2) as v:
                        for s in range(2):
                            inverse_sigma(s, b * TB + v * 2 + s, ln_mv, ln_ve, ln_rs)
                    end_phase(pool, b, 0)

                    for t in range(3):
                        for h in range(2):
                            for k in range(2):
                                project(b, 0, t, h, k)
                    with pool.Fori(0, PAIRS - 1) as hp:
                        attend(b, hp, body)
                    attend(b, PAIRS - 1, tail_body)
                    end_phase(pool, b, 1)
                    end_phase(pool, b, 2)

                    for mb in range(TB):
                        pool.wait_ge(e_rd, b * TB + mb + 1)
                        alone(pool)
                        pool.tensor_scalar(c_probs[:, mb % 2, :], c_probs[:, mb % 2, :], rden[:, mb:mb + 1], 1.0,
                                           ALU.mult, ALU.mult).then_inc(e_norm, 1)
                    end_phase(pool, b, 3)

                    def tail_norm(i, k):
                        inverse_sigma(k, norm_base(b, i, k), t_mv, t_ve, t_rs)

                    tail_norm(0, 0)
                    tail_norm(1, 0)
                    with pool.Fori(0, TB - 2) as i:
                        tail_norm(i, 1)
                        tail_norm(i + 2, 0)
                    tail_norm(TB - 2, 1)
                    tail_norm(TB - 1, 1)
                    end_phase(pool, b, 4)


def kernel(x, ctx_1024, L0_attn_w_qkv, L0_attn_w_out, L0_xattn_Wq, L0_xattn_bq, L0_xattn_Wk, L0_xattn_bk,
           L0_ffn_select_weight, L0_ffn_select_mean_diff, L0_ffn_imp_center, L0_ffn_imp_slope,
           L0_ffn_lora_update, L0_ffn_lora_degen, L0_ffn_bias_w, L0_ffn_debias_w):
    import numpy as np
    import concourse.bacc as bacc
    from concourse.bass_utils import run_bass_kernel_spmd

    def by_columns(w, n):
        return np.asarray(w).transpose(1, 0, 2).reshape(DM, n)

    w = np.asarray(L0_attn_w_qkv).reshape(2, CC, P, 3, PAIRS, P).transpose(4, 3, 2, 0, 1, 5)
    arrays = {
        "x": np.asarray(x).reshape(BATCH, TB, P, DM),
        "w_qkv": w.reshape(3 * PAIRS, P, 2, CC, P),
        "w_out": np.asarray(L0_attn_w_out).reshape(KC, P, DM),
        "ctx_t": np.asarray(ctx_1024).transpose(0, 2, 1).reshape(BATCH, CC, P, SEQ).transpose(0, 2, 1, 3),
        "w_ctx": np.stack([np.asarray(m).T.reshape(CC, P, CD) for m in (L0_xattn_Wq, L0_xattn_Wk)]).transpose(2, 0, 1, 3),
        "b_ctx": np.stack([np.asarray(L0_xattn_bq), np.asarray(L0_xattn_bk)], axis=1),
        "w_ffn": np.concatenate([by_columns(L0_ffn_select_weight, 64), by_columns(L0_ffn_lora_update, 64),
                                 np.asarray(L0_ffn_select_mean_diff).T], axis=1),
        "v_ffn": np.concatenate([np.asarray(L0_ffn_select_mean_diff).T, np.asarray(L0_ffn_debias_w).T], axis=1),
        "w_up": np.concatenate([np.asarray(L0_ffn_lora_degen).transpose(0, 2, 1).reshape(EXPERTS * LOW, DM),
                                np.asarray(L0_ffn_bias_w)], axis=0),
        "center": np.asarray(L0_ffn_imp_center).reshape(1, EXPERTS),
        "slope": np.asarray(L0_ffn_imp_slope).reshape(1, EXPERTS),
    }
    arrays = {n: np.ascontiguousarray(a) for n, a in arrays.items()}
    nc = bacc.Bacc("TRN2", target_bir_lowering=False, num_devices=1)
    args = [nc.dram_tensor(f"in_{n}", a.shape, mybir.dt.from_np(a.dtype), kind="ExternalInput").ap()
            for n, a in arrays.items()]
    out = nc.dram_tensor("out", (BATCH, TB, P, DM), F32, kind="ExternalOutput").ap()
    decoder_layer(nc, *args, out)
    result = run_bass_kernel_spmd(nc, [{f"in_{n}": a for n, a in arrays.items()}], core_ids=[0])
    return result.results[0]["out"].reshape(BATCH, SEQ, DM)
```

```python
from contextlib import ExitStack

import concourse.bass as bass
from concourse import mybir

F32 = mybir.dt.float32
F32R = mybir.dt.float32r
BF16 = mybir.dt.bfloat16
ALU = mybir.AluOpType
ACT = mybir.ActivationFunctionType
AX_X = mybir.AxisListType.X

P = 128
BATCH, SEQ, DM = 4, 1024, 1024
HEADS, HD = 16, 64
PAIRS = HEADS // 2
TB = SEQ // P
KC = DM // P
CTX, CD = 512, 128
CC = CTX // P
EXPERTS, SEL, LOW = 8, 8, 8
FW = EXPERTS * SEL + EXPERTS * LOW + EXPERTS
GK = EXPERTS * LOW + EXPERTS
HALF = 512
EPS = 1e-5
NEG = -1e10
PARTS = 4
A, B = 0, 1



PAIR_STEPS = """
    SA0 SA1 KB0 EA0 NA0 P EA1 P SA2 SA3 KB1 KB2 P P NA1 SA4 EA2 NA2 EA3 NA3 C00 EA4 SA5 VA EA5 NA4 P
    P SA6 NA5 TA00 SA7 TA01 P EA6 TA02 EA7 NA6 MA00 NA7 SB0 P C01 MA01 SB1 MA02 EB0 TA03 P TA10 MA03
    OA0 SB2 EB1 NB0 P TA11 TA12 MA10 P TA13 MA11 SB3 EB2 TA14 NB1 MA12 P SB4 C10 MA13 TA15 VB NB2 P
    MA14 MA15 TA16 EB3 NB3 TA17 P EB4 SB5 NB4 MA16 TB00 MA17 OA1 P EB5 NB5 SB6 TB01 MB00 TB02 EB6 P
    C11 SB7 MB01 TB03 MB02 EB7 NB6 NB7 P MB03 KA0 P P OB0 TB10 TB11 P MB10 C20 TB12 KA1 TB13 MB11 P
    P MB12 KA2 TB14 MB13 TB15 P TB16 MB14 TB17 MB15 P MB16 C21 MB17 OB1
"""
LAST_STEPS = """
    SA0 SA1 KB0 EA0 NA0 EA1 SA2 SA3 KB1 KB2 NA1 SA4 EA2 NA2 EA3 NA3 EA4 SA5 VA EA5 NA4 SA6 NA5 TA00
    SA7 TA01 EA6 TA02 EA7 NA6 MA00 NA7 SB0 MA01 SB1 MA02 EB0 TA03 TA10 MA03 OA0 SB2 EB1 NB0 TA11
    TA12 MA10 TA13 MA11 SB3 EB2 TA14 NB1 MA12 SB4 MA13 TA15 VB NB2 MA14 MA15 TA16 EB3 NB3 TA17 EB4
    SB5 NB4 MA16 TB00 MA17 OA1 EB5 NB5 SB6 TB01 MB00 TB02 EB6 SB7 MB01 TB03 MB02 EB7 NB6 NB7 MB03
    OB0 TB10 TB11 MB10 TB12 TB13 MB11 MB12 TB14 MB13 TB15 TB16 MB14 TB17 MB15 MB16 MB17 OB1
"""
KINDS = {"S": "scores", "E": "exp", "N": "norm", "T": "turn", "M": "mix", "O": "take", "V": "vturn",
         "K": "stack", "P": "proj", "C": "copy"}


def attention_order(text):
    parts = [(t, h, k) for t in range(3) for h in range(2) for k in range(PARTS)]
    order = []
    for word in text.split():
        args = parts.pop(0) if word == "P" else [("AB".index(c) if c in "AB" else int(c)) for c in word[1:]]
        order.append((KINDS[word[0]], *args))
    return order


def decoder_layer(nc, x, w_qkv, w_out, ctx_t, w_ctx, b_ctx, w_ffn, v_ffn, w_up, center, slope, out):
    es = ExitStack()
    with es:
        def sem(name):
            return es.enter_context(nc.semaphore(name))

        def sb(stack, name, shape, dt=F32):
            return stack.enter_context(nc.sbuf_tensor(name, shape, dt))

        ident = sb(es, "ident", [P, P])
        ident_bf = sb(es, "ident_bf", [P, P], BF16)
        mask_bf = sb(es, "mask_bf", [P, P], BF16)
        ffn_hi = sb(es, "ffn_hi", [P, KC, FW], F32R)
        ffn_lo = sb(es, "ffn_lo", [P, KC, FW], F32R)
        up_hi = sb(es, "up_hi", [GK, DM], F32R)
        up_lo = sb(es, "up_lo", [GK, DM], F32R)
        ffn_c = sb(es, "ffn_c", [P, FW])
        center_b = sb(es, "center_b", [P, EXPERTS])
        slope_b = sb(es, "slope_b", [P, EXPERTS])
        rank = sb(es, "rank", [P, EXPERTS])
        neg_half = sb(es, "neg_half", [P, 1])
        bias_c = sb(es, "bias_c", [P, 2])
        otx = sb(es, "otx", [P, TB, KC, P])
        w_raw = sb(es, "w_raw", [P, 2, CC, P])
        w_hi = sb(es, "w_hi", [P, 3, CC, P], F32R)
        w_lo = sb(es, "w_lo", [P, 3, CC, P], F32R)
        bn = sb(es, "bn", [P, 3, 2, 6])
        mv = sb(es, "mv", [P, 3, 2])
        veps = sb(es, "veps", [P, 3])
        rstd = sb(es, "rstd", [P, 3])
        shift = sb(es, "shift", [P, 3])
        low = sb(es, "low", [P, 2 * HEADS])
        den = sb(es, "den", [P, 2 * HEADS])
        rden = sb(es, "rden", [P, 2 * HEADS])

        with ExitStack() as s0:
            ffn_raw = sb(s0, "ffn_raw", [P, KC, FW])
            vec_raw = sb(s0, "vec_raw", [P, KC, 2 * EXPERTS])
            ffn_prod = sb(s0, "ffn_prod", [P, KC, FW])
            up_raw = sb(s0, "up_raw", [GK, DM])
            ones = sb(s0, "ones", [P, P])
        with ExitStack() as s1:
            xt_hi = sb(s1, "xt_hi", [P, KC, SEQ], F32R)
            xt_lo = sb(s1, "xt_lo", [P, KC, SEQ], F32R)
            with ExitStack() as s2:
                x_in = sb(s2, "x_in", [P, 2, DM])
                xn = sb(s2, "xn", [P, 2, DM])
            qkv = sb(s1, "qkv", [P, 3, SEQ])
            q_st = [sb(s1, f"q_st{j}", [P, SEQ], F32R) for j in range(2)]
            k_hi = [sb(s1, f"k_hi{j}", [P, SEQ], F32R) for j in range(2)]
            k_lo = [sb(s1, f"k_lo{j}", [P, SEQ], F32R) for j in range(2)]
            v_st = [sb(s1, f"v_st{j}", [P, TB, 2 * HD], F32R) for j in range(2)]
            probs = sb(s1, "probs", [P, TB * (TB + 1) // 2 * P])
            pt_hi = sb(s1, "pt_hi", [P, 2, HALF], F32R)
            pt_lo = sb(s1, "pt_lo", [P, 2, HALF], F32R)
            o_lo = sb(s1, "o_lo", [HD, HALF])
        with ExitStack() as s3:
            wo_hi = sb(s3, "wo_hi", [P, KC, DM], F32R)
            wo_lo = sb(s3, "wo_lo", [P, KC, DM], F32R)
            wo_raw = sb(s3, "wo_raw", [P, 2, DM])
            o_hi = sb(s3, "o_hi", [P, 2, KC, P], F32R)
            o_rest = sb(s3, "o_rest", [P, 2, KC, P], F32R)
            x_res = sb(s3, "x_res", [P, 2, DM])
        with ExitStack() as s4:
            at_hi = sb(s4, "at_hi", [P, KC, DM], F32R)
            at_lo = sb(s4, "at_lo", [P, KC, DM], F32R)
            with ExitStack() as s5:
                wc_raw = sb(s5, "wc_raw", [P, 2, CC, CD])
                wc_hi = sb(s5, "wc_hi", [P, 2, CC, CD], F32R)
                wc_lo = sb(s5, "wc_lo", [P, 2, CC, CD], F32R)
                ctx_raw = sb(s5, "ctx_raw", [P, CC, HALF])
                ctx_hi = sb(s5, "ctx_hi", [P, CC, HALF], F32R)
                ctx_lo = sb(s5, "ctx_lo", [P, CC, HALF], F32R)
                qk_hi = sb(s5, "qk_hi", [P, 2, SEQ], F32R)
                qk_lo = sb(s5, "qk_lo", [P, 2, SEQ], F32R)
                c_probs = sb(s5, "c_probs", [P, 2, SEQ])
            with ExitStack() as s6:
                xn2 = sb(s6, "xn2", [P, DM])
                xn3 = sb(s6, "xn3", [P, 2, DM])
                t2_hi = sb(s6, "t2_hi", [P, KC, P], F32R)
                t2_lo = sb(s6, "t2_lo", [P, KC, P], F32R)
                t3_hi = sb(s6, "t3_hi", [P, KC, P], F32R)
                t3_lo = sb(s6, "t3_lo", [P, KC, P], F32R)
                sel_u = sb(s6, "sel_u", [P, EXPERTS * SEL])
                sel_sq = sb(s6, "sel_sq", [P, EXPERTS * SEL])
                g8 = sb(s6, "g8", [P, 12, EXPERTS])
                g1 = sb(s6, "g1", [P, 8])
                low_h = sb(s6, "low_h", [P, GK])
                lt_hi = sb(s6, "lt_hi", [GK, P], F32R)
                lt_lo = sb(s6, "lt_lo", [GK, P], F32R)

        ps_s = [es.enter_context(nc.psum_tensor(f"ps_s{i}", [P, DM], F32)) for i in range(2)]
        ps_t = [es.enter_context(nc.psum_tensor(f"ps_t{i}", [P, HALF], F32)) for i in range(2)]
        ps_o = es.enter_context(nc.psum_tensor("ps_o", [P, HALF], F32))
        ps_p = es.enter_context(nc.psum_tensor("ps_p", [P, HALF], F32))

        phase_done = sem("phase_done")
        passed = sem("passed")
        PHASES = 5
        setup_in, setup_cst, setup_prod, setup_mm, setup_split = (
            sem(n) for n in ("setup_in", "setup_cst", "setup_prod", "setup_mm", "setup_split"))
        ln_in = [sem(f"ln_in{s}") for s in range(2)]
        ln_bn, ln_mv, ln_ve, ln_rs, ln_xn, ln_turn, ln_hi, ln_lo = (
            sem(n) for n in ("ln_bn", "ln_mv", "ln_ve", "ln_rs", "ln_xn", "ln_turn", "ln_hi", "ln_lo"))
        w_in = [sem(f"w_in{s}") for s in range(2)]
        w_hi_ok, w_split, part_ok, proj_out = (sem(n) for n in ("w_hi_ok", "w_split", "part_ok", "proj_out"))
        q_hi_ok, k_hi_ok, k_lo_ok, stack_ok = (sem(n) for n in ("q_hi_ok", "k_hi_ok", "k_lo_ok", "stack_ok"))
        scores_ok, low_ok, exp_ok, rden_ok, norm_ok = (
            sem(n) for n in ("scores_ok", "low_ok", "exp_ok", "rden_ok", "norm_ok"))
        turn_ok, hi_ok, lo_ok, mix_ok, o_lo_ok, o_ok = (
            sem(n) for n in ("turn_ok", "hi_ok", "lo_ok", "mix_ok", "o_lo_ok", "o_ok"))
        wo_in = [sem(f"wo_in{s}") for s in range(2)]
        wo_hi_ok, wo_ok, st_hi, st_ok, out_mm, x1_ok = (
            sem(n) for n in ("wo_hi_ok", "wo_ok", "st_hi", "st_ok", "out_mm", "x1_ok"))
        xr_in = [sem(f"xr_in{s}") for s in range(2)]
        c_win, c_in, c_whi, c_wok, c_hi, c_split, c_mm, c_qhi, c_qk = (
            sem(n) for n in ("c_win", "c_in", "c_whi", "c_wok", "c_hi", "c_split", "c_mm", "c_qhi", "c_qk"))
        e_mm, e_mx, e_neg, e_exp, e_rd, e_norm, e_turn, e_hi, e_lo = (
            sem(n) for n in ("e_mm", "e_mx", "e_neg", "e_exp", "e_rd", "e_norm", "e_turn", "e_hi", "e_lo"))
        t_bn, t_mv, t_ve, t_rs, t_sh, t_xn2, t_xn3 = (
            sem(n) for n in ("t_bn", "t_mv", "t_ve", "t_rs", "t_sh", "t_xn2", "t_xn3"))
        t_turn, t_hi, t_lo, xm_ok, x2_ok = (sem(n) for n in ("t_turn", "t_hi", "t_lo", "xm_ok", "x2_ok"))
        f_mm, f_step, f_e, f_z, f_w, f_x, f_g, l_turn, l_hi, l_ok, u_mm, y_ok, y_out = (
            sem(n) for n in ("f_mm", "f_step", "f_e", "f_z", "f_w", "f_x", "f_g", "l_turn", "l_hi", "l_ok", "u_mm", "y_ok", "y_out"))

        C_EXP, C_LO, C_TURN, C_MIX, C_O, C_PROJ, C_SCORES, C_PART, C_SPLIT = 2, 2, 26, 24, 1, 1, 16, 8, 2
        C_LN_TURN, C_LN, C_OUT, C_ONE = 4, 2, 2, 1

        body, tail_body = attention_order(PAIR_STEPS), attention_order(LAST_STEPS)
        TURNS = sum(e[0] in ("turn", "vturn") for e in body)
        MIXES = sum(e[0] == "mix" for e in body)
        TURNS_B = PAIRS * TURNS
        PROJ = 6 * PARTS
        assert TURNS % 2 == 0 and C_TURN == TURNS and C_MIX == MIXES

        def numbered(order, kinds):
            n, at = 0, {}
            for e in order:
                if e[0] in kinds:
                    at[e] = n
                    n += 1
            return at

        body_turns, body_mixes = numbered(body, ("turn", "vturn")), numbered(body, ("mix",))
        assert numbered(tail_body, ("turn", "vturn")) == body_turns
        assert numbered(tail_body, ("mix",)) == body_mixes
        prev_last_turn = {g: body_turns[("turn", B, g, 4 * g + 3)] for g in range(2)}

        def off(qb):
            return qb * (qb + 1) // 2 * P

        def cols(g, kb):
            return max(kb - 4 * g, 0) * P

        def opposite(j):
            return slice(HD * (1 - j), HD * (1 - j) + HD)

        def own(j):
            return slice(HD * j, HD * j + HD)

        def f(ap):
            return ap.bitcast(F32)

        def alone(eng):
            eng.sem_inc(passed, 1)

        def end_phase(eng, b, k):
            alone(eng)
            eng.drain().then_inc(phase_done, 1)
            eng.wait_ge(phase_done, b * (5 * PHASES) + 5 * (k + 2))
            alone(eng)

        def end_setup(eng):
            eng.drain().then_inc(phase_done, 1)
            eng.wait_ge(phase_done, 5)

        def turns4(ps, half):
            return ps[:, :].rearrange("p (k t) -> p k t", k=4)

        def turn_base(b, i, k):
            base = b * (4 * TB)
            if isinstance(i, int):
                if k == 0:
                    return base + (0 if i == 0 else 2 if i == 1 else 4 * i - 2)
                return base + (4 * i + 4 if i < TB - 1 else 4 * TB - 2)
            return base + i * 4 - 2 if k == 0 else base + i * 4 + 4

        def norm_base(b, i, k):
            base = b * (2 * TB)
            if k == 0:
                return base + (0 if isinstance(i, int) and i == 0 else i * 2 - 1)
            return base + (2 * TB - 1 if isinstance(i, int) and i == TB - 1 else i * 2 + 2)

        def second(i):
            return not isinstance(i, int) or i >= 2

        def first(i):
            return isinstance(i, int) and i == 0

        def has(i):
            return not isinstance(i, int) or i < TB

        def tail_blocks(eng, tail_block):
            tail_block(0, 0)
            tail_block(1, 1)
            with eng.Fori(0, TB // 2 - 2) as v:
                tail_block(v * 2 + 2, 0)
                tail_block(v * 2 + 3, 1)
            tail_block(TB - 2, 0)
            tail_block(TB - 1, 1)

        with nc.Block() as block:

            @block.sync
            def _(sp):
                sp.dma_start(ffn_raw[:, :, :], w_ffn.rearrange("(k p) c -> p k c", p=P)).then_inc(setup_in, 16)
                sp.dma_start(vec_raw[:, :, :], v_ffn.rearrange("(k p) c -> p k c", p=P)).then_inc(setup_in, 16)
                sp.dma_start(up_raw[:, :], w_up).then_inc(setup_in, 16)
                sp.dma_start(center_b[:, :], center.broadcast_to([P, EXPERTS])).then_inc(setup_in, 16)
                sp.dma_start(slope_b[:, :], slope.broadcast_to([P, EXPERTS])).then_inc(setup_in, 16)
                sp.dma_start(bias_c[:, :], b_ctx).then_inc(setup_in, 16)
                for u in range(2):
                    sp.dma_start(w_raw[:, u, :, :], w_qkv[0, :, u]).then_inc(w_in[u], 16)
                sp.wait_ge(setup_in, 96)
                end_setup(sp)

                with sp.Fori(0, BATCH) as b:
                    with sp.Fori(0, TB // 2) as v:
                        for s in range(2):
                            sp.wait_ge(ln_xn, b * TB + v * 2 + s + 1)
                            alone(sp)
                            sp.dma_start(x_in[:, s, :], x[b, v * 2 + s]).then_inc(ln_in[s], 16)
                    end_phase(sp, b, 0)

                    with sp.Fori(0, 3 * PAIRS - 1) as t:
                        for u in range(2):
                            sp.wait_ge(w_split, b * (6 * PAIRS) + t * 2 + u + C_SPLIT + 1)
                            alone(sp)
                            sp.dma_start(w_raw[:, u, :, :], w_qkv[t + 1, :, u]).then_inc(w_in[u], 16)
                    for u in range(2):
                        sp.wait_ge(w_split, b * (6 * PAIRS) + 6 * PAIRS - 2 + u + C_SPLIT + 1)
                        alone(sp)
                        sp.dma_start(w_raw[:, u, :, :], w_qkv[0, :, u]).then_inc(w_in[u], 16)
                    end_phase(sp, b, 1)

                    with sp.Fori(0, KC // 2) as v:
                        for s in range(2):
                            sp.wait_ge(wo_ok, b * KC + v * 2 + s + 1)
                            alone(sp)
                            sp.dma_start(wo_raw[:, s, :], w_out[v * 2 + s]).then_inc(wo_in[s], 16)
                    with sp.Fori(0, TB // 2) as v:
                        for s in range(2):
                            sp.wait_ge(x1_ok, b * TB + v * 2 + s + 1)
                            alone(sp)
                            sp.dma_start(x_res[:, s, :], x[b, v * 2 + s]).then_inc(xr_in[s], 16)
                    end_phase(sp, b, 2)

                    sp.dma_start(wc_raw[:, :, :, :], w_ctx).then_inc(c_win, 16)
                    for h in range(2):
                        sp.wait_ge(c_split, b * 2 + h + 1)
                        alone(sp)
                        sp.dma_start(ctx_raw[:, :, :], ctx_t[b, :, :, h * HALF:(h + 1) * HALF]).then_inc(c_in, 16)
                    end_phase(sp, b, 3)

                    with sp.Fori(0, TB) as i:
                        sp.wait_ge(y_ok, b * TB + i + 1 + C_ONE)
                        alone(sp)
                        sp.dma_start(out[b, i], otx[:, i, :, :].rearrange("p k t -> p (k t)")).then_inc(y_out, 16)
                    sp.wait_ge(y_out, b * (16 * TB) + 16 * TB)
                    alone(sp)
                    end_phase(sp, b, 4)

            @block.tensor
            def _(pe):
                def split_mm(ps, lhs, rhs, n, steps, start, stop):
                    for k in steps:
                        (lh, ll), (rh, rl) = lhs(k), rhs(k)
                        pe.matmul(ps, lh, rh, start=start and k == steps[0], stop=False)
                        pe.matmul(ps, lh, rl, start=False, stop=False)
                        mm = pe.matmul(ps, ll, rh, start=False, stop=stop and k == steps[-1])
                    return mm

                pe.wait_ge(setup_prod, 1)
                pe.wait_ge(setup_cst, 1)
                for k in range(KC):
                    mm = pe.matmul(ps_p[:, 0:FW], ones[:, :], ffn_prod[:, k, :], start=k == 0, stop=k == KC - 1)
                mm.then_inc(setup_mm, 1)
                end_setup(pe)

                def project(b, pair, t, h, k):
                    n = b * PAIRS + pair
                    piece = k * 2 // PARTS
                    if k == 0:
                        pe.wait_ge(proj_out, n * 6 + 2 * t + h + C_PROJ)
                    if h == 0 and k * 2 % PARTS == 0:
                        pe.wait_ge(w_split, n * 6 + 2 * t + piece + 1 + C_SPLIT)
                    slot = (2 * t + piece) % 3
                    split_mm(ps_p[:, :],
                             lambda c: (w_hi[:, slot, c - CC * piece, :], w_lo[:, slot, c - CC * piece, :]),
                             lambda c: (xt_hi[:, c, h * HALF:(h + 1) * HALF], xt_lo[:, c, h * HALF:(h + 1) * HALF]),
                             HALF, list(range(KC // PARTS * k, KC // PARTS * (k + 1))), k == 0,
                             k == PARTS - 1).then_inc(part_ok, 1)

                def turn_values(b, pair, j, turn, bank):
                    pe.wait_ge(lo_ok, turn + C_LO - 1)
                    pe.wait_ge(proj_out, (b * PAIRS + pair) * 6 + 6 + C_PROJ)
                    alone(pe)
                    for kb in range(TB):
                        mm = pe.transpose(bank[:, kb * HD:(kb + 1) * HD],
                                          qkv[own(j), 2, kb * P:(kb + 1) * P], ident[own(j), own(j)])
                    mm.then_inc(turn_ok, 1)

                def attend(b, hp, order):
                    n = b * PAIRS + hp
                    t0 = b * TURNS_B + hp * TURNS
                    for e in order:
                        if e[0] == "scores":
                            _, j, qb = e
                            i, w = 8 * j + qb, (qb + 1) * P
                            pe.wait_ge(exp_ok, n * 16 + i + C_EXP - 1)
                            if qb == 0:
                                pe.wait_ge(stack_ok, n * 2 + j + 1)
                            q = q_st[j][:, qb * P:(qb + 1) * P]
                            for c in range(0, w, HALF):
                                d = min(c + HALF, w)
                                o = ps_s[qb % 2][:, c:d]
                                pe.matmul(o, q, k_hi[j][:, c:d], start=True, stop=False)
                                pe.matmul(o, q, k_lo[j][:, c:d], start=False, stop=True)
                            mm = pe.matmul(ps_s[qb % 2][:, w - P:w], ident_bf[:, :], mask_bf[:, :],
                                           start=False, stop=True, skip_group_check=True)
                            mm.then_inc(scores_ok, 1)
                        elif e[0] == "turn":
                            _, j, g, kb = e
                            pe.wait_ge(lo_ok, t0 + body_turns[e] + C_LO - 1)
                            if kb == 0:
                                pe.wait_ge(norm_ok, n * 16 + 8 * j + 4 * g + 4)
                            for qb in range(max(4 * g, kb), 4 * g + 4):
                                mm = pe.transpose(ps_t[body_turns[e] % 2][:, (qb - 4 * g) * P:(qb - 4 * g + 1) * P],
                                                  probs[:, off(qb) + kb * P:off(qb) + (kb + 1) * P], ident[:, :])
                            mm.then_inc(turn_ok, 1)
                        elif e[0] == "mix":
                            _, j, g, kb = e
                            pe.wait_ge(lo_ok, t0 + body_turns[("turn", j, g, kb)] + 1 + C_LO)
                            if kb == 0:
                                pe.wait_ge(o_ok, n * 4 + 2 * j + g + C_O)
                            s, c, end = body_mixes[e] % 2, cols(g, kb), kb == 4 * g + 3
                            pe.matmul(ps_o[:, c:HALF], v_st[j][:, kb, :], pt_hi[:, s, c:HALF],
                                      start=kb == 0, stop=False)
                            mm = pe.matmul(ps_o[:, c:HALF], v_st[j][:, kb, :], pt_lo[:, s, c:HALF],
                                           start=False, stop=end)
                            mm.then_inc(mix_ok, 1)
                        elif e[0] == "vturn":
                            bank = ps_t[body_turns[e] % 2]
                            turn_values(b, hp, e[1], t0 + body_turns[e], bank)
                        elif e[0] == "proj":
                            project(b, hp + 1, *e[1:])

                pe.sem_inc(turn_ok, C_TURN)
                pe.sem_inc(mix_ok, C_MIX)
                pe.sem_inc(scores_ok, C_SCORES)
                pe.sem_inc(part_ok, C_PART)
                pe.sem_inc(ln_turn, C_LN_TURN)
                pe.sem_inc(out_mm, C_OUT)
                pe.sem_inc(u_mm, C_ONE)

                with pe.Fori(0, BATCH) as b:
                    with pe.Fori(0, TB // 2) as v:
                        for s in range(2):
                            for h in range(2):
                                if h == 0:
                                    pe.wait_ge(ln_xn, b * TB + v * 2 + s + 1 + C_LN)
                                pe.wait_ge(ln_lo, b * (2 * TB) + v * 4 + 2 * s + h + 1)
                                for c in range(4):
                                    mm = pe.transpose(ps_t[h][:, c * P:(c + 1) * P],
                                                      xn[:, s, (4 * h + c) * P:(4 * h + c + 1) * P], ident[:, :])
                                mm.then_inc(ln_turn, 1)
                    end_phase(pe, b, 0)

                    for t in range(3):
                        for h in range(2):
                            for k in range(PARTS):
                                project(b, 0, t, h, k)
                    with pe.Fori(0, PAIRS - 1) as hp:
                        attend(b, hp, body)
                    attend(b, PAIRS - 1, tail_body)
                    end_phase(pe, b, 1)

                    with pe.Fori(0, TB // 2) as v:
                        for s in range(2):
                            pe.wait_ge(st_ok, b * TB + v * 2 + s + 1)
                            pe.wait_ge(wo_ok, b * KC + KC + 2)
                            pe.wait_ge(x1_ok, b * TB + v * 2 + s + 1)
                            for h in range(2):
                                r = slice(h * HALF, (h + 1) * HALF)
                                mm = split_mm(ps_s[s][:, r], lambda c: (o_hi[:, s, c, :], o_rest[:, s, c, :]),
                                              lambda c: (wo_hi[:, c, r], wo_lo[:, c, r]), HALF, list(range(KC)), True, True)
                            mm.then_inc(out_mm, 1)
                    end_phase(pe, b, 2)

                    pe.wait_ge(c_wok, b + 1)
                    for h in range(2):
                        pe.wait_ge(c_split, b * 2 + h + 1 + 1)
                        for t in range(2):
                            if h == 1:
                                pe.wait_ge(c_qk, b * 4 + t + 1)
                            split_mm(ps_t[t][:, :], lambda c: (wc_hi[:, t, c, :], wc_lo[:, t, c, :]),
                                     lambda c: (ctx_hi[:, c, :], ctx_lo[:, c, :]), HALF, list(range(CC)),
                                     True, True).then_inc(c_mm, 1)
                    pe.wait_ge(c_qk, b * 4 + 4)

                    def energy(mb):
                        if mb >= 2:
                            pe.wait_ge(e_exp, b * TB + mb - 1)
                        q = slice(mb * P, (mb + 1) * P)
                        for h in range(2):
                            r = slice(h * HALF, (h + 1) * HALF)
                            mm = split_mm(ps_s[mb % 2][:, r], lambda c: (qk_hi[:, 0, q], qk_lo[:, 0, q]),
                                          lambda c: (qk_hi[:, 1, r], qk_lo[:, 1, r]), HALF, [0], True, True)
                        mm.then_inc(e_mm, 1)

                    def turn_energy(mb):
                        pe.wait_ge(e_norm, b * TB + mb + 1)
                        for h in range(2):
                            if mb >= 1:
                                pe.wait_ge(e_lo, b * (2 * TB) + 2 * mb + h - 1)
                            for c in range(4):
                                mm = pe.transpose(ps_t[h][:, c * P:(c + 1) * P],
                                                  c_probs[:, mb % 2, (4 * h + c) * P:(4 * h + c + 1) * P], ident[:, :])
                            mm.then_inc(e_turn, 1)

                    for mb in range(TB):
                        energy(mb)
                        if mb >= 1:
                            turn_energy(mb - 1)
                    turn_energy(TB - 1)
                    end_phase(pe, b, 3)

                    def turn_block(i, k, src, ready):
                        pe.wait_ge(ready, b * TB + i + 1)
                        for h in range(2):
                            pe.wait_ge(t_lo, turn_base(b, i, k) + h + 1)
                            for c in range(4):
                                mm = pe.transpose(ps_t[h][:, c * P:(c + 1) * P],
                                                  src[:, (4 * h + c) * P:(4 * h + c + 1) * P], ident[:, :])
                            mm.then_inc(t_turn, 1)

                    def cross(i, h):
                        if h == 0:
                            pe.wait_ge(t_lo, turn_base(b, i, 0) + 2 + 2)
                            pe.wait_ge(x2_ok, b * TB + i + 1)
                        r = slice(h * HALF, (h + 1) * HALF)
                        mm = split_mm(ps_s[0][:, r], lambda c: (t2_hi[:, c, :], t2_lo[:, c, :]),
                                      lambda c: (at_hi[:, c, r], at_lo[:, c, r]), HALF, list(range(KC)), True, True)
                        mm.then_inc(xm_ok, 1)

                    def select(i):
                        pe.wait_ge(t_lo, turn_base(b, i, 1) + 2 + 2)
                        pe.wait_ge(f_g, b * TB + i + 1)
                        split_mm(ps_p[:, 0:FW], lambda c: (t3_hi[:, c, :], t3_lo[:, c, :]),
                                 lambda c: (ffn_hi[:, c, :], ffn_lo[:, c, :]), FW, list(range(KC)),
                                 True, True).then_inc(f_mm, 1)

                    def turn_low(i):
                        pe.wait_ge(f_g, b * TB + i + 1 + 1)
                        pe.wait_ge(l_ok, b * TB + i + 1)
                        pe.transpose(ps_o[0:GK, 0:P], low_h[:, :], ident[:, :]).then_inc(l_turn, 1)

                    def expand(i):
                        pe.wait_ge(l_ok, b * TB + i + 1 + 1)
                        pe.wait_ge(y_ok, b * TB + i + 1)
                        for h in range(2):
                            r = slice(h * HALF, (h + 1) * HALF)
                            mm = split_mm(ps_s[1][:, r], lambda c: (lt_hi[:, :], lt_lo[:, :]),
                                          lambda c: (up_hi[:, r], up_lo[:, r]), HALF, [0], True, True)
                        mm.then_inc(u_mm, 1)

                    def tail_block(i, par):
                        cross(i, 0)
                        if second(i):
                            turn_low(i - 2)
                        if not first(i):
                            turn_block(i - 1, 1, xn3[:, 1 - par, :], t_xn3)
                        cross(i, 1)
                        if has(i + 1):
                            turn_block(i + 1, 0, xn2, t_xn2)
                        if second(i):
                            expand(i - 2)
                        if not first(i):
                            select(i - 1)

                    turn_block(0, 0, xn2, t_xn2)
                    tail_blocks(pe, tail_block)
                    turn_low(TB - 2)
                    turn_block(TB - 1, 1, xn3[:, 1, :], t_xn3)
                    expand(TB - 2)
                    select(TB - 1)
                    turn_low(TB - 1)
                    expand(TB - 1)
                    end_phase(pe, b, 4)

            @block.scalar
            def _(act):
                end_setup(act)
                act.sem_inc(exp_ok, C_EXP)
                act.sem_inc(proj_out, C_PROJ)

                def copy_out(b, pair, t, h, reuse):
                    n = b * PAIRS + pair
                    act.wait_ge(part_ok, n * PROJ + (2 * t + h + 1) * PARTS + C_PART)
                    if reuse is not None:
                        if t < 2:
                            act.wait_ge(stack_ok, n * 2)
                        else:
                            act.wait_ge(turn_ok, reuse + 1 + C_TURN)
                    act.activation(qkv[:, t, h * HALF:(h + 1) * HALF], ps_p[:, :], ACT.Copy,
                                   scale=-(HD ** -0.5) if t == 0 else 1.0).then_inc(proj_out, 1)

                def stack(b, pair, j, part):
                    n = b * PAIRS + pair
                    if part == 0:
                        act.wait_ge(proj_out, n * 6 + 4 + C_PROJ)
                        act.wait_ge(scores_ok, n * 16 + 8 * j + 8 - 16 + C_SCORES)
                        act.activation(q_st[j][own(j), :], qkv[own(j), 0, :], ACT.Copy).then_inc(q_hi_ok, 1)
                    else:
                        rows = own(j) if part == 1 else opposite(j)
                        act.activation(k_hi[j][rows, :], qkv[own(j), 1, :], ACT.Copy).then_inc(k_hi_ok, 1)

                def split_values(j, turn, bank, mixes):
                    act.wait_ge(turn_ok, turn + 1 + C_TURN)
                    act.wait_ge(mix_ok, mixes + C_MIX)
                    act.activation(v_st[j][:, :, 0:HD], bank[:, :].rearrange("p (k d) -> p k d", d=HD),
                                   ACT.Copy).then_inc(hi_ok, 1)

                def attend(b, hp, order):
                    n = b * PAIRS + hp
                    t0 = b * TURNS_B + hp * TURNS
                    for e in order:
                        if e[0] == "exp":
                            _, j, qb = e
                            i, w = 8 * j + qb, (qb + 1) * P
                            act.wait_ge(low_ok, n * 16 + i + 1)
                            if qb % 4 == 0:
                                if j == B:
                                    act.wait_ge(turn_ok, t0 + body_turns[("turn", A, qb // 4, 4 * (qb // 4) + 3)] + 1 + C_TURN)
                                else:
                                    act.wait_ge(turn_ok, t0 - TURNS + prev_last_turn[qb // 4] + 1 + C_TURN)
                            act.activation(probs[:, off(qb):off(qb) + w], ps_s[qb % 2][:, 0:w], ACT.Exp,
                                           bias=low[:, i:i + 1], scale=-1.0,
                                           accum_out=den[:, i:i + 1]).then_inc(exp_ok, 1)
                        elif e[0] == "turn":
                            _, j, g, kb = e
                            c, m = cols(g, kb), body_mixes[("mix", j, g, kb)]
                            act.wait_ge(turn_ok, t0 + body_turns[e] + 1 + C_TURN)
                            act.wait_ge(mix_ok, n * MIXES + m - 1 + C_MIX)
                            act.activation(pt_hi[:, m % 2, c:HALF], ps_t[body_turns[e] % 2][:, c:HALF],
                                           ACT.Copy).then_inc(hi_ok, 1)
                        elif e[0] == "take":
                            _, j, g = e
                            act.wait_ge(mix_ok, n * MIXES + body_mixes[("mix", j, g, 4 * g + 3)] + 1 + C_MIX)
                            act.wait_ge(o_ok, n * 4 + 2 * j + g + C_O)
                            act.activation(o_lo[:, :], ps_o[HD:P, :], ACT.Copy).then_inc(o_lo_ok, 1)
                        elif e[0] == "vturn":
                            bank = ps_t[body_turns[e] % 2]
                            split_values(e[1], t0 + body_turns[e], bank, n * MIXES - (MIXES // 2 if e[1] == A else 0))
                        elif e[0] == "stack":
                            stack(b, hp + 1 if e[1] == A else hp, *e[1:])
                        elif e[0] == "copy":
                            copy_out(b, hp + 1, *e[1:], reuse=t0 + body_turns[("vturn", B)])

                with act.Fori(0, BATCH) as b:
                    with act.Fori(0, TB // 2) as v:
                        for s in range(2):
                            for h in range(2):
                                act.wait_ge(ln_turn, b * (2 * TB) + v * 4 + 2 * s + h + 1 + C_LN_TURN)
                                act.activation(xt_hi[:, 4 * h:4 * h + 4, bass.ts(v * 2 + s, P)], turns4(ps_t[h], h),
                                               ACT.Copy).then_inc(ln_hi, 1)
                    end_phase(act, b, 0)

                    for t in range(3):
                        for h in range(2):
                            copy_out(b, 0, t, h, None)
                    for part in range(3):
                        stack(b, 0, A, part)
                    with act.Fori(0, PAIRS - 1) as hp:
                        attend(b, hp, body)
                    attend(b, PAIRS - 1, tail_body)
                    end_phase(act, b, 1)

                    with act.Fori(0, KC // 2) as v:
                        for s in range(2):
                            act.wait_ge(wo_in[s], b * (16 * KC // 2) + v * 16 + 16)
                            act.activation(wo_hi[:, v * 2 + s, :], wo_raw[:, s, :], ACT.Copy).then_inc(wo_hi_ok, 1)
                    with act.Fori(0, TB // 2) as v:
                        for s in range(2):
                            act.wait_ge(out_mm, b * TB + v * 2 + s + 1)
                            act.activation(o_hi[:, s, :, :], otx[:, v * 2 + s, :, :], ACT.Copy).then_inc(st_hi, 1)
                    end_phase(act, b, 2)

                    act.wait_ge(c_win, b * 16 + 16)
                    act.activation(wc_hi[:, :, :, :], wc_raw[:, :, :, :], ACT.Copy).then_inc(c_whi, 1)
                    for h in range(2):
                        act.wait_ge(c_in, b * 32 + h * 16 + 16)
                        if h == 1:
                            act.wait_ge(c_mm, b * 4 + 2)
                        act.activation(ctx_hi[:, :, :], ctx_raw[:, :, :], ACT.Copy).then_inc(c_hi, 1)
                        for t in range(2):
                            act.wait_ge(c_mm, b * 4 + 2 * h + t + 1)
                            act.activation(qk_hi[:, t, h * HALF:(h + 1) * HALF], ps_t[t][:, :], ACT.Identity,
                                           bias=bias_c[:, t:t + 1], scale=1.0).then_inc(c_qhi, 1)

                    def turned(mb):
                        for h in range(2):
                            act.wait_ge(e_turn, b * (2 * TB) + 2 * mb + h + 1)
                            act.activation(at_hi[:, 4 * h:4 * h + 4, mb * P:(mb + 1) * P], turns4(ps_t[h], h),
                                           ACT.Copy).then_inc(e_hi, 1)

                    for mb in range(TB):
                        act.wait_ge(e_neg, b * TB + mb + 1)
                        if mb >= 2:
                            act.wait_ge(e_turn, b * (2 * TB) + 2 * mb - 2)
                        act.activation(c_probs[:, mb % 2, :], ps_s[mb % 2][:, :], ACT.Exp, bias=low[:, 8 + mb:9 + mb],
                                       scale=1.0, accum_out=den[:, mb:mb + 1]).then_inc(e_exp, 1)
                        if mb >= 1:
                            turned(mb - 1)
                    turned(TB - 1)
                    end_phase(act, b, 3)

                    def turned_block(i, k, dst, used):
                        used()
                        for h in range(2):
                            act.wait_ge(t_turn, turn_base(b, i, k) + h + 1)
                            act.activation(dst[:, 4 * h:4 * h + 4, :], turns4(ps_t[h], h), ACT.Copy).then_inc(t_hi, 1)

                    def normalise(i, k, slot, dst, ok):
                        act.wait_ge(t_sh, norm_base(b, i, k) + 1)
                        if k == 1 and second(i):
                            act.wait_ge(f_x, b * TB + i - 1)
                        act.activation(dst, otx[:, i, :, :].rearrange("p k t -> p (k t)"), ACT.Identity,
                                       bias=shift[:, slot:slot + 1], scale=rstd[:, slot:slot + 1]).then_inc(ok, 1)

                    def turned2(i):
                        turned_block(i, 0, t2_hi, lambda: None if first(i) else act.wait_ge(xm_ok, b * (2 * TB) + i * 2))

                    def turned3(i):
                        turned_block(i, 1, t3_hi, lambda: None if first(i) else act.wait_ge(f_mm, b * TB + i))

                    def gate(i):
                        act.wait_ge(f_z, b * TB + i + 1)
                        act.activation(g8[:, 5, :], g8[:, 4, :], ACT.Exp, scale=-1.0).then_inc(f_e, 1)

                    def lowered(i):
                        act.wait_ge(l_turn, b * TB + i + 1)
                        act.wait_ge(u_mm, b * TB + i + 1)
                        act.activation(lt_hi[:, :], ps_o[0:GK, 0:P], ACT.Copy).then_inc(l_hi, 1)

                    def tail_block(i, par):
                        if has(i + 1):
                            turned2(i + 1)
                        normalise(i, 1, 1 + par, xn3[:, par, :], t_xn3)
                        if not first(i):
                            gate(i - 1)
                        if not first(i):
                            lowered(i - 1)
                        turned3(i)
                        if has(i + 2):
                            normalise(i + 2, 0, 0, xn2[:, :], t_xn2)

                    normalise(0, 0, 0, xn2[:, :], t_xn2)
                    turned2(0)
                    normalise(1, 0, 0, xn2[:, :], t_xn2)
                    tail_blocks(act, tail_block)
                    gate(TB - 1)
                    lowered(TB - 1)
                    end_phase(act, b, 4)

            @block.vector
            def _(dve):
                dve.wait_ge(setup_in, 96)
                for lo_c, hi_c, src in ((0, 64, 0), (64, 128, EXPERTS)):
                    dve.tensor_tensor(
                        ffn_prod[:, :, lo_c:hi_c].rearrange("p k (n s) -> p k n s", s=SEL),
                        ffn_raw[:, :, lo_c:hi_c].rearrange("p k (n s) -> p k n s", s=SEL),
                        vec_raw[:, :, src:src + EXPERTS].unsqueeze(3).broadcast_to([P, KC, EXPERTS, SEL]), ALU.mult)
                dve.tensor_tensor(ffn_prod[:, :, 128:FW], ffn_raw[:, :, 128:FW], vec_raw[:, :, 0:EXPERTS],
                                  ALU.mult).then_inc(setup_prod, 1)
                dve.tensor_copy(ffn_hi[:, :, :], ffn_raw[:, :, :]).then_inc(setup_split, 1)
                dve.tensor_copy(up_hi[:, :], up_raw[:, :]).then_inc(setup_split, 1)
                dve.wait_ge(setup_split, 2)
                dve.tensor_tensor(ffn_lo[:, :, :], ffn_raw[:, :, :], f(ffn_hi[:, :, :]), ALU.subtract)
                dve.tensor_tensor(up_lo[:, :], up_raw[:, :], f(up_hi[:, :]), ALU.subtract)
                dve.wait_ge(setup_mm, 1)
                dve.tensor_copy(ffn_c[:, :], ps_p[:, 0:FW])
                end_setup(dve)
                dve.sem_inc(lo_ok, C_LO)
                dve.sem_inc(o_ok, C_O)
                for s, c in ((ln_xn, 2), (ln_lo, 2), (wo_ok, 2), (x1_ok, 2), (c_split, 1), (t_lo, 2), (x2_ok, 1),
                             (f_g, 1), (l_ok, 1), (y_ok, 1)):
                    dve.sem_inc(s, c)

                def stack(b, pair, j, part):
                    n = b * PAIRS + pair
                    if part == 0:
                        dve.wait_ge(q_hi_ok, n * 2 + j + 1)
                        dve.tensor_tensor(q_st[j][opposite(j), :], qkv[own(j), 0, :], f(q_st[j][own(j), :]), ALU.subtract)
                    elif part == 1:
                        dve.wait_ge(k_hi_ok, n * 4 + 2 * j + 1)
                        dve.tensor_tensor(k_lo[j][own(j), :], qkv[own(j), 1, :], f(k_hi[j][own(j), :]),
                                          ALU.subtract).then_inc(k_lo_ok, 1)
                    else:
                        dve.wait_ge(k_hi_ok, n * 4 + 2 * j + 2)
                        dve.wait_ge(k_lo_ok, n * 2 + j + 1)
                        dve.tensor_copy(k_lo[j][opposite(j), :], f(k_lo[j][own(j), :])).then_inc(stack_ok, 1)

                def split_values(j, turn, bank):
                    dve.wait_ge(hi_ok, turn + 1)
                    dve.tensor_tensor(v_st[j][:, :, HD:2 * HD], bank[:, :].rearrange("p (k d) -> p k d", d=HD),
                                      f(v_st[j][:, :, 0:HD]), ALU.subtract).then_inc(lo_ok, 1)

                def attend(b, hp, order):
                    n = b * PAIRS + hp
                    t0 = b * TURNS_B + hp * TURNS
                    for e in order:
                        if e[0] == "scores":
                            _, j, qb = e
                            i, w = 8 * j + qb, (qb + 1) * P
                            dve.wait_ge(scores_ok, n * 16 + i + 1 + C_SCORES)
                            dve.tensor_reduce(low[:, i:i + 1], ps_s[qb % 2][:, 0:w], AX_X, ALU.min).then_inc(low_ok, 1)
                        elif e[0] == "norm":
                            _, j, qb = e
                            i = 8 * j + qb
                            dve.wait_ge(exp_ok, n * 16 + i + 1 + C_EXP)
                            dve.reciprocal(rden[:, i:i + 1], den[:, i:i + 1]).then_inc(rden_ok, 1)
                        elif e[0] == "turn":
                            _, j, g, kb = e
                            c, m = cols(g, kb), body_mixes[("mix", j, g, kb)]
                            dve.wait_ge(hi_ok, t0 + body_turns[e] + 1)
                            dve.tensor_tensor(pt_lo[:, m % 2, c:HALF], ps_t[body_turns[e] % 2][:, c:HALF],
                                              f(pt_hi[:, m % 2, c:HALF]), ALU.subtract).then_inc(lo_ok, 1)
                        elif e[0] == "take":
                            _, j, g = e
                            dve.wait_ge(o_lo_ok, n * 4 + 2 * j + g + 1)
                            dve.tensor_tensor(otx[own(j), 4 * g:4 * g + 4, hp, :],
                                              ps_o[0:HD, :].rearrange("p (t q) -> p t q", q=P),
                                              o_lo[:, :].rearrange("p (t q) -> p t q", q=P),
                                              ALU.add).then_inc(o_ok, 1)
                        elif e[0] == "vturn":
                            split_values(e[1], t0 + body_turns[e], ps_t[body_turns[e] % 2])
                        elif e[0] == "stack":
                            stack(b, hp + 1 if e[1] == A else hp, *e[1:])

                def split_heads(b, v, s):
                    tb = v * 2 + s
                    dve.wait_ge(st_hi, b * TB + tb + 1)
                    dve.tensor_tensor(o_rest[:, s, :, :], otx[:, tb, :, :], f(o_hi[:, s, :, :]),
                                      ALU.subtract).then_inc(st_ok, 1)

                def add_out(b, v, s):
                    tb = v * 2 + s
                    dve.wait_ge(out_mm, b * TB + tb + 1 + C_OUT)
                    dve.wait_ge(xr_in[s], b * (16 * TB // 2) + v * 16 + 16)
                    dve.tensor_tensor(otx[:, tb, :, :].rearrange("p k t -> p (k t)"), ps_s[s][:, :], x_res[:, s, :],
                                      ALU.add).then_inc(x1_ok, 1)

                def stats(src, s, n_bn, ok_bn, ok_mv):
                    alone(dve)
                    for h in range(2):
                        ins = dve.bn_stats(bn[:, s, h, :], src[:, h * HALF:(h + 1) * HALF])
                    ins.then_inc(ok_bn, 1)
                    dve.wait_ge(ok_bn, n_bn)
                    alone(dve)
                    dve.bn_aggr(mv[:, s, :], bn[:, s, :, :].rearrange("p h c -> p (h c)")).then_inc(ok_mv, 1)

                with dve.Fori(0, BATCH) as b:
                    with dve.Fori(0, TB // 2) as v:
                        for s in range(2):
                            dve.wait_ge(ln_in[s], b * (16 * TB // 2) + v * 16 + 16)
                            stats(x_in[:, s, :], s, b * TB + v * 2 + s + 1, ln_bn, ln_mv)
                        for s in range(2):
                            dve.wait_ge(ln_rs, b * TB + v * 2 + s + 1)
                            dve.wait_ge(ln_turn, b * (2 * TB) + v * 4 + 2 * s - 2 + C_LN_TURN)
                            dve.tensor_scalar(xn[:, s, :], x_in[:, s, :], mv[:, s, 0:1], rstd[:, s:s + 1],
                                              ALU.subtract, ALU.mult).then_inc(ln_xn, 1)
                        for s in range(2):
                            for h in range(2):
                                dve.wait_ge(ln_hi, b * (2 * TB) + v * 4 + 2 * s + h + 1)
                                r = bass.ts(v * 2 + s, P)
                                dve.tensor_tensor(xt_lo[:, 4 * h:4 * h + 4, r], turns4(ps_t[h], h),
                                                  f(xt_hi[:, 4 * h:4 * h + 4, r]), ALU.subtract).then_inc(ln_lo, 1)
                    end_phase(dve, b, 0)

                    for part in range(3):
                        stack(b, 0, A, part)
                    with dve.Fori(0, PAIRS - 1) as hp:
                        attend(b, hp, body)
                    attend(b, PAIRS - 1, tail_body)
                    end_phase(dve, b, 1)

                    with dve.Fori(0, KC // 2) as v:
                        for s in range(2):
                            dve.wait_ge(wo_hi_ok, b * KC + v * 2 + s + 1)
                            dve.tensor_tensor(wo_lo[:, v * 2 + s, :], wo_raw[:, s, :], f(wo_hi[:, v * 2 + s, :]),
                                              ALU.subtract).then_inc(wo_ok, 1)
                    for s in range(2):
                        split_heads(b, 0, s)
                    with dve.Fori(0, TB // 2 - 1) as v:
                        for s in range(2):
                            add_out(b, v, s)
                            split_heads(b, v + 1, s)
                    for s in range(2):
                        add_out(b, TB // 2 - 1, s)
                    end_phase(dve, b, 2)

                    dve.wait_ge(c_whi, b + 1)
                    dve.tensor_tensor(wc_lo[:, :, :, :], wc_raw[:, :, :, :], f(wc_hi[:, :, :, :]),
                                      ALU.subtract).then_inc(c_wok, 1)
                    for h in range(2):
                        dve.wait_ge(c_hi, b * 2 + h + 1)
                        dve.tensor_tensor(ctx_lo[:, :, :], ctx_raw[:, :, :], f(ctx_hi[:, :, :]),
                                          ALU.subtract).then_inc(c_split, 1)
                        for t in range(2):
                            dve.wait_ge(c_qhi, b * 4 + 2 * h + t + 1)
                            dve.scalar_tensor_tensor(out=qk_lo[:, t, h * HALF:(h + 1) * HALF], in0=ps_t[t][:, :],
                                                     scalar=bias_c[:, t:t + 1],
                                                     in1=f(qk_hi[:, t, h * HALF:(h + 1) * HALF]),
                                                     op0=ALU.add, op1=ALU.subtract).then_inc(c_qk, 1)

                    def turned(mb):
                        for h in range(2):
                            dve.wait_ge(e_hi, b * (2 * TB) + 2 * mb + h + 1)
                            r = slice(mb * P, (mb + 1) * P)
                            dve.tensor_tensor(at_lo[:, 4 * h:4 * h + 4, r], turns4(ps_t[h], h),
                                              f(at_hi[:, 4 * h:4 * h + 4, r]), ALU.subtract).then_inc(e_lo, 1)

                    for mb in range(TB):
                        dve.wait_ge(e_mm, b * TB + mb + 1)
                        dve.tensor_reduce(low[:, mb:mb + 1], ps_s[mb % 2][:, :], AX_X, ALU.max).then_inc(e_mx, 1)
                        dve.wait_ge(e_mx, b * TB + mb + 1)
                        dve.tensor_scalar(low[:, 8 + mb:9 + mb], low[:, mb:mb + 1], -1.0, None, ALU.mult).then_inc(e_neg, 1)
                        if mb >= 1:
                            turned(mb - 1)
                        dve.wait_ge(e_exp, b * TB + mb + 1)
                        dve.reciprocal(rden[:, mb:mb + 1], den[:, mb:mb + 1]).then_inc(e_rd, 1)
                    turned(TB - 1)
                    end_phase(dve, b, 3)

                    def flat(i):
                        return otx[:, i, :, :].rearrange("p k t -> p (k t)")

                    def norm(i, k, slot):
                        if k == 1:
                            dve.wait_ge(x2_ok, b * TB + i + 2)
                        stats(flat(i), slot, norm_base(b, i, k) + 1, t_bn, t_mv)

                    def turned_block(i, k, lo_t, hi_t):
                        for h in range(2):
                            dve.wait_ge(t_hi, turn_base(b, i, k) + h + 1)
                            dve.tensor_tensor(lo_t[:, 4 * h:4 * h + 4, :], turns4(ps_t[h], h),
                                              f(hi_t[:, 4 * h:4 * h + 4, :]), ALU.subtract).then_inc(t_lo, 1)

                    def cross(i):
                        dve.wait_ge(xm_ok, b * (2 * TB) + i * 2 + 2)
                        dve.tensor_tensor(flat(i), ps_s[0][:, :], flat(i), ALU.add).then_inc(x2_ok, 1)

                    STEPS = 13

                    def gate(i, par):
                        base = (b * TB + i) * STEPS
                        count = [0]

                        def step(ins):
                            count[0] += 1
                            ins.then_inc(f_step, 1)
                            dve.wait_ge(f_step, base + count[0])

                        dve.wait_ge(f_mm, b * TB + i + 1)
                        step(dve.tensor_tensor(sel_u[:, :], ps_p[:, 0:64], ffn_c[:, 0:64], ALU.subtract))
                        dve.tensor_tensor(sel_sq[:, :], sel_u[:, :], sel_u[:, :], ALU.mult)
                        step(dve.tensor_scalar(g1[:, 0:1], mv[:, 1 + par, 1:2], float(DM), rstd[:, 1 + par:2 + par], ALU.mult, ALU.mult))
                        step(dve.tensor_scalar(g1[:, 1:2], g1[:, 0:1], rstd[:, 1 + par:2 + par], None, ALU.mult))
                        dve.tensor_reduce(g8[:, 0, :], sel_sq[:, :].rearrange("p (n s) -> p n s", s=SEL), AX_X, ALU.add)
                        step(dve.scalar_tensor_tensor(out=g8[:, 1, :], in0=ps_p[:, 128:FW], scalar=-2.0,
                                                      in1=ffn_c[:, 128:FW], op0=ALU.mult, op1=ALU.add))
                        step(dve.tensor_scalar(g8[:, 2, :], g8[:, 1, :], g1[:, 1:2], None, ALU.add))
                        step(dve.reciprocal(g8[:, 1, :], g8[:, 2, :]))
                        step(dve.tensor_tensor(g8[:, 3, :], g8[:, 0, :], g8[:, 1, :], ALU.mult))
                        step(dve.tensor_tensor(g8[:, 2, :], g8[:, 3, :], center_b[:, :], ALU.subtract))
                        dve.tensor_tensor(g8[:, 4, :], g8[:, 2, :], slope_b[:, :], ALU.mult).then_inc(f_z, 1)
                        dve.tensor_tensor(low_h[:, 0:64], ps_p[:, 64:128], ffn_c[:, 64:128], ALU.subtract)
                        dve.wait_ge(f_e, b * TB + i + 1)
                        step(dve.tensor_scalar(g8[:, 6, :], g8[:, 5, :], 1.0, None, ALU.add))
                        step(dve.reciprocal(g8[:, 7, :], g8[:, 6, :]))
                        step(dve.tensor_reduce(g1[:, 2:3], g8[:, 7, :], AX_X, ALU.max))
                        dve.tensor_scalar(g1[:, 4:5], g1[:, 2:3], -1.0, 1.0, ALU.mult, ALU.add)
                        step(dve.scalar_tensor_tensor(out=g8[:, 8, :], in0=g8[:, 7, :], scalar=g1[:, 2:3],
                                                      in1=rank[:, :], op0=ALU.is_equal, op1=ALU.mult))
                        step(dve.tensor_reduce(g1[:, 3:4], g8[:, 8, :], AX_X, ALU.max))
                        assert count[0] == STEPS
                        dve.tensor_scalar(low_h[:, 64:GK], g8[:, 8, :], g1[:, 3:4], g1[:, 2:3], ALU.is_equal,
                                          ALU.mult).then_inc(f_w, 1)
                        dve.wait_ge(f_w, b * TB + i + 1)
                        lh = low_h[:, 0:64].rearrange("p (n h) -> p n h", h=LOW)
                        dve.tensor_tensor(lh, lh, low_h[:, 64:GK].unsqueeze(2).broadcast_to([P, EXPERTS, LOW]),
                                          ALU.mult).then_inc(f_g, 1)
                        dve.scalar_tensor_tensor(out=flat(i), in0=xn3[:, par, :], scalar=g1[:, 4:5], in1=flat(i),
                                                 op0=ALU.mult, op1=ALU.add).then_inc(f_x, 1)

                    def lowered(i):
                        dve.wait_ge(l_hi, b * TB + i + 1)
                        dve.tensor_tensor(lt_lo[:, :], ps_o[0:GK, 0:P], f(lt_hi[:, :]), ALU.subtract).then_inc(l_ok, 1)

                    def finish(i):
                        dve.wait_ge(u_mm, b * TB + i + 1 + 1)
                        dve.wait_ge(f_x, b * TB + i + 1)
                        dve.tensor_tensor(flat(i), ps_s[1][:, :], flat(i), ALU.add).then_inc(y_ok, 1)

                    def tail_block(i, par):
                        cross(i)
                        if has(i + 1):
                            turned_block(i + 1, 0, t2_lo, t2_hi)
                        norm(i, 1, 1 + par)
                        if second(i):
                            finish(i - 2)
                        if not first(i):
                            gate(i - 1, 1 - par)
                        if has(i + 2):
                            norm(i + 2, 0, 0)
                        if not first(i):
                            lowered(i - 1)
                        turned_block(i, 1, t3_lo, t3_hi)

                    norm(0, 0, 0)
                    turned_block(0, 0, t2_lo, t2_hi)
                    norm(1, 0, 0)
                    tail_blocks(dve, tail_block)
                    finish(TB - 2)
                    gate(TB - 1, 1)
                    lowered(TB - 1)
                    finish(TB - 1)
                    end_phase(dve, b, 4)

            @block.gpsimd
            def _(pool):
                pool.memset(ones[:, :], 1.0).then_inc(setup_cst, 1)
                pool.memset(neg_half[:, :], -0.5)
                for n in range(EXPERTS):
                    pool.memset(rank[:, n:n + 1], float(EXPERTS - n))
                pool.memset(ident[:, :], 0.0)
                pool.memset(ident_bf[:, :], 0.0)
                pool.memset(mask_bf[:, :], 0.0).then_inc(setup_cst, 1)
                pool.wait_ge(setup_cst, 2)
                for m in (ident, ident_bf):
                    pool.affine_select(out=m[:, :], in_=m[:, :], compare_op=ALU.not_equal, fill=1.0,
                                       base=0, pattern=[[-1, P]], channel_multiplier=1)
                pool.affine_select(out=mask_bf[:, :], in_=mask_bf[:, :], compare_op=ALU.is_ge, fill=-NEG,
                                   base=0, pattern=[[-1, P]], channel_multiplier=1)

                def split_piece(n, k):
                    slot = k % 3
                    pool.wait_ge(w_in[k % 2], n * 48 + 16 * (k // 2 + 1))
                    if not (isinstance(n, int) and n == 0 and k < 2):
                        t, half = divmod(k - 3, 2)
                        pool.wait_ge(part_ok, n * PROJ + (2 * t + 1) * PARTS + (half + 1) * (PARTS // 2) + C_PART)
                        alone(pool)
                    alone(pool)
                    pool.tensor_scalar(w_hi[:, slot, :, :], w_raw[:, k % 2, :, :], 1.0, 1.0, ALU.mult,
                                       ALU.mult).then_inc(w_hi_ok, 1)
                    pool.wait_ge(w_hi_ok, n * 6 + k + 1)
                    pool.tensor_tensor(w_lo[:, slot, :, :], w_raw[:, k % 2, :, :], f(w_hi[:, slot, :, :]),
                                       ALU.subtract).then_inc(w_split, 1)

                def project(b, pair, t, h, k):
                    if (h, k) == (0, 0):
                        split_piece(b * PAIRS + pair, 2 * t + 2)
                    if (h, k) == (1, PARTS // 2):
                        split_piece(b * PAIRS + pair, 2 * t + 3)

                def attend(b, hp, order):
                    n = b * PAIRS + hp
                    for e in order:
                        if e[0] == "norm":
                            _, j, qb = e
                            i, r = 8 * j + qb, slice(off(qb), off(qb + 1))
                            pool.wait_ge(rden_ok, n * 16 + i + 1)
                            alone(pool)
                            pool.tensor_scalar(probs[:, r], probs[:, r], rden[:, i:i + 1], 1.0, ALU.mult,
                                               ALU.mult).then_inc(norm_ok, 1)
                        elif e[0] == "proj":
                            project(b, hp + 1, *e[1:])

                def inverse_sigma(s, n, mv_ok, ve_ok, rs_ok):
                    pool.wait_ge(mv_ok, n + 1)
                    alone(pool)
                    pool.tensor_scalar(veps[:, s:s + 1], mv[:, s, 1:2], EPS, 1.0, ALU.add, ALU.mult).then_inc(ve_ok, 1)
                    pool.wait_ge(ve_ok, n + 1)
                    pool.tensor_tensor(rstd[:, s:s + 1], veps[:, s:s + 1], neg_half[:, :], ALU.pow).then_inc(rs_ok, 1)

                end_setup(pool)
                pool.sem_inc(w_split, C_SPLIT)
                for k in range(2):
                    split_piece(0, k)
                with pool.Fori(0, BATCH) as b:
                    with pool.Fori(0, TB // 2) as v:
                        for s in range(2):
                            inverse_sigma(s, b * TB + v * 2 + s, ln_mv, ln_ve, ln_rs)
                    end_phase(pool, b, 0)

                    for t in range(3):
                        for h in range(2):
                            for k in range(PARTS):
                                project(b, 0, t, h, k)
                    with pool.Fori(0, PAIRS - 1) as hp:
                        attend(b, hp, body)
                    attend(b, PAIRS - 1, tail_body)
                    end_phase(pool, b, 1)
                    end_phase(pool, b, 2)

                    for mb in range(TB):
                        pool.wait_ge(e_rd, b * TB + mb + 1)
                        alone(pool)
                        pool.tensor_scalar(c_probs[:, mb % 2, :], c_probs[:, mb % 2, :], rden[:, mb:mb + 1], 1.0,
                                           ALU.mult, ALU.mult).then_inc(e_norm, 1)
                    end_phase(pool, b, 3)

                    def tail_norm(i, k, slot):
                        n = norm_base(b, i, k)
                        inverse_sigma(slot, n, t_mv, t_ve, t_rs)
                        pool.wait_ge(t_rs, n + 1)
                        alone(pool)
                        pool.tensor_scalar(shift[:, slot:slot + 1], mv[:, slot, 0:1], rstd[:, slot:slot + 1], -1.0,
                                           ALU.mult, ALU.mult).then_inc(t_sh, 1)

                    def tail_block(i, par):
                        tail_norm(i, 1, 1 + par)
                        if has(i + 2):
                            tail_norm(i + 2, 0, 0)

                    tail_norm(0, 0, 0)
                    tail_norm(1, 0, 0)
                    tail_blocks(pool, tail_block)
                    end_phase(pool, b, 4)


def kernel(x, ctx_1024, L0_attn_w_qkv, L0_attn_w_out, L0_xattn_Wq, L0_xattn_bq, L0_xattn_Wk, L0_xattn_bk,
           L0_ffn_select_weight, L0_ffn_select_mean_diff, L0_ffn_imp_center, L0_ffn_imp_slope,
           L0_ffn_lora_update, L0_ffn_lora_degen, L0_ffn_bias_w, L0_ffn_debias_w):
    import numpy as np
    import concourse.bacc as bacc
    from concourse.bass_utils import run_bass_kernel_spmd

    def by_columns(w, n):
        return np.asarray(w).transpose(1, 0, 2).reshape(DM, n)

    w = np.asarray(L0_attn_w_qkv).reshape(2, CC, P, 3, PAIRS, P).transpose(4, 3, 2, 0, 1, 5)
    arrays = {
        "x": np.asarray(x).reshape(BATCH, TB, P, DM),
        "w_qkv": w.reshape(3 * PAIRS, P, 2, CC, P),
        "w_out": np.asarray(L0_attn_w_out).reshape(KC, P, DM),
        "ctx_t": np.asarray(ctx_1024).transpose(0, 2, 1).reshape(BATCH, CC, P, SEQ).transpose(0, 2, 1, 3),
        "w_ctx": np.stack([np.asarray(m).T.reshape(CC, P, CD) for m in (L0_xattn_Wq, L0_xattn_Wk)]).transpose(2, 0, 1, 3),
        "b_ctx": np.stack([np.asarray(L0_xattn_bq), np.asarray(L0_xattn_bk)], axis=1),
        "w_ffn": np.concatenate([by_columns(L0_ffn_select_weight, 64), by_columns(L0_ffn_lora_update, 64),
                                 np.asarray(L0_ffn_select_mean_diff).T], axis=1),
        "v_ffn": np.concatenate([np.asarray(L0_ffn_select_mean_diff).T, np.asarray(L0_ffn_debias_w).T], axis=1),
        "w_up": np.concatenate([np.asarray(L0_ffn_lora_degen).transpose(0, 2, 1).reshape(EXPERTS * LOW, DM),
                                np.asarray(L0_ffn_bias_w)], axis=0),
        "center": np.asarray(L0_ffn_imp_center).reshape(1, EXPERTS),
        "slope": np.asarray(L0_ffn_imp_slope).reshape(1, EXPERTS),
    }
    arrays = {n: np.ascontiguousarray(a) for n, a in arrays.items()}
    nc = bacc.Bacc("TRN2", target_bir_lowering=False, num_devices=1)
    args = [nc.dram_tensor(f"in_{n}", a.shape, mybir.dt.from_np(a.dtype), kind="ExternalInput").ap()
            for n, a in arrays.items()]
    out = nc.dram_tensor("out", (BATCH, TB, P, DM), F32, kind="ExternalOutput").ap()
    decoder_layer(nc, *args, out)
    result = run_bass_kernel_spmd(nc, [{f"in_{n}": a for n, a in arrays.items()}], core_ids=[0])
    return result.results[0]["out"].reshape(BATCH, SEQ, DM)
```

```python
from contextlib import ExitStack

import concourse.bass as bass
from concourse import mybir

F32 = mybir.dt.float32
F32R = mybir.dt.float32r
BF16 = mybir.dt.bfloat16
ALU = mybir.AluOpType
ACT = mybir.ActivationFunctionType
AX_X = mybir.AxisListType.X

P = 128
BATCH, SEQ, DM = 4, 1024, 1024
HEADS, HD = 16, 64
PAIRS = HEADS // 2
TB = SEQ // P
KC = DM // P
CTX, CD = 512, 128
CC = CTX // P
CQ = SEQ // 4
EXPERTS, SEL, LOW = 8, 8, 8
FW = EXPERTS * SEL + EXPERTS * LOW + EXPERTS
GK = EXPERTS * LOW + EXPERTS
HALF = 512
EPS = 1e-5
NEG = -1e10
PARTS = 4
A, B = 0, 1



PAIR_STEPS = """
    P SA0 KB0 SA1 P P KB1 SA2 EA0 SA3 P EA1 KB2 EA2 NA0 NA1 EA3 SA4 NA2 C00 NA3 EA4 SA5 NA4 VA P EA5
    SA6 TA00 P SA7 EA6 TA01 TA02 MA00 P P NA5 NA6 SB0 EA7 MA01 NA7 SB1 C01 MA02 TA03 P EB0 P MA03
    NB0 SB2 OA0 TA10 P P EB1 C10 TA11 MA10 TA12 NB1 P EB2 SB3 MA11 TA13 TA14 MA12 EB3 NB2 P SB4 NB3
    MA13 TA15 VB MA14 P SB5 TA16 EB4 TA17 EB5 MA15 NB4 P SB6 C11 NB5 MA16 TB00 SB7 P MA17 EB6 NB6
    OA1 TB01 P EB7 P NB7 TB02 MB00 MB01 TB03 KA0 P MB02 C20 MB03 TB10 OB0 TB11 P KA1 P MB10 TB12
    TB13 KA2 MB11 P MB12 TB14 TB15 MB13 P MB14 C21 TB16 TB17 MB15 MB16 MB17 OB1
"""
LAST_STEPS = """
    SA0 W SA1 KB0 W W SA2 W SA3 EA0 EA1 KB1 W EA2 EA3 W SA4 NA0 NA1 NA2 NA3 W SA5 KB2 SA6 EA4 EA5
    NA4 VA NA5 SA7 TA00 EA6 NA6 TA01 SB0 EA7 NA7 W MA00 TA02 W MA01 TA03 SB1 MA02 MA03 OA0 TA10 EB0
    NB0 TA11 EB1 W SB2 MA10 W TA12 TA13 MA11 SB3 NB1 EB2 TA14 MA12 MA13 TA15 W SB4 EB3 VB MA14 NB2
    NB3 TA16 EB4 SB5 MA15 NB4 TA17 MA16 SB6 EB5 W MA17 NB5 OA1 EB6 SB7 TB00 EB7 NB6 NB7 TB01 MB00
    TB02 W TB03 MB01 MB02 TB10 MB03 OB0 W TB11 TB12 W MB10 MB11 TB13 MB12 TB14 TB15 MB13 TB16 MB14
    TB17 MB15 MB16 MB17 OB1
"""
KINDS = {"S": "scores", "E": "exp", "N": "norm", "T": "turn", "M": "mix", "O": "take", "V": "vturn",
         "K": "stack", "P": "proj", "C": "copy", "W": "split_out"}


def attention_order(text):
    parts = {"P": [(t, h, k) for t in range(3) for h in range(2) for k in range(PARTS)],
             "W": [(q,) for q in range(2 * KC)]}
    order = []
    for word in text.split():
        args = parts[word].pop(0) if word in parts else [("AB".index(c) if c in "AB" else int(c)) for c in word[1:]]
        order.append((KINDS[word[0]], *args))
    return order


def decoder_layer(nc, x, w_qkv, w_out, ctx_t, w_ctx, b_ctx, w_ffn, v_ffn, w_up, center, slope, out):
    es = ExitStack()
    with es:
        def sem(name):
            return es.enter_context(nc.semaphore(name))

        def sb(stack, name, shape, dt=F32):
            return stack.enter_context(nc.sbuf_tensor(name, shape, dt))

        ident = sb(es, "ident", [P, P])
        ident_bf = sb(es, "ident_bf", [P, P], BF16)
        mask_bf = sb(es, "mask_bf", [P, P], BF16)
        ffn_hi = sb(es, "ffn_hi", [P, KC, FW], F32R)
        ffn_lo = sb(es, "ffn_lo", [P, KC, FW], F32R)
        up_hi = sb(es, "up_hi", [GK, DM], F32R)
        up_lo = sb(es, "up_lo", [GK, DM], F32R)
        ffn_c = sb(es, "ffn_c", [P, FW])
        center_b = sb(es, "center_b", [P, EXPERTS])
        slope_b = sb(es, "slope_b", [P, EXPERTS])
        rank = sb(es, "rank", [P, EXPERTS])
        neg_half = sb(es, "neg_half", [P, 1])
        bias_c = sb(es, "bias_c", [P, 2])
        otx = sb(es, "otx", [P, TB, KC, P])
        w_raw = sb(es, "w_raw", [P, 2, CC, P])
        w_hi = sb(es, "w_hi", [P, 3, CC, P], F32R)
        w_lo = sb(es, "w_lo", [P, 3, CC, P], F32R)
        bn = sb(es, "bn", [P, 5, 2, 6])
        mv = sb(es, "mv", [P, 5, 2])
        veps = sb(es, "veps", [P, 5])
        rstd = sb(es, "rstd", [P, 5])
        shift = sb(es, "shift", [P, 5])
        low = sb(es, "low", [P, 2 * HEADS])
        den = sb(es, "den", [P, 2 * HEADS])
        rden = sb(es, "rden", [P, 2 * HEADS])

        with ExitStack() as s0:
            ffn_raw = sb(s0, "ffn_raw", [P, KC, FW])
            vec_raw = sb(s0, "vec_raw", [P, KC, 2 * EXPERTS])
            ffn_prod = sb(s0, "ffn_prod", [P, KC, FW])
            up_raw = sb(s0, "up_raw", [GK, DM])
            ones = sb(s0, "ones", [P, P])
        with ExitStack() as s1:
            xt_hi = sb(s1, "xt_hi", [P, KC, SEQ], F32R)
            xt_lo = sb(s1, "xt_lo", [P, KC, SEQ], F32R)
            qkv = sb(s1, "qkv", [P, 3, SEQ])
            q_st = [sb(s1, f"q_st{j}", [P, SEQ], F32R) for j in range(2)]
            k_hi = [sb(s1, f"k_hi{j}", [P, SEQ], F32R) for j in range(2)]
            k_lo = [sb(s1, f"k_lo{j}", [P, SEQ], F32R) for j in range(2)]
            v_st = [sb(s1, f"v_st{j}", [P, TB, 2 * HD], F32R) for j in range(2)]
            probs = sb(s1, "probs", [P, TB * (TB + 1) // 2 * P])
            pt_hi = sb(s1, "pt_hi", [P, 2, HALF], F32R)
            pt_lo = sb(s1, "pt_lo", [P, 2, HALF], F32R)
            o_lo = sb(s1, "o_lo", [HD, HALF])
        with ExitStack() as s4:
            at_hi = sb(s4, "at_hi", [P, KC, DM], F32R)
            at_lo = sb(s4, "at_lo", [P, KC, DM], F32R)
            wo_hi, wo_lo = at_hi, at_lo
            with ExitStack() as s3:
                o_hi = sb(s3, "o_hi", [P, 2, KC, P], F32R)
                o_rest = sb(s3, "o_rest", [P, 2, KC, P], F32R)
                x_res = sb(s3, "x_res", [P, 2, DM])
            x_in = sb(s4, "x_in", [P, TB, DM])
            xn2 = sb(s4, "xn2", [P, DM])
            with ExitStack() as s5:
                qk_hi = sb(s5, "qk_hi", [P, 2, SEQ], F32R)
                qk_lo = sb(s5, "qk_lo", [P, 2, SEQ], F32R)
                with ExitStack() as s7:
                    wc_raw = sb(s7, "wc_raw", [P, 2, CC, CD])
                    wc_hi = sb(s7, "wc_hi", [P, 2, CC, CD], F32R)
                    wc_lo = sb(s7, "wc_lo", [P, 2, CC, CD], F32R)
                    ctx_raw = sb(s7, "ctx_raw", [P, CC, CQ])
                    ctx_hi = sb(s7, "ctx_hi", [P, CC, CQ], F32R)
                    ctx_lo = sb(s7, "ctx_lo", [P, CC, CQ], F32R)
                c_probs = sb(s5, "c_probs", [P, 4, SEQ])
                t2_hi = sb(s5, "t2_hi", [P, KC, P], F32R)
                t2_lo = sb(s5, "t2_lo", [P, KC, P], F32R)
            with ExitStack() as s6:
                xn3 = sb(s6, "xn3", [P, 2, DM])
                t3_hi = sb(s6, "t3_hi", [P, KC, P], F32R)
                t3_lo = sb(s6, "t3_lo", [P, KC, P], F32R)
                sel_u = sb(s6, "sel_u", [P, EXPERTS * SEL])
                sel_sq = sb(s6, "sel_sq", [P, EXPERTS * SEL])
                g8 = sb(s6, "g8", [P, 12, EXPERTS])
                g1 = sb(s6, "g1", [P, 8])
                low_h = sb(s6, "low_h", [P, GK])
                lt_hi = sb(s6, "lt_hi", [GK, P], F32R)
                lt_lo = sb(s6, "lt_lo", [GK, P], F32R)

        ps_s = [es.enter_context(nc.psum_tensor(f"ps_s{i}", [P, DM], F32)) for i in range(2)]
        ps_t = [es.enter_context(nc.psum_tensor(f"ps_t{i}", [P, HALF], F32)) for i in range(2)]
        ps_op = es.enter_context(nc.psum_tensor("ps_op", [P, DM], F32))
        ps_o, ps_p = ps_op[:, 0:HALF], ps_op[:, HALF:DM]

        phase_done = sem("phase_done")
        passed = sem("passed")
        PHASES = 2
        setup_in, setup_cst, setup_prod, setup_mm, setup_split = (
            sem(n) for n in ("setup_in", "setup_cst", "setup_prod", "setup_mm", "setup_split"))
        ln_in, ln_bn, ln_mv, ln_ve, ln_rs, ln_sh, ln_xn, ln_turn, ln_hi, ln_lo = (
            sem(n) for n in ("ln_in", "ln_bn", "ln_mv", "ln_ve", "ln_rs", "ln_sh", "ln_xn", "ln_turn", "ln_hi", "ln_lo"))
        w_in = [sem(f"w_in{s}") for s in range(2)]
        w_hi_ok, w_split, part_ok, proj_out = (sem(n) for n in ("w_hi_ok", "w_split", "part_ok", "proj_out"))
        q_hi_ok, k_hi_ok, k_lo_ok, stack_ok = (sem(n) for n in ("q_hi_ok", "k_hi_ok", "k_lo_ok", "stack_ok"))
        scores_ok, low_ok, exp_ok, rden_ok, norm_ok = (
            sem(n) for n in ("scores_ok", "low_ok", "exp_ok", "rden_ok", "norm_ok"))
        turn_ok, hi_ok, lo_ok, mix_ok, o_lo_ok, o_ok = (
            sem(n) for n in ("turn_ok", "hi_ok", "lo_ok", "mix_ok", "o_lo_ok", "o_ok"))
        wo_in = [sem(f"wo_in{s}") for s in range(2)]
        wo_hi_ok, wo_ok, st_hi, st_ok, out_mm, x1_ok = (
            sem(n) for n in ("wo_hi_ok", "wo_ok", "st_hi", "st_ok", "out_mm", "x1_ok"))
        xr_in = [sem(f"xr_in{s}") for s in range(2)]
        c_win, c_in, c_whi, c_wok, c_hi, c_split, c_mm, c_qhi, c_qk = (
            sem(n) for n in ("c_win", "c_in", "c_whi", "c_wok", "c_hi", "c_split", "c_mm", "c_qhi", "c_qk"))
        e_mm, e_mx, e_neg, e_exp, e_rd, e_norm, e_turn, e_hi, e_lo = (
            sem(n) for n in ("e_mm", "e_mx", "e_neg", "e_exp", "e_rd", "e_norm", "e_turn", "e_hi", "e_lo"))
        t_bn, t_mv, t_ve, t_rs, t_sh, t_xn2, t_xn3 = (
            sem(n) for n in ("t_bn", "t_mv", "t_ve", "t_rs", "t_sh", "t_xn2", "t_xn3"))
        t_turn, t_hi, t_lo, xm_ok, x2_ok = (sem(n) for n in ("t_turn", "t_hi", "t_lo", "xm_ok", "x2_ok"))
        f_mm, f_step, f_e, f_z, f_w, f_x, f_g, l_turn, l_hi, l_ok, u_mm, y_ok, y_out = (
            sem(n) for n in ("f_mm", "f_step", "f_e", "f_z", "f_w", "f_x", "f_g", "l_turn", "l_hi", "l_ok", "u_mm", "y_ok", "y_out"))

        C_EXP, C_LO, C_TURN, C_MIX, C_O, C_PROJ, C_SCORES, C_PART, C_SPLIT = 2, 2, 26, 24, 1, 2, 16, 8, 2
        C_LN, C_OUT, C_ONE = 2, 2, 1

        body, tail_body = attention_order(PAIR_STEPS), attention_order(LAST_STEPS)
        TURNS = sum(e[0] in ("turn", "vturn") for e in body)
        MIXES = sum(e[0] == "mix" for e in body)
        TURNS_B = PAIRS * TURNS
        PROJ = 6 * PARTS
        assert TURNS % 2 == 0 and C_TURN == TURNS and C_MIX == MIXES

        def numbered(order, kinds):
            n, at = 0, {}
            for e in order:
                if e[0] in kinds:
                    at[e] = n
                    n += 1
            return at

        body_turns, body_mixes = numbered(body, ("turn", "vturn")), numbered(body, ("mix",))
        assert numbered(tail_body, ("turn", "vturn")) == body_turns
        assert numbered(tail_body, ("mix",)) == body_mixes
        prev_last_turn = {g: body_turns[("turn", B, g, 4 * g + 3)] for g in range(2)}

        def off(qb):
            return qb * (qb + 1) // 2 * P

        def cols(g, kb):
            return max(kb - 4 * g, 0) * P

        def opposite(j):
            return slice(HD * (1 - j), HD * (1 - j) + HD)

        def own(j):
            return slice(HD * j, HD * j + HD)

        def f(ap):
            return ap.bitcast(F32)

        def alone(eng):
            eng.sem_inc(passed, 1)

        def end_phase(eng, b, k):
            alone(eng)
            eng.drain().then_inc(phase_done, 1)
            eng.wait_ge(phase_done, b * (5 * PHASES) + 5 * (k + 2))
            alone(eng)

        def end_setup(eng):
            eng.drain().then_inc(phase_done, 1)
            eng.wait_ge(phase_done, 5)

        def x_bank(i, h):
            return ps_t[h][:, :] if i % 2 else ps_s[0][:, h * HALF:(h + 1) * HALF]

        EARLY = 4

        def e_bank(mb):
            return ps_op if mb < EARLY else ps_s[mb % 2]

        def at_bank(mb, h):
            return ps_op[:, h * HALF:(h + 1) * HALF] if mb % 2 else ps_t[h][:, :]

        first_banks = [ps_p, ps_o]

        def turns4(bank):
            return bank.rearrange("p (k t) -> p k t", k=4)

        def turn_base(b, i, k):
            base = b * (4 * TB)
            if isinstance(i, int):
                if k == 0:
                    return base + (0 if i == 0 else 2 if i == 1 else 4 * i - 2)
                return base + (4 * i + 4 if i < TB - 1 else 4 * TB - 2)
            return base + i * 4 - 2 if k == 0 else base + i * 4 + 4

        def norm_base(b, i, k):
            base = b * (2 * TB)
            if k == 0:
                return base + (0 if isinstance(i, int) and i == 0 else i * 2 - 1)
            return base + (2 * TB - 1 if isinstance(i, int) and i == TB - 1 else i * 2 + 2)

        def second(i):
            return not isinstance(i, int) or i >= 2

        def first(i):
            return isinstance(i, int) and i == 0

        def last(i):
            return isinstance(i, int) and i == TB - 1

        def has(i):
            return not isinstance(i, int) or i < TB

        def tail_blocks(eng, tail_block):
            tail_block(0, 0)
            tail_block(1, 1)
            with eng.Fori(0, TB // 2 - 2) as v:
                tail_block(v * 2 + 2, 0)
                tail_block(v * 2 + 3, 1)
            tail_block(TB - 2, 0)
            tail_block(TB - 1, 1)

        def load_x(sp, b):
            for h in range(2):
                sp.dma_start(x_in[:, 4 * h:4 * h + 4, :],
                             x[b, 4 * h:4 * h + 4].rearrange("t p d -> p t d")).then_inc(ln_in, 16)

        with nc.Block() as block:

            @block.sync
            def _(sp):
                sp.dma_start(ffn_raw[:, :, :], w_ffn.rearrange("(k p) c -> p k c", p=P)).then_inc(setup_in, 16)
                sp.dma_start(vec_raw[:, :, :], v_ffn.rearrange("(k p) c -> p k c", p=P)).then_inc(setup_in, 16)
                sp.dma_start(up_raw[:, :], w_up).then_inc(setup_in, 16)
                sp.dma_start(center_b[:, :], center.broadcast_to([P, EXPERTS])).then_inc(setup_in, 16)
                sp.dma_start(slope_b[:, :], slope.broadcast_to([P, EXPERTS])).then_inc(setup_in, 16)
                sp.dma_start(bias_c[:, :], b_ctx).then_inc(setup_in, 16)
                for u in range(2):
                    sp.dma_start(w_raw[:, u, :, :], w_qkv[0, :, u]).then_inc(w_in[u], 16)
                load_x(sp, 0)
                sp.wait_ge(setup_in, 96)
                end_setup(sp)
                for u in range(2):
                    sp.wait_ge(w_split, u + 1 + C_SPLIT)
                    sp.dma_start(w_raw[:, u, :, :], w_qkv[1, :, u]).then_inc(w_in[u], 16)

                with sp.Fori(0, BATCH) as b:
                    with sp.Fori(2, 3 * PAIRS) as t:
                        for u in range(2):
                            sp.wait_ge(w_split, b * (6 * PAIRS) + t * 2 + u - 1 + C_SPLIT)
                            alone(sp)
                            sp.dma_start(w_raw[:, u, :, :], w_qkv[t, :, u]).then_inc(w_in[u], 16)
                    for u in range(2):
                        sp.wait_ge(w_split, b * (6 * PAIRS) + 6 * PAIRS - 1 + u + C_SPLIT)
                        alone(sp)
                        sp.dma_start(w_raw[:, u, :, :], w_qkv[0, :, u]).then_inc(w_in[u], 16)
                    sp.wait_ge(w_split, b * (6 * PAIRS) + 6 * PAIRS + 2 + C_SPLIT)
                    alone(sp)
                    with sp.Fori(0, KC) as k:
                        for u in range(2):
                            sp.wait_ge(wo_ok, b * (2 * KC) + k * 2 + u - 1 + C_OUT)
                            alone(sp)
                            sp.dma_start(w_raw[:, u, :, :].rearrange("p c d -> p (c d)"),
                                         w_out[k, :, u * HALF:(u + 1) * HALF]).then_inc(wo_in[u], 16)
                    sp.wait_ge(wo_ok, b * (2 * KC) + 2 * KC + C_OUT)
                    alone(sp)
                    for u in range(2):
                        sp.dma_start(w_raw[:, u, :, :], w_qkv[1, :, u]).then_inc(w_in[u], 16)
                    end_phase(sp, b, 0)

                    def load_ctx(q):
                        sp.wait_ge(c_split, b * 4 + q + C_ONE)
                        alone(sp)
                        sp.dma_start(ctx_raw[:, :, :], ctx_t[b, :, :, q * CQ:(q + 1) * CQ]).then_inc(c_in, 16)

                    def load_x_again(t):
                        sp.wait_ge(x1_ok, b * TB + t + 1)
                        alone(sp)
                        sp.dma_start(x_res[:, t % 2, :], x[b, t]).then_inc(xr_in[t % 2], 16)

                    sp.dma_start(wc_raw[:, :, :, :], w_ctx).then_inc(c_win, 16)
                    load_ctx(0)
                    load_x_again(0)
                    load_x_again(1)
                    for t in range(2, TB):
                        if t - 1 < 4:
                            load_ctx(t - 1)
                        load_x_again(t)

                    sp.wait_ge(x1_ok, b * TB + TB + C_OUT)
                    alone(sp)
                    load_x(sp, (b + 1) % BATCH)

                    with sp.Fori(0, TB) as i:
                        sp.wait_ge(y_ok, b * TB + i + 1 + C_ONE)
                        alone(sp)
                        sp.dma_start(out[b, i], otx[:, i, :, :].rearrange("p k t -> p (k t)")).then_inc(y_out, 16)
                    sp.wait_ge(y_out, b * (16 * TB) + 16 * TB)
                    alone(sp)
                    end_phase(sp, b, 1)

            @block.tensor
            def _(pe):
                def split_mm(ps, lhs, rhs, n, steps, start, stop):
                    for k in steps:
                        (lh, ll), (rh, rl) = lhs(k), rhs(k)
                        pe.matmul(ps, lh, rh, start=start and k == steps[0], stop=False)
                        pe.matmul(ps, lh, rl, start=False, stop=False)
                        mm = pe.matmul(ps, ll, rh, start=False, stop=stop and k == steps[-1])
                    return mm

                pe.wait_ge(setup_prod, 1)
                pe.wait_ge(setup_cst, 1)
                for k in range(KC):
                    mm = pe.matmul(ps_p[:, 0:FW], ones[:, :], ffn_prod[:, k, :], start=k == 0, stop=k == KC - 1)
                mm.then_inc(setup_mm, 1)
                end_setup(pe)

                def project(b, pair, t, h, k, banks):
                    n = b * PAIRS + pair
                    piece = k * 2 // PARTS
                    bank = banks[(2 * t + h) % len(banks)]
                    if k == 0:
                        pe.wait_ge(proj_out, n * 6 + 2 * t + h + 1 - len(banks) + C_PROJ)
                    if h == 0 and k * 2 % PARTS == 0:
                        pe.wait_ge(w_split, n * 6 + 2 * t + piece + 1 + C_SPLIT)
                    slot = (2 * t + piece) % 3
                    split_mm(bank[:, :],
                             lambda c: (w_hi[:, slot, c - CC * piece, :], w_lo[:, slot, c - CC * piece, :]),
                             lambda c: (xt_hi[:, c, h * HALF:(h + 1) * HALF], xt_lo[:, c, h * HALF:(h + 1) * HALF]),
                             HALF, list(range(KC // PARTS * k, KC // PARTS * (k + 1))), k == 0,
                             k == PARTS - 1).then_inc(part_ok, 1)

                def turn_values(b, pair, j, turn, bank):
                    pe.wait_ge(lo_ok, turn + C_LO - 1)
                    pe.wait_ge(proj_out, (b * PAIRS + pair) * 6 + 6 + C_PROJ)
                    alone(pe)
                    for kb in range(TB):
                        mm = pe.transpose(bank[:, kb * HD:(kb + 1) * HD],
                                          qkv[own(j), 2, kb * P:(kb + 1) * P], ident[own(j), own(j)])
                    mm.then_inc(turn_ok, 1)

                def attend(b, hp, order):
                    n = b * PAIRS + hp
                    t0 = b * TURNS_B + hp * TURNS
                    for e in order:
                        if e[0] == "scores":
                            _, j, qb = e
                            i, w = 8 * j + qb, (qb + 1) * P
                            pe.wait_ge(exp_ok, n * 16 + i + C_EXP - 1)
                            if qb == 0:
                                pe.wait_ge(stack_ok, n * 2 + j + 1)
                            q = q_st[j][:, qb * P:(qb + 1) * P]
                            for c in range(0, w, HALF):
                                d = min(c + HALF, w)
                                o = ps_s[qb % 2][:, c:d]
                                pe.matmul(o, q, k_hi[j][:, c:d], start=True, stop=False)
                                pe.matmul(o, q, k_lo[j][:, c:d], start=False, stop=True)
                            mm = pe.matmul(ps_s[qb % 2][:, w - P:w], ident_bf[:, :], mask_bf[:, :],
                                           start=False, stop=True, skip_group_check=True)
                            mm.then_inc(scores_ok, 1)
                        elif e[0] == "turn":
                            _, j, g, kb = e
                            pe.wait_ge(lo_ok, t0 + body_turns[e] + C_LO - 1)
                            if kb == 0:
                                pe.wait_ge(norm_ok, n * 16 + 8 * j + 4 * g + 4)
                            for qb in range(max(4 * g, kb), 4 * g + 4):
                                mm = pe.transpose(ps_t[body_turns[e] % 2][:, (qb - 4 * g) * P:(qb - 4 * g + 1) * P],
                                                  probs[:, off(qb) + kb * P:off(qb) + (kb + 1) * P], ident[:, :])
                            mm.then_inc(turn_ok, 1)
                        elif e[0] == "mix":
                            _, j, g, kb = e
                            pe.wait_ge(lo_ok, t0 + body_turns[("turn", j, g, kb)] + 1 + C_LO)
                            if kb == 0:
                                pe.wait_ge(o_ok, n * 4 + 2 * j + g + C_O)
                            s, c, end = body_mixes[e] % 2, cols(g, kb), kb == 4 * g + 3
                            pe.matmul(ps_o[:, c:HALF], v_st[j][:, kb, :], pt_hi[:, s, c:HALF],
                                      start=kb == 0, stop=False)
                            mm = pe.matmul(ps_o[:, c:HALF], v_st[j][:, kb, :], pt_lo[:, s, c:HALF],
                                           start=False, stop=end)
                            mm.then_inc(mix_ok, 1)
                        elif e[0] == "vturn":
                            bank = ps_t[body_turns[e] % 2]
                            turn_values(b, hp, e[1], t0 + body_turns[e], bank)
                        elif e[0] == "proj":
                            project(b, hp + 1, *e[1:], [ps_p])

                pe.sem_inc(turn_ok, C_TURN)
                pe.sem_inc(mix_ok, C_MIX)
                pe.sem_inc(scores_ok, C_SCORES)
                pe.sem_inc(part_ok, C_PART)
                pe.sem_inc(out_mm, C_OUT)
                pe.sem_inc(u_mm, C_ONE)

                def turn_x(n, i):
                    pe.wait_ge(ln_xn, n * TB + i + 1 + C_LN)
                    for h in range(2):
                        pe.wait_ge(ln_lo, n * (2 * TB) + 2 * i + h + 1)
                        for c in range(4):
                            mm = pe.transpose(x_bank(i, h)[:, c * P:(c + 1) * P],
                                              x_in[:, i, (4 * h + c) * P:(4 * h + c + 1) * P], ident[:, :])
                        mm.then_inc(ln_turn, 1)

                for i in range(TB):
                    turn_x(0, i)
                with pe.Fori(0, BATCH) as b:
                    pe.wait_ge(ln_lo, b * (2 * TB) + 2 * TB + 4)
                    for t in range(3):
                        for h in range(2):
                            for k in range(PARTS):
                                project(b, 0, t, h, k, first_banks)
                    with pe.Fori(0, PAIRS - 1) as hp:
                        attend(b, hp, body)
                    attend(b, PAIRS - 1, tail_body)
                    alone(pe)
                    pe.drain().then_inc(phase_done, 1)

                    def project_out(v, s, h):
                        if h == 0:
                            pe.wait_ge(st_ok, b * TB + v * 2 + s + 1)
                            pe.wait_ge(wo_ok, b * (2 * KC) + 2 * KC + C_OUT)
                            pe.wait_ge(x1_ok, b * TB + v * 2 + s + 1)
                        r = slice(h * HALF, (h + 1) * HALF)
                        mm = split_mm(ps_s[s][:, r], lambda c: (o_hi[:, s, c, :], o_rest[:, s, c, :]),
                                      lambda c: (wo_hi[:, c, r], wo_lo[:, c, r]), HALF, list(range(KC)), True, True)
                        if h == 1:
                            mm.then_inc(out_mm, 1)

                    def queries_keys(v):
                        pe.wait_ge(c_wok, b + 1)
                        pe.wait_ge(c_split, b * 4 + v + 1 + C_ONE)
                        for t in range(2):
                            pe.wait_ge(c_qk, b * 8 + v * 2 + t + 1)
                            split_mm(ps_t[t][:, 0:CQ], lambda c: (wc_hi[:, t, c, :], wc_lo[:, t, c, :]),
                                     lambda c: (ctx_hi[:, c, :], ctx_lo[:, c, :]), CQ, list(range(CC)),
                                     True, True).then_inc(c_mm, 1)

                    def turn_block(i, k, src, ready):
                        pe.wait_ge(ready, b * TB + i + 1)
                        for h in range(2):
                            pe.wait_ge(t_lo, turn_base(b, i, k) + h + 1)
                            for c in range(4):
                                mm = pe.transpose(ps_t[h][:, c * P:(c + 1) * P],
                                                  src[:, (4 * h + c) * P:(4 * h + c + 1) * P], ident[:, :])
                            mm.then_inc(t_turn, 1)

                    def energy(mb):
                        if mb == 0:
                            pe.wait_ge(c_qk, b * 8 + 8 + 2)
                            pe.wait_ge(o_ok, b * (4 * PAIRS) + 4 * PAIRS + C_O)
                        elif mb < EARLY:
                            pe.wait_ge(e_exp, b * TB + mb)
                        elif mb < EARLY + 2:
                            pe.wait_ge(x1_ok, b * TB + TB - 1 + mb - EARLY + C_OUT)
                        else:
                            pe.wait_ge(e_exp, b * TB + mb - 1)
                        q = slice(mb * P, (mb + 1) * P)
                        for h in range(2):
                            r = slice(h * HALF, (h + 1) * HALF)
                            mm = split_mm(e_bank(mb)[:, r], lambda c: (qk_hi[:, 0, q], qk_lo[:, 0, q]),
                                          lambda c: (qk_hi[:, 1, r], qk_lo[:, 1, r]), HALF, [0], True, True)
                        mm.then_inc(e_mm, 1)

                    def turn_energy(mb):
                        pe.wait_ge(e_norm, b * TB + mb + 1)
                        for h in range(2):
                            if mb >= 2:
                                pe.wait_ge(e_lo, b * (2 * TB) + 2 * mb + h - 3)
                            elif mb == 1:
                                pe.wait_ge(e_exp, b * TB + EARLY)
                            for c in range(4):
                                mm = pe.transpose(at_bank(mb, h)[:, c * P:(c + 1) * P],
                                                  c_probs[:, mb % 4, (4 * h + c) * P:(4 * h + c + 1) * P], ident[:, :])
                            mm.then_inc(e_turn, 1)

                    for t in range(TB):
                        project_out(t // 2, t % 2, 0)
                        if t == TB - 1:
                            energy(EARLY - 1)
                        project_out(t // 2, t % 2, 1)
                        if t < 4:
                            queries_keys(t)
                        elif t < TB - 1:
                            energy(t - 4)
                    turn_block(0, 0, xn2, t_xn2)
                    for mb in range(TB):
                        if mb + EARLY < TB:
                            energy(mb + EARLY)
                        if mb == 0:
                            pe.wait_ge(t_lo, turn_base(b, 0, 0) + 2 + 2)
                        turn_energy(mb)

                    def cross(i, h):
                        if h == 0:
                            pe.wait_ge(t_lo, turn_base(b, i, 0) + 2 + 2)
                            pe.wait_ge(x2_ok, b * TB + i + 1)
                        r = slice(h * HALF, (h + 1) * HALF)
                        mm = split_mm(ps_s[0][:, r], lambda c: (t2_hi[:, c, :], t2_lo[:, c, :]),
                                      lambda c: (at_hi[:, c, r], at_lo[:, c, r]), HALF, list(range(KC)), True, True)
                        mm.then_inc(xm_ok, 1)

                    def select(i):
                        pe.wait_ge(t_lo, turn_base(b, i, 1) + 2 + 2)
                        pe.wait_ge(f_g, b * TB + i + 1)
                        split_mm(ps_p[:, 0:FW], lambda c: (t3_hi[:, c, :], t3_lo[:, c, :]),
                                 lambda c: (ffn_hi[:, c, :], ffn_lo[:, c, :]), FW, list(range(KC)),
                                 True, True).then_inc(f_mm, 1)

                    def turn_low(i):
                        pe.wait_ge(f_g, b * TB + i + 1 + 1)
                        pe.wait_ge(l_ok, b * TB + i + 1)
                        pe.transpose(ps_o[0:GK, 0:P], low_h[:, :], ident[:, :]).then_inc(l_turn, 1)

                    def expand(i):
                        pe.wait_ge(l_ok, b * TB + i + 1 + 1)
                        pe.wait_ge(y_ok, b * TB + i + 1)
                        for h in range(2):
                            r = slice(h * HALF, (h + 1) * HALF)
                            mm = split_mm(ps_s[1][:, r], lambda c: (lt_hi[:, :], lt_lo[:, :]),
                                          lambda c: (up_hi[:, r], up_lo[:, r]), HALF, [0], True, True)
                        mm.then_inc(u_mm, 1)

                    def tail_block(i, par):
                        cross(i, 0)
                        if not first(i):
                            turn_block(i - 1, 1, xn3[:, 1 - par, :], t_xn3)
                        if second(i):
                            turn_low(i - 2)
                        cross(i, 1)
                        if has(i + 1):
                            turn_block(i + 1, 0, xn2, t_xn2)
                        if second(i):
                            expand(i - 2)
                        if not first(i):
                            select(i - 1)

                    pe.wait_ge(e_lo, b * (2 * TB) + 2 * TB)
                    tail_blocks(pe, tail_block)
                    pe.wait_ge(x2_ok, b * TB + TB + 1)
                    turn_x(b + 1, 0)
                    turn_block(TB - 1, 1, xn3[:, 1, :], t_xn3)
                    turn_low(TB - 2)
                    select(TB - 1)
                    turn_x(b + 1, 1)
                    expand(TB - 2)
                    turn_x(b + 1, 2)
                    turn_low(TB - 1)
                    turn_x(b + 1, 3)
                    expand(TB - 1)
                    for i in range(4, TB):
                        turn_x(b + 1, i)
                    end_phase(pe, b, 1)

            @block.scalar
            def _(act):
                end_setup(act)
                act.sem_inc(exp_ok, C_EXP)
                act.sem_inc(proj_out, C_PROJ)

                def copy_out(b, pair, t, h, reuse, banks):
                    n = b * PAIRS + pair
                    act.wait_ge(part_ok, n * PROJ + (2 * t + h + 1) * PARTS + C_PART)
                    if reuse is not None:
                        if t < 2:
                            act.wait_ge(stack_ok, n * 2)
                        else:
                            act.wait_ge(turn_ok, reuse + 1 + C_TURN)
                    act.activation(qkv[:, t, h * HALF:(h + 1) * HALF], banks[(2 * t + h) % len(banks)][:, :], ACT.Copy,
                                   scale=-(HD ** -0.5) if t == 0 else 1.0).then_inc(proj_out, 1)

                def stack(b, pair, j, part):
                    n = b * PAIRS + pair
                    if part == 0:
                        act.wait_ge(proj_out, n * 6 + 4 + C_PROJ)
                        act.wait_ge(scores_ok, n * 16 + 8 * j + 8 - 16 + C_SCORES)
                        act.activation(q_st[j][own(j), :], qkv[own(j), 0, :], ACT.Copy).then_inc(q_hi_ok, 1)
                    else:
                        rows = own(j) if part == 1 else opposite(j)
                        act.activation(k_hi[j][rows, :], qkv[own(j), 1, :], ACT.Copy).then_inc(k_hi_ok, 1)

                def split_values(j, turn, bank, mixes):
                    act.wait_ge(turn_ok, turn + 1 + C_TURN)
                    act.wait_ge(mix_ok, mixes + C_MIX)
                    act.activation(v_st[j][:, :, 0:HD], bank[:, :].rearrange("p (k d) -> p k d", d=HD),
                                   ACT.Copy).then_inc(hi_ok, 1)

                def attend(b, hp, order):
                    n = b * PAIRS + hp
                    t0 = b * TURNS_B + hp * TURNS
                    for e in order:
                        if e[0] == "exp":
                            _, j, qb = e
                            i, w = 8 * j + qb, (qb + 1) * P
                            act.wait_ge(low_ok, n * 16 + i + 1)
                            if qb % 4 == 0:
                                if j == B:
                                    act.wait_ge(turn_ok, t0 + body_turns[("turn", A, qb // 4, 4 * (qb // 4) + 3)] + 1 + C_TURN)
                                else:
                                    act.wait_ge(turn_ok, t0 - TURNS + prev_last_turn[qb // 4] + 1 + C_TURN)
                            act.activation(probs[:, off(qb):off(qb) + w], ps_s[qb % 2][:, 0:w], ACT.Exp,
                                           bias=low[:, i:i + 1], scale=-1.0,
                                           accum_out=den[:, i:i + 1]).then_inc(exp_ok, 1)
                        elif e[0] == "turn":
                            _, j, g, kb = e
                            c, m = cols(g, kb), body_mixes[("mix", j, g, kb)]
                            act.wait_ge(turn_ok, t0 + body_turns[e] + 1 + C_TURN)
                            act.wait_ge(mix_ok, n * MIXES + m - 1 + C_MIX)
                            act.activation(pt_hi[:, m % 2, c:HALF], ps_t[body_turns[e] % 2][:, c:HALF],
                                           ACT.Copy).then_inc(hi_ok, 1)
                        elif e[0] == "take":
                            _, j, g = e
                            if order is tail_body and (j, g) == (B, 1):
                                act.wait_ge(o_ok, n * 4 + 3 + C_O)
                                heads_hi(b, 0, 0)
                            act.wait_ge(mix_ok, n * MIXES + body_mixes[("mix", j, g, 4 * g + 3)] + 1 + C_MIX)
                            act.wait_ge(o_ok, n * 4 + 2 * j + g + C_O)
                            act.activation(o_lo[:, :], ps_o[HD:P, :], ACT.Copy).then_inc(o_lo_ok, 1)
                        elif e[0] == "vturn":
                            bank = ps_t[body_turns[e] % 2]
                            split_values(e[1], t0 + body_turns[e], bank, n * MIXES - (MIXES // 2 if e[1] == A else 0))
                        elif e[0] == "stack":
                            stack(b, hp + 1 if e[1] == A else hp, *e[1:])
                        elif e[0] == "copy":
                            copy_out(b, hp + 1, *e[1:], t0 + body_turns[("vturn", B)], [ps_p])

                def heads_hi(b, v, s):
                    act.wait_ge(out_mm, b * TB + v * 2 + s + 1)
                    act.activation(o_hi[:, s, :, :], otx[:, v * 2 + s, :, :], ACT.Copy).then_inc(st_hi, 1)

                def first_norm(n, i, par):
                    act.wait_ge(ln_sh, n + 1)
                    act.activation(x_in[:, i, :], x_in[:, i, :], ACT.Identity, bias=shift[:, 3 + par:4 + par],
                                   scale=rstd[:, 3 + par:4 + par]).then_inc(ln_xn, 1)

                def turned_x(n, i):
                    for h in range(2):
                        act.wait_ge(ln_turn, n * (2 * TB) + 2 * i + h + 1)
                        act.activation(xt_hi[:, 4 * h:4 * h + 4, i * P:(i + 1) * P],
                                       turns4(x_bank(i, h)), ACT.Copy).then_inc(ln_hi, 1)

                for i in range(TB):
                    first_norm(i, i, i % 2)
                    if i >= 1:
                        turned_x(0, i - 1)
                turned_x(0, TB - 1)
                with act.Fori(0, BATCH) as b:
                    for t in range(3):
                        for h in range(2):
                            copy_out(b, 0, t, h, None, first_banks)
                        if t == 1:
                            for part in range(3):
                                stack(b, 0, A, part)
                    with act.Fori(0, PAIRS - 1) as hp:
                        attend(b, hp, body)
                    attend(b, PAIRS - 1, tail_body)
                    heads_hi(b, 0, 1)
                    end_phase(act, b, 0)

                    def ctx_part(q):
                        act.wait_ge(c_in, b * 64 + q * 16 + 16)
                        act.activation(ctx_hi[:, :, :], ctx_raw[:, :, :], ACT.Copy).then_inc(c_hi, 1)

                    def queries_keys(q):
                        for t in range(2):
                            act.wait_ge(c_mm, b * 8 + q * 2 + t + 1)
                            act.activation(qk_hi[:, t, bass.ts(q, CQ)], ps_t[t][:, 0:CQ], ACT.Identity,
                                           bias=bias_c[:, t:t + 1], scale=1.0).then_inc(c_qhi, 1)

                    def normalise(i, k, slot, dst, ok):
                        act.wait_ge(t_sh, norm_base(b, i, k) + 1)
                        if k == 1 and second(i):
                            act.wait_ge(f_x, b * TB + i - 1)
                        act.activation(dst, otx[:, i, :, :].rearrange("p k t -> p (k t)"), ACT.Identity,
                                       bias=shift[:, slot:slot + 1], scale=rstd[:, slot:slot + 1]).then_inc(ok, 1)

                    act.wait_ge(c_win, b * 16 + 16)
                    act.activation(wc_hi[:, :, :, :], wc_raw[:, :, :, :], ACT.Copy).then_inc(c_whi, 1)
                    ctx_part(0)
                    def turned(mb):
                        for h in range(2):
                            act.wait_ge(e_turn, b * (2 * TB) + 2 * mb + h + 1)
                            act.activation(at_hi[:, 4 * h:4 * h + 4, mb * P:(mb + 1) * P], turns4(at_bank(mb, h)),
                                           ACT.Copy).then_inc(e_hi, 1)

                    def turned_block(i, k, dst, used):
                        used()
                        for h in range(2):
                            act.wait_ge(t_turn, turn_base(b, i, k) + h + 1)
                            act.activation(dst[:, 4 * h:4 * h + 4, :], turns4(ps_t[h][:, :]), ACT.Copy).then_inc(t_hi, 1)

                    def turned2(i):
                        turned_block(i, 0, t2_hi, lambda: None if first(i) else act.wait_ge(xm_ok, b * (2 * TB) + i * 2))

                    def exponentials(mb):
                        act.wait_ge(e_neg, b * TB + mb + 1)
                        if mb >= 4:
                            act.wait_ge(e_turn, b * (2 * TB) + 2 * mb - 6)
                        act.activation(c_probs[:, mb % 4, :], e_bank(mb)[:, :], ACT.Exp, bias=low[:, 8 + mb:9 + mb],
                                       scale=1.0, accum_out=den[:, mb:mb + 1]).then_inc(e_exp, 1)

                    for t in range(TB):
                        if t < 4:
                            queries_keys(t)
                        if t + 1 < 4:
                            ctx_part(t + 1)
                        if t + 2 < TB:
                            heads_hi(b, (t + 2) // 2, t % 2)
                        if t == 4:
                            normalise(0, 0, 0, xn2[:, :], t_xn2)
                        if t >= 4:
                            exponentials(t - 4)
                    turned2(0)
                    for mb in range(TB):
                        turned(mb)
                        if mb + EARLY < TB:
                            exponentials(mb + EARLY)

                    def turned3(i):
                        turned_block(i, 1, t3_hi, lambda: None if first(i) else act.wait_ge(f_mm, b * TB + i))

                    def gate(i):
                        act.wait_ge(f_z, b * TB + i + 1)
                        act.activation(g8[:, 5, :], g8[:, 4, :], ACT.Exp, scale=-1.0).then_inc(f_e, 1)

                    def lowered(i):
                        act.wait_ge(l_turn, b * TB + i + 1)
                        act.wait_ge(u_mm, b * TB + i + 1)
                        act.activation(lt_hi[:, :], ps_o[0:GK, 0:P], ACT.Copy).then_inc(l_hi, 1)

                    def tail_block(i, par):
                        if has(i + 1):
                            turned2(i + 1)
                        if last(i):
                            turned_x(b + 1, 0)
                        normalise(i, 1, 1 + par, xn3[:, par, :], t_xn3)
                        if not first(i):
                            gate(i - 1)
                        turned3(i)
                        if not first(i):
                            lowered(i - 1)
                        if has(i + 2):
                            normalise(i + 2, 0, 0, xn2[:, :], t_xn2)
                        if first(i):
                            first_norm(b * TB + TB, 0, 0)
                        if not last(i):
                            first_norm(b * TB + TB + i + 1, i + 1, 1 - par)

                    normalise(1, 0, 0, xn2[:, :], t_xn2)
                    tail_blocks(act, tail_block)
                    turned_x(b + 1, 1)
                    gate(TB - 1)
                    turned_x(b + 1, 2)
                    lowered(TB - 1)
                    for i in range(3, TB):
                        turned_x(b + 1, i)
                    end_phase(act, b, 1)

            @block.vector
            def _(dve):
                dve.wait_ge(setup_in, 96)
                for lo_c, hi_c, src in ((0, 64, 0), (64, 128, EXPERTS)):
                    dve.tensor_tensor(
                        ffn_prod[:, :, lo_c:hi_c].rearrange("p k (n s) -> p k n s", s=SEL),
                        ffn_raw[:, :, lo_c:hi_c].rearrange("p k (n s) -> p k n s", s=SEL),
                        vec_raw[:, :, src:src + EXPERTS].unsqueeze(3).broadcast_to([P, KC, EXPERTS, SEL]), ALU.mult)
                dve.tensor_tensor(ffn_prod[:, :, 128:FW], ffn_raw[:, :, 128:FW], vec_raw[:, :, 0:EXPERTS],
                                  ALU.mult).then_inc(setup_prod, 1)
                dve.tensor_copy(ffn_hi[:, :, :], ffn_raw[:, :, :]).then_inc(setup_split, 1)
                dve.tensor_copy(up_hi[:, :], up_raw[:, :]).then_inc(setup_split, 1)
                dve.wait_ge(setup_split, 2)
                dve.tensor_tensor(ffn_lo[:, :, :], ffn_raw[:, :, :], f(ffn_hi[:, :, :]), ALU.subtract)
                dve.tensor_tensor(up_lo[:, :], up_raw[:, :], f(up_hi[:, :]), ALU.subtract)
                dve.wait_ge(setup_mm, 1)
                dve.tensor_copy(ffn_c[:, :], ps_p[:, 0:FW])
                end_setup(dve)
                dve.sem_inc(lo_ok, C_LO)
                dve.sem_inc(o_ok, C_O)
                for s, c in ((ln_xn, C_LN), (ln_lo, 4), (wo_ok, C_OUT), (x1_ok, 2), (c_split, C_ONE), (c_qk, 2), (t_lo, 2), (x2_ok, 1),
                             (f_g, 1), (l_ok, 1), (y_ok, 1)):
                    dve.sem_inc(s, c)

                def stack(b, pair, j, part):
                    n = b * PAIRS + pair
                    if part == 0:
                        dve.wait_ge(q_hi_ok, n * 2 + j + 1)
                        dve.tensor_tensor(q_st[j][opposite(j), :], qkv[own(j), 0, :], f(q_st[j][own(j), :]), ALU.subtract)
                    elif part == 1:
                        dve.wait_ge(k_hi_ok, n * 4 + 2 * j + 1)
                        dve.tensor_tensor(k_lo[j][own(j), :], qkv[own(j), 1, :], f(k_hi[j][own(j), :]),
                                          ALU.subtract).then_inc(k_lo_ok, 1)
                    else:
                        dve.wait_ge(k_hi_ok, n * 4 + 2 * j + 2)
                        dve.wait_ge(k_lo_ok, n * 2 + j + 1)
                        dve.tensor_copy(k_lo[j][opposite(j), :], f(k_lo[j][own(j), :])).then_inc(stack_ok, 1)

                def split_values(j, turn, bank):
                    dve.wait_ge(hi_ok, turn + 1)
                    dve.tensor_tensor(v_st[j][:, :, HD:2 * HD], bank[:, :].rearrange("p (k d) -> p k d", d=HD),
                                      f(v_st[j][:, :, 0:HD]), ALU.subtract).then_inc(lo_ok, 1)

                def attend(b, hp, order):
                    n = b * PAIRS + hp
                    t0 = b * TURNS_B + hp * TURNS
                    for e in order:
                        if e[0] == "scores":
                            _, j, qb = e
                            i, w = 8 * j + qb, (qb + 1) * P
                            dve.wait_ge(scores_ok, n * 16 + i + 1 + C_SCORES)
                            dve.tensor_reduce(low[:, i:i + 1], ps_s[qb % 2][:, 0:w], AX_X, ALU.min).then_inc(low_ok, 1)
                        elif e[0] == "norm":
                            _, j, qb = e
                            i = 8 * j + qb
                            dve.wait_ge(exp_ok, n * 16 + i + 1 + C_EXP)
                            dve.reciprocal(rden[:, i:i + 1], den[:, i:i + 1]).then_inc(rden_ok, 1)
                        elif e[0] == "turn":
                            _, j, g, kb = e
                            c, m = cols(g, kb), body_mixes[("mix", j, g, kb)]
                            dve.wait_ge(hi_ok, t0 + body_turns[e] + 1)
                            dve.tensor_tensor(pt_lo[:, m % 2, c:HALF], ps_t[body_turns[e] % 2][:, c:HALF],
                                              f(pt_hi[:, m % 2, c:HALF]), ALU.subtract).then_inc(lo_ok, 1)
                        elif e[0] == "take":
                            _, j, g = e
                            if order is tail_body and (j, g) == (B, 1):
                                split_heads(b, 0, 0)
                            dve.wait_ge(o_lo_ok, n * 4 + 2 * j + g + 1)
                            dve.tensor_tensor(otx[own(j), 4 * g:4 * g + 4, hp, :],
                                              ps_o[0:HD, :].rearrange("p (t q) -> p t q", q=P),
                                              o_lo[:, :].rearrange("p (t q) -> p t q", q=P),
                                              ALU.add).then_inc(o_ok, 1)
                        elif e[0] == "vturn":
                            split_values(e[1], t0 + body_turns[e], ps_t[body_turns[e] % 2])
                        elif e[0] == "stack":
                            stack(b, hp + 1 if e[1] == A else hp, *e[1:])

                def split_heads(b, v, s):
                    tb = v * 2 + s
                    dve.wait_ge(st_hi, b * TB + tb + 1)
                    dve.tensor_tensor(o_rest[:, s, :, :], otx[:, tb, :, :], f(o_hi[:, s, :, :]),
                                      ALU.subtract).then_inc(st_ok, 1)

                def add_out(b, v, s):
                    tb = v * 2 + s
                    dve.wait_ge(out_mm, b * TB + tb + 1 + C_OUT)
                    dve.wait_ge(xr_in[s], b * (16 * TB // 2) + v * 16 + 16)
                    dve.tensor_tensor(otx[:, tb, :, :].rearrange("p k t -> p (k t)"), ps_s[s][:, :], x_res[:, s, :],
                                      ALU.add).then_inc(x1_ok, 1)

                def stats(src, s, n_bn, ok_bn, ok_mv):
                    alone(dve)
                    for h in range(2):
                        ins = dve.bn_stats(bn[:, s, h, :], src[:, h * HALF:(h + 1) * HALF])
                    ins.then_inc(ok_bn, 1)
                    dve.wait_ge(ok_bn, n_bn)
                    alone(dve)
                    dve.bn_aggr(mv[:, s, :], bn[:, s, :, :].rearrange("p h c -> p (h c)")).then_inc(ok_mv, 1)

                def first_norm(n, i, par):
                    dve.wait_ge(ln_xn, n + 1)
                    stats(x_in[:, i, :], 3 + par, n + 1, ln_bn, ln_mv)

                dve.wait_ge(ln_in, 32)
                def turned_x(n, i):
                    for h in range(2):
                        dve.wait_ge(ln_hi, n * (2 * TB) + 2 * i + h + 1)
                        r = slice(i * P, (i + 1) * P)
                        dve.tensor_tensor(xt_lo[:, 4 * h:4 * h + 4, r], turns4(x_bank(i, h)),
                                          f(xt_hi[:, 4 * h:4 * h + 4, r]), ALU.subtract).then_inc(ln_lo, 1)

                for i in range(TB):
                    first_norm(i, i, i % 2)
                    if i >= 2:
                        turned_x(0, i - 2)
                for i in range(TB - 2, TB):
                    turned_x(0, i)
                with dve.Fori(0, BATCH) as b:
                    for part in range(3):
                        stack(b, 0, A, part)
                    with dve.Fori(0, PAIRS - 1) as hp:
                        attend(b, hp, body)
                    attend(b, PAIRS - 1, tail_body)
                    split_heads(b, 0, 1)
                    end_phase(dve, b, 0)

                    def ctx_part(q):
                        dve.wait_ge(c_hi, b * 4 + q + 1)
                        dve.tensor_tensor(ctx_lo[:, :, :], ctx_raw[:, :, :], f(ctx_hi[:, :, :]),
                                          ALU.subtract).then_inc(c_split, 1)

                    def queries_keys(q):
                        for t in range(2):
                            dve.wait_ge(c_qhi, b * 8 + q * 2 + t + 1)
                            r = bass.ts(q, CQ)
                            dve.scalar_tensor_tensor(out=qk_lo[:, t, r], in0=ps_t[t][:, 0:CQ], scalar=bias_c[:, t:t + 1],
                                                     in1=f(qk_hi[:, t, r]), op0=ALU.add,
                                                     op1=ALU.subtract).then_inc(c_qk, 1)

                    def flat(i):
                        return otx[:, i, :, :].rearrange("p k t -> p (k t)")

                    def norm(i, k, slot):
                        if k == 1:
                            dve.wait_ge(x2_ok, b * TB + i + 2)
                        elif first(i):
                            dve.wait_ge(x1_ok, b * TB + 1 + C_OUT)
                        stats(flat(i), slot, norm_base(b, i, k) + 1, t_bn, t_mv)

                    dve.wait_ge(c_whi, b + 1)
                    dve.tensor_tensor(wc_lo[:, :, :, :], wc_raw[:, :, :, :], f(wc_hi[:, :, :, :]),
                                      ALU.subtract).then_inc(c_wok, 1)
                    ctx_part(0)

                    def turned(mb):
                        for h in range(2):
                            dve.wait_ge(e_hi, b * (2 * TB) + 2 * mb + h + 1)
                            r = slice(mb * P, (mb + 1) * P)
                            dve.tensor_tensor(at_lo[:, 4 * h:4 * h + 4, r], turns4(at_bank(mb, h)),
                                              f(at_hi[:, 4 * h:4 * h + 4, r]), ALU.subtract).then_inc(e_lo, 1)

                    def turned_block(i, k, lo_t, hi_t):
                        for h in range(2):
                            dve.wait_ge(t_hi, turn_base(b, i, k) + h + 1)
                            dve.tensor_tensor(lo_t[:, 4 * h:4 * h + 4, :], turns4(ps_t[h][:, :]),
                                              f(hi_t[:, 4 * h:4 * h + 4, :]), ALU.subtract).then_inc(t_lo, 1)

                    def peaks(mb):
                        dve.wait_ge(e_mm, b * TB + mb + 1)
                        dve.tensor_reduce(low[:, mb:mb + 1], e_bank(mb)[:, :], AX_X, ALU.max).then_inc(e_mx, 1)
                        dve.wait_ge(e_mx, b * TB + mb + 1)
                        dve.tensor_scalar(low[:, 8 + mb:9 + mb], low[:, mb:mb + 1], -1.0, None, ALU.mult).then_inc(e_neg, 1)

                    def inverse_sums(mb):
                        dve.wait_ge(e_exp, b * TB + mb + 1)
                        dve.reciprocal(rden[:, mb:mb + 1], den[:, mb:mb + 1]).then_inc(e_rd, 1)

                    for t in range(TB):
                        if t == TB - 1:
                            peaks(EARLY - 1)
                        add_out(b, t // 2, t % 2)
                        if t < 4:
                            queries_keys(t)
                        if t + 1 < 4:
                            ctx_part(t + 1)
                        if t + 2 < TB:
                            split_heads(b, (t + 2) // 2, t % 2)
                        if t == 3:
                            norm(0, 0, 0)
                        if 4 <= t < TB - 1:
                            peaks(t - 4)
                        if t >= 4:
                            inverse_sums(t - 4)
                    turned_block(0, 0, t2_lo, t2_hi)
                    for mb in range(TB):
                        if mb + EARLY < TB:
                            peaks(mb + EARLY)
                        if 1 <= mb <= TB - EARLY:
                            inverse_sums(mb + EARLY - 1)
                        turned(mb)

                    def cross(i):
                        dve.wait_ge(xm_ok, b * (2 * TB) + i * 2 + 2)
                        dve.tensor_tensor(flat(i), ps_s[0][:, :], flat(i), ALU.add).then_inc(x2_ok, 1)

                    STEPS = 13

                    def gate(i, par):
                        base = (b * TB + i) * STEPS
                        count = [0]

                        def step(ins):
                            count[0] += 1
                            ins.then_inc(f_step, 1)
                            dve.wait_ge(f_step, base + count[0])

                        dve.wait_ge(f_mm, b * TB + i + 1)
                        step(dve.tensor_tensor(sel_u[:, :], ps_p[:, 0:64], ffn_c[:, 0:64], ALU.subtract))
                        dve.tensor_tensor(sel_sq[:, :], sel_u[:, :], sel_u[:, :], ALU.mult)
                        step(dve.tensor_scalar(g1[:, 0:1], mv[:, 1 + par, 1:2], float(DM), rstd[:, 1 + par:2 + par], ALU.mult, ALU.mult))
                        step(dve.tensor_scalar(g1[:, 1:2], g1[:, 0:1], rstd[:, 1 + par:2 + par], None, ALU.mult))
                        dve.tensor_reduce(g8[:, 0, :], sel_sq[:, :].rearrange("p (n s) -> p n s", s=SEL), AX_X, ALU.add)
                        step(dve.scalar_tensor_tensor(out=g8[:, 1, :], in0=ps_p[:, 128:FW], scalar=-2.0,
                                                      in1=ffn_c[:, 128:FW], op0=ALU.mult, op1=ALU.add))
                        step(dve.tensor_scalar(g8[:, 2, :], g8[:, 1, :], g1[:, 1:2], None, ALU.add))
                        step(dve.reciprocal(g8[:, 1, :], g8[:, 2, :]))
                        step(dve.tensor_tensor(g8[:, 3, :], g8[:, 0, :], g8[:, 1, :], ALU.mult))
                        step(dve.tensor_tensor(g8[:, 2, :], g8[:, 3, :], center_b[:, :], ALU.subtract))
                        dve.tensor_tensor(g8[:, 4, :], g8[:, 2, :], slope_b[:, :], ALU.mult).then_inc(f_z, 1)
                        dve.tensor_tensor(low_h[:, 0:64], ps_p[:, 64:128], ffn_c[:, 64:128], ALU.subtract)
                        dve.wait_ge(f_e, b * TB + i + 1)
                        step(dve.tensor_scalar(g8[:, 6, :], g8[:, 5, :], 1.0, None, ALU.add))
                        step(dve.reciprocal(g8[:, 7, :], g8[:, 6, :]))
                        step(dve.tensor_reduce(g1[:, 2:3], g8[:, 7, :], AX_X, ALU.max))
                        dve.tensor_scalar(g1[:, 4:5], g1[:, 2:3], -1.0, 1.0, ALU.mult, ALU.add)
                        step(dve.scalar_tensor_tensor(out=g8[:, 8, :], in0=g8[:, 7, :], scalar=g1[:, 2:3],
                                                      in1=rank[:, :], op0=ALU.is_equal, op1=ALU.mult))
                        step(dve.tensor_reduce(g1[:, 3:4], g8[:, 8, :], AX_X, ALU.max))
                        assert count[0] == STEPS
                        dve.tensor_scalar(low_h[:, 64:GK], g8[:, 8, :], g1[:, 3:4], g1[:, 2:3], ALU.is_equal,
                                          ALU.mult).then_inc(f_w, 1)
                        dve.wait_ge(f_w, b * TB + i + 1)
                        lh = low_h[:, 0:64].rearrange("p (n h) -> p n h", h=LOW)
                        dve.tensor_tensor(lh, lh, low_h[:, 64:GK].unsqueeze(2).broadcast_to([P, EXPERTS, LOW]),
                                          ALU.mult).then_inc(f_g, 1)
                        dve.scalar_tensor_tensor(out=flat(i), in0=xn3[:, par, :], scalar=g1[:, 4:5], in1=flat(i),
                                                 op0=ALU.mult, op1=ALU.add).then_inc(f_x, 1)

                    def lowered(i):
                        dve.wait_ge(l_hi, b * TB + i + 1)
                        dve.tensor_tensor(lt_lo[:, :], ps_o[0:GK, 0:P], f(lt_hi[:, :]), ALU.subtract).then_inc(l_ok, 1)

                    def finish(i):
                        dve.wait_ge(u_mm, b * TB + i + 1 + 1)
                        dve.wait_ge(f_x, b * TB + i + 1)
                        dve.tensor_tensor(flat(i), ps_s[1][:, :], flat(i), ALU.add).then_inc(y_ok, 1)

                    def tail_block(i, par):
                        cross(i)
                        if second(i):
                            norm(i, 1, 1 + par)
                        if has(i + 1):
                            turned_block(i + 1, 0, t2_lo, t2_hi)
                        if not second(i):
                            norm(i, 1, 1 + par)
                        if not first(i):
                            gate(i - 1, 1 - par)
                        if second(i) and not last(i):
                            finish(i - 2)
                        if has(i + 2):
                            norm(i + 2, 0, 0)
                        turned_block(i, 1, t3_lo, t3_hi)
                        if not first(i):
                            lowered(i - 1)
                        if last(i):
                            finish(i - 2)
                            turned_x(b + 1, 0)
                        if first(i):
                            first_norm(b * TB + TB, 0, 0)
                        if not last(i):
                            first_norm(b * TB + TB + i + 1, i + 1, 1 - par)

                    dve.wait_ge(ln_in, b * 32 + 64)
                    norm(1, 0, 0)
                    tail_blocks(dve, tail_block)
                    gate(TB - 1, 1)
                    turned_x(b + 1, 1)
                    lowered(TB - 1)
                    turned_x(b + 1, 2)
                    finish(TB - 2)
                    turned_x(b + 1, 3)
                    finish(TB - 1)
                    for i in range(4, TB):
                        turned_x(b + 1, i)
                    end_phase(dve, b, 1)

            @block.gpsimd
            def _(pool):
                pool.memset(ones[:, :], 1.0).then_inc(setup_cst, 1)
                pool.memset(neg_half[:, :], -0.5)
                for n in range(EXPERTS):
                    pool.memset(rank[:, n:n + 1], float(EXPERTS - n))
                pool.memset(ident[:, :], 0.0)
                pool.memset(ident_bf[:, :], 0.0)
                pool.memset(mask_bf[:, :], 0.0).then_inc(setup_cst, 1)
                pool.wait_ge(setup_cst, 2)
                for m in (ident, ident_bf):
                    pool.affine_select(out=m[:, :], in_=m[:, :], compare_op=ALU.not_equal, fill=1.0,
                                       base=0, pattern=[[-1, P]], channel_multiplier=1)
                pool.affine_select(out=mask_bf[:, :], in_=mask_bf[:, :], compare_op=ALU.is_ge, fill=-NEG,
                                   base=0, pattern=[[-1, P]], channel_multiplier=1)

                def split_piece(n, k):
                    slot = k % 3
                    pool.wait_ge(w_in[k % 2], n * 48 + 16 * (k // 2 + 1))
                    if not (isinstance(n, int) and n == 0 and k < 2):
                        t, half = divmod(k - 3, 2)
                        pool.wait_ge(part_ok, n * PROJ + (2 * t + 1) * PARTS + (half + 1) * (PARTS // 2) + C_PART)
                        alone(pool)
                    alone(pool)
                    pool.tensor_scalar(w_hi[:, slot, :, :], w_raw[:, k % 2, :, :], 1.0, 1.0, ALU.mult,
                                       ALU.mult).then_inc(w_hi_ok, 1)
                    pool.wait_ge(w_hi_ok, n * 6 + k + 1)
                    pool.tensor_tensor(w_lo[:, slot, :, :], w_raw[:, k % 2, :, :], f(w_hi[:, slot, :, :]),
                                       ALU.subtract).then_inc(w_split, 1)

                def project(b, pair, t, h, k):
                    if (h, k) == (0, 0):
                        split_piece(b * PAIRS + pair, 2 * t + 2)
                    if (h, k) == (1, PARTS // 2):
                        split_piece(b * PAIRS + pair, 2 * t + 3)

                def split_out(b, q):
                    k, u = q // 2, q % 2
                    r = slice(u * HALF, (u + 1) * HALF)
                    raw = w_raw[:, u, :, :].rearrange("p c d -> p (c d)")
                    pool.wait_ge(wo_in[u], b * (16 * KC) + 16 * (k + 1))
                    if q == 0:
                        pool.wait_ge(part_ok, b * (PAIRS * PROJ) + PAIRS * PROJ + C_PART)
                    alone(pool)
                    pool.tensor_scalar(wo_hi[:, k, r], raw, 1.0, 1.0, ALU.mult, ALU.mult).then_inc(wo_hi_ok, 1)
                    pool.wait_ge(wo_hi_ok, b * (2 * KC) + q + 1)
                    pool.tensor_tensor(wo_lo[:, k, r], raw, f(wo_hi[:, k, r]), ALU.subtract).then_inc(wo_ok, 1)

                def attend(b, hp, order):
                    n = b * PAIRS + hp
                    for e in order:
                        if e[0] == "norm":
                            _, j, qb = e
                            i, r = 8 * j + qb, slice(off(qb), off(qb + 1))
                            pool.wait_ge(rden_ok, n * 16 + i + 1)
                            alone(pool)
                            pool.tensor_scalar(probs[:, r], probs[:, r], rden[:, i:i + 1], 1.0, ALU.mult,
                                               ALU.mult).then_inc(norm_ok, 1)
                        elif e[0] == "split_out":
                            split_out(b, e[1])
                        elif e[0] == "proj":
                            project(b, hp + 1, *e[1:])

                def sigma(s, n, mv_ok, ve_ok, rs_ok, sh_ok):
                    pool.wait_ge(mv_ok, n + 1)
                    alone(pool)
                    pool.tensor_scalar(veps[:, s:s + 1], mv[:, s, 1:2], EPS, 1.0, ALU.add, ALU.mult).then_inc(ve_ok, 1)
                    pool.wait_ge(ve_ok, n + 1)
                    pool.tensor_tensor(rstd[:, s:s + 1], veps[:, s:s + 1], neg_half[:, :], ALU.pow).then_inc(rs_ok, 1)
                    pool.wait_ge(rs_ok, n + 1)
                    alone(pool)
                    pool.tensor_scalar(shift[:, s:s + 1], mv[:, s, 0:1], rstd[:, s:s + 1], -1.0, ALU.mult,
                                       ALU.mult).then_inc(sh_ok, 1)

                end_setup(pool)
                pool.sem_inc(w_split, C_SPLIT)
                for k in range(2):
                    split_piece(0, k)
                for i in range(TB):
                    sigma(3 + i % 2, i, ln_mv, ln_ve, ln_rs, ln_sh)
                with pool.Fori(0, BATCH) as b:
                    for t in range(3):
                        for h in range(2):
                            for k in range(PARTS):
                                project(b, 0, t, h, k)
                    with pool.Fori(0, PAIRS - 1) as hp:
                        attend(b, hp, body)
                    attend(b, PAIRS - 1, tail_body)
                    end_phase(pool, b, 0)

                    def tail_norm(i, k, slot):
                        sigma(slot, norm_base(b, i, k), t_mv, t_ve, t_rs, t_sh)

                    tail_norm(0, 0, 0)
                    for mb in range(TB):
                        pool.wait_ge(e_rd, b * TB + mb + 1)
                        alone(pool)
                        pool.tensor_scalar(c_probs[:, mb % 4, :], c_probs[:, mb % 4, :], rden[:, mb:mb + 1], 1.0,
                                           ALU.mult, ALU.mult).then_inc(e_norm, 1)

                    def tail_block(i, par):
                        tail_norm(i, 1, 1 + par)
                        if has(i + 2):
                            tail_norm(i + 2, 0, 0)
                        if first(i):
                            sigma(3, b * TB + TB, ln_mv, ln_ve, ln_rs, ln_sh)
                        if not last(i):
                            sigma(4 - par, b * TB + TB + i + 1, ln_mv, ln_ve, ln_rs, ln_sh)

                    tail_norm(1, 0, 0)
                    tail_blocks(pool, tail_block)
                    end_phase(pool, b, 1)


def kernel(x, ctx_1024, L0_attn_w_qkv, L0_attn_w_out, L0_xattn_Wq, L0_xattn_bq, L0_xattn_Wk, L0_xattn_bk,
           L0_ffn_select_weight, L0_ffn_select_mean_diff, L0_ffn_imp_center, L0_ffn_imp_slope,
           L0_ffn_lora_update, L0_ffn_lora_degen, L0_ffn_bias_w, L0_ffn_debias_w):
    import numpy as np
    import concourse.bacc as bacc
    from concourse.bass_utils import run_bass_kernel_spmd

    def by_columns(w, n):
        return np.asarray(w).transpose(1, 0, 2).reshape(DM, n)

    w = np.asarray(L0_attn_w_qkv).reshape(2, CC, P, 3, PAIRS, P).transpose(4, 3, 2, 0, 1, 5)
    arrays = {
        "x": np.asarray(x).reshape(BATCH, TB, P, DM),
        "w_qkv": w.reshape(3 * PAIRS, P, 2, CC, P),
        "w_out": np.asarray(L0_attn_w_out).reshape(KC, P, DM),
        "ctx_t": np.asarray(ctx_1024).transpose(0, 2, 1).reshape(BATCH, CC, P, SEQ).transpose(0, 2, 1, 3),
        "w_ctx": np.stack([np.asarray(m).T.reshape(CC, P, CD) for m in (L0_xattn_Wq, L0_xattn_Wk)]).transpose(2, 0, 1, 3),
        "b_ctx": np.stack([np.asarray(L0_xattn_bq), np.asarray(L0_xattn_bk)], axis=1),
        "w_ffn": np.concatenate([by_columns(L0_ffn_select_weight, 64), by_columns(L0_ffn_lora_update, 64),
                                 np.asarray(L0_ffn_select_mean_diff).T], axis=1),
        "v_ffn": np.concatenate([np.asarray(L0_ffn_select_mean_diff).T, np.asarray(L0_ffn_debias_w).T], axis=1),
        "w_up": np.concatenate([np.asarray(L0_ffn_lora_degen).transpose(0, 2, 1).reshape(EXPERTS * LOW, DM),
                                np.asarray(L0_ffn_bias_w)], axis=0),
        "center": np.asarray(L0_ffn_imp_center).reshape(1, EXPERTS),
        "slope": np.asarray(L0_ffn_imp_slope).reshape(1, EXPERTS),
    }
    arrays = {n: np.ascontiguousarray(a) for n, a in arrays.items()}
    nc = bacc.Bacc("TRN2", target_bir_lowering=False, num_devices=1)
    args = [nc.dram_tensor(f"in_{n}", a.shape, mybir.dt.from_np(a.dtype), kind="ExternalInput").ap()
            for n, a in arrays.items()]
    out = nc.dram_tensor("out", (BATCH, TB, P, DM), F32, kind="ExternalOutput").ap()
    decoder_layer(nc, *args, out)
    result = run_bass_kernel_spmd(nc, [{f"in_{n}": a for n, a in arrays.items()}], core_ids=[0])
    return result.results[0]["out"].reshape(BATCH, SEQ, DM)
```
